# Optimizing a Trainium2 kernel written in Bass

```python
import numpy as np
import jax
import jax.numpy as jnp

def _softmax(x, axis=-1):
    return jax.nn.softmax(x, axis=axis)

def _gelu(x):
    return jax.nn.gelu(x, approximate=True)

def _silu(x):
    return jax.nn.silu(x)

def _sigmoid(x):
    return jax.nn.sigmoid(x)

def _layernorm(x, axis=-1, eps=1e-05):
    m = jnp.mean(x, axis=axis, keepdims=True)
    v = jnp.var(x, axis=axis, keepdims=True)
    return (x - m) / jnp.sqrt(v + eps)

def _scatter_add(tgt, idx, src, axis=0):
    return tgt.at[idx].add(src)

def _segment_sum(src, seg, n):
    return jax.ops.segment_sum(src, seg, n)
kernel_name = 'mk_decoder_postln_d1_seqx_r4_21324e'

def setup_inputs(seed: int=0):
    np.random.seed(seed)
    _w = jnp.asarray

    def _rec_inputs():
        import jax
        import jax.numpy as jnp
        _rk = jax.random.key(seed)
        x = 7.22e-05 + 1 * jax.random.normal(jax.random.fold_in(_rk, 1), (16, 256, 256), jnp.float32)
        _lenS = 256 - jax.random.randint(jax.random.fold_in(_rk, 7), (16,), 0, max(1, 256 // 4) + 1, jnp.int32)
        _lenS2 = 256 - jax.random.randint(jax.random.fold_in(_rk, 8), (16,), 0, max(1, 256 // 4) + 1, jnp.int32)
        _ctx_1024P = jax.random.normal(jax.random.fold_in(_rk, 11), (16, 16, 256), jnp.float32)
        _ctx_1024c = jax.random.dirichlet(jax.random.fold_in(_rk, 511), 0.3 * jnp.ones((16,), jnp.float32), (16, 256))
        _ctx_1024t = jnp.einsum('bsk,bkd->bsd', _ctx_1024c, _ctx_1024P)
        _ctx_1024t = _ctx_1024t * jax.lax.rsqrt(jnp.mean(jnp.square(_ctx_1024t)) + 1e-12) * 0.953939
        ctx_1024 = 4.13588e-05 + 0.999923 * (_ctx_1024t + 0.3 * jax.random.normal(jax.random.fold_in(_rk, 611), (16, 256, 256), jnp.float32))
        return (x, ctx_1024)
    x, ctx_1024 = _rec_inputs()

    def _L0_attn_setup():
        import jax, jax.numpy as jnp
        import numpy as np
        B, L, D = (2, 512, 256)
        K, M, A = (32, 4, 4)
        H = D // K
        CK = 4
        TOTAL = 2 * D + K

        def _glorot(k, shape):
            lim = np.sqrt(6.0 / (shape[0] + shape[1]))
            return jax.random.uniform(k, shape, jnp.float32, -lim, lim)
        key = jax.random.key(seed)
        ks = jax.random.split(key, 8)
        grid = np.linspace(-np.pi / 3, np.pi / 3, M, dtype=np.float32)
        theta = np.tile(grid.reshape(1, 1, 1, 1, M), (1, 1, K, H, 1)).astype(np.float32)
        dr = np.geomspace(0.001, 0.1, K - A).astype(np.float32)
        ar = np.geomspace(0.01, 0.1, A).astype(np.float32)
        return {'x': jax.random.normal(ks[0], (B, L, D), jnp.float32), 'in_proj_w': _glorot(ks[1], (D, TOTAL)), 'conv_w': jax.random.normal(ks[2], (CK, 1, TOTAL), jnp.float32) * 0.1, 'conv_b': jnp.zeros((TOTAL,), jnp.float32), 'theta': jnp.asarray(theta), 'decay_slopes': jnp.asarray(np.log(np.exp(dr) - 1.0)), 'anchor_slopes': jnp.asarray(np.log(np.exp(ar) - 1.0)), 'score_scale': jnp.ones((K,), jnp.float32), 'deriv_logits': jnp.asarray([5.0, 0.0, 0.0], jnp.float32), 'norm_scale': jnp.ones((2 * H * M,), jnp.float32), 'W_re': _glorot(ks[3], (H * M, H)), 'W_im': _glorot(ks[4], (H * M, H)), 'out_proj_w': _glorot(ks[5], (D, D))}
    _L0_attn_all = _L0_attn_setup()
    _L0_attn_in = {k: v for k, v in _L0_attn_all.items() if k in ('in_proj_w', 'conv_w', 'conv_b', 'theta', 'decay_slopes', 'anchor_slopes', 'score_scale', 'deriv_logits', 'norm_scale', 'W_re', 'W_im', 'out_proj_w')}
    del _L0_attn_all

    def _L0_xattn_setup():
        import jax, jax.numpy as jnp
        import numpy as np
        import math
        D_MODEL = 256
        NHEAD = 16
        FACTOR = 1
        B, L = (2, 1024)

        def _autocorr_forward(query, key, value, Wq, bq, Wk, bk, Wv, bv, Wo, bo):
            Bq, Lq, d = query.shape
            Lk = key.shape[1]
            H = NHEAD
            Dk = d // H
            Q = (query @ Wq + bq).reshape(Bq, Lq, H, Dk).transpose(0, 2, 1, 3)
            K = (key @ Wk + bk).reshape(Bq, Lk, H, Dk).transpose(0, 2, 1, 3)
            V = (value @ Wv + bv).reshape(Bq, Lk, H, Dk).transpose(0, 2, 1, 3)
            if Lk > Lq:
                K = K[:, :, :Lq, :]
                V = V[:, :, :Lq, :]
            elif Lq > Lk:
                pad = [(0, 0), (0, 0), (0, Lq - Lk), (0, 0)]
                K = jnp.pad(K, pad)
                V = jnp.pad(V, pad)
            Lloc = Lq
            Qf = jnp.fft.rfft(Q, axis=2)
            Kf = jnp.fft.rfft(K, axis=2)
            corr = jnp.fft.irfft(Qf * jnp.conj(Kf), n=Lloc, axis=2)
            corr_mean = corr.mean(axis=-1)
            top_k = min(max(1, int(FACTOR * math.log(Lloc + 1))), Lloc)
            w, idx = jax.lax.top_k(corr_mean, top_k)
            w = jax.nn.softmax(w, axis=-1)
            ar = jnp.arange(Lloc)
            shifted = (ar[None, None, None, :] + idx[..., None]) % Lloc
            rolled = jnp.take_along_axis(V[:, :, None, :, :], shifted[..., None], axis=3)
            out = jnp.einsum('bhk,bhkld->bhld', w, rolled)
            out = out.transpose(0, 2, 1, 3).reshape(Bq, Lq, d)
            return out @ Wo + bo
        key = jax.random.key(seed)
        ks = jax.random.split(key, 12)
        s = 0.02
        inp = {'query': jax.random.normal(ks[0], (B, L, D_MODEL), dtype=jnp.float32), 'key': jax.random.normal(ks[1], (B, L, D_MODEL), dtype=jnp.float32), 'value': jax.random.normal(ks[2], (B, L, D_MODEL), dtype=jnp.float32), 'Wq': jax.random.normal(ks[3], (D_MODEL, D_MODEL), dtype=jnp.float32) * s, 'bq': jnp.zeros((D_MODEL,), dtype=jnp.float32), 'Wk': jax.random.normal(ks[4], (D_MODEL, D_MODEL), dtype=jnp.float32) * s, 'bk': jnp.zeros((D_MODEL,), dtype=jnp.float32), 'Wv': jax.random.normal(ks[5], (D_MODEL, D_MODEL), dtype=jnp.float32) * s, 'bv': jnp.zeros((D_MODEL,), dtype=jnp.float32), 'Wo': jax.random.normal(ks[6], (D_MODEL, D_MODEL), dtype=jnp.float32) * s, 'bo': jnp.zeros((D_MODEL,), dtype=jnp.float32)}
        return inp
    _L0_xattn_all = _L0_xattn_setup()
    _L0_xattn_in = {k: v for k, v in _L0_xattn_all.items() if k in ('Wq', 'bq', 'Wk', 'bk', 'Wv', 'bv', 'Wo', 'bo')}
    del _L0_xattn_all

    def _L0_ffn_setup():
        import jax, jax.numpy as jnp
        import numpy as np
        B, T, D, R, KEXP = (4, 1024, 256, 64, 8)
        RH = max(D, 32)
        SCALE = 0.02

        def _fused_branch(Q_side, K_side, V, W, U, b, router_w1, router_b1, router_w2, router_b2, expert_bias):
            xV = jnp.einsum('btd,kdr->btkr', Q_side, V)
            yW = jnp.einsum('btd,kdr->btkr', K_side, W)
            cum_yW = jnp.cumsum(yW, axis=1)
            prod = xV * cum_yW
            h = jax.nn.gelu(Q_side @ router_w1.T + router_b1, approximate=False)
            logits = h @ router_w2.T + router_b2 + expert_bias
            weights = jax.nn.softmax(logits, axis=-1)
            out = jnp.einsum('btkr,kdr->btd', prod * weights[..., None], U)
            out = out + weights @ b
            n_valid = jnp.arange(1, Q_side.shape[1] + 1, dtype=Q_side.dtype)
            return out / n_valid[None, :, None]
        key = jax.random.key(seed)
        ks = jax.random.split(key, 20)
        x = jax.random.normal(ks[0], (B, T, D), dtype=jnp.float32)
        W_Q = jax.random.normal(ks[1], (D, D), dtype=jnp.float32) * (1.0 / np.sqrt(D))
        W_K = jax.random.normal(ks[2], (D, D), dtype=jnp.float32) * (1.0 / np.sqrt(D))
        W_O = jax.random.normal(ks[3], (D, D), dtype=jnp.float32) * (1.0 / np.sqrt(D))
        W_inv = jnp.eye(D, dtype=jnp.float32) + 0.01 * jax.random.normal(ks[4], (D, D), dtype=jnp.float32)
        V_fwd = jax.random.normal(ks[5], (KEXP, D, R), dtype=jnp.float32) * SCALE
        W_fwd = jax.random.normal(ks[6], (KEXP, D, R), dtype=jnp.float32) * SCALE
        U_fwd = jax.random.normal(ks[7], (KEXP, D, R), dtype=jnp.float32) * SCALE
        b_fwd = jnp.zeros((KEXP, D), dtype=jnp.float32)
        V_inv = jax.random.normal(ks[8], (KEXP, D, R), dtype=jnp.float32) * SCALE
        W_inv_exp = jax.random.normal(ks[9], (KEXP, D, R), dtype=jnp.float32) * SCALE
        U_inv = jax.random.normal(ks[10], (KEXP, D, R), dtype=jnp.float32) * SCALE
        b_inv = jnp.zeros((KEXP, D), dtype=jnp.float32)
        router_w1 = jax.random.normal(ks[11], (RH, D), dtype=jnp.float32) * (1.0 / np.sqrt(D))
        router_b1 = jnp.zeros((RH,), dtype=jnp.float32)
        router_w2 = jax.random.normal(ks[12], (KEXP, RH), dtype=jnp.float32) * (1.0 / np.sqrt(RH))
        router_b2 = jnp.zeros((KEXP,), dtype=jnp.float32)
        alpha_bi = jnp.asarray(0.5, dtype=jnp.float32)
        expert_bias = jnp.zeros((KEXP,), dtype=jnp.float32)
        return dict(x=x, W_Q=W_Q, W_K=W_K, W_O=W_O, W_inv=W_inv, V_fwd=V_fwd, W_fwd=W_fwd, U_fwd=U_fwd, b_fwd=b_fwd, V_inv=V_inv, W_inv_exp=W_inv_exp, U_inv=U_inv, b_inv=b_inv, router_w1=router_w1, router_b1=router_b1, router_w2=router_w2, router_b2=router_b2, alpha_bi=alpha_bi, expert_bias=expert_bias)
    _L0_ffn_all = _L0_ffn_setup()
    _L0_ffn_in = {k: v for k, v in _L0_ffn_all.items() if k in ('W_Q', 'W_K', 'W_O', 'W_inv', 'V_fwd', 'W_fwd', 'U_fwd', 'b_fwd', 'V_inv', 'W_inv_exp', 'U_inv', 'b_inv', 'router_w1', 'router_b1', 'router_w2', 'router_b2', 'alpha_bi', 'expert_bias')}
    del _L0_ffn_all
    return {'x': x, 'ctx_1024': ctx_1024, 'L0_attn_in_proj_w': _L0_attn_in['in_proj_w'], 'L0_attn_conv_w': _L0_attn_in['conv_w'], 'L0_attn_conv_b': _L0_attn_in['conv_b'], 'L0_attn_theta': _L0_attn_in['theta'], 'L0_attn_decay_slopes': _L0_attn_in['decay_slopes'], 'L0_attn_anchor_slopes': _L0_attn_in['anchor_slopes'], 'L0_attn_score_scale': _L0_attn_in['score_scale'], 'L0_attn_deriv_logits': _L0_attn_in['deriv_logits'], 'L0_attn_norm_scale': _L0_attn_in['norm_scale'], 'L0_attn_W_re': _L0_attn_in['W_re'], 'L0_attn_W_im': _L0_attn_in['W_im'], 'L0_attn_out_proj_w': _L0_attn_in['out_proj_w'], 'L0_xattn_Wq': _L0_xattn_in['Wq'], 'L0_xattn_bq': _L0_xattn_in['bq'], 'L0_xattn_Wk': _L0_xattn_in['Wk'], 'L0_xattn_bk': _L0_xattn_in['bk'], 'L0_xattn_Wv': _L0_xattn_in['Wv'], 'L0_xattn_bv': _L0_xattn_in['bv'], 'L0_xattn_Wo': _L0_xattn_in['Wo'], 'L0_xattn_bo': _L0_xattn_in['bo'], 'L0_ffn_W_Q': _L0_ffn_in['W_Q'], 'L0_ffn_W_K': _L0_ffn_in['W_K'], 'L0_ffn_W_O': _L0_ffn_in['W_O'], 'L0_ffn_W_inv': _L0_ffn_in['W_inv'], 'L0_ffn_V_fwd': _L0_ffn_in['V_fwd'], 'L0_ffn_W_fwd': _L0_ffn_in['W_fwd'], 'L0_ffn_U_fwd': _L0_ffn_in['U_fwd'], 'L0_ffn_b_fwd': _L0_ffn_in['b_fwd'], 'L0_ffn_V_inv': _L0_ffn_in['V_inv'], 'L0_ffn_W_inv_exp': _L0_ffn_in['W_inv_exp'], 'L0_ffn_U_inv': _L0_ffn_in['U_inv'], 'L0_ffn_b_inv': _L0_ffn_in['b_inv'], 'L0_ffn_router_w1': _L0_ffn_in['router_w1'], 'L0_ffn_router_b1': _L0_ffn_in['router_b1'], 'L0_ffn_router_w2': _L0_ffn_in['router_w2'], 'L0_ffn_router_b2': _L0_ffn_in['router_b2'], 'L0_ffn_alpha_bi': _L0_ffn_in['alpha_bi'], 'L0_ffn_expert_bias': _L0_ffn_in['expert_bias']}

def reference(x, ctx_1024, L0_attn_in_proj_w, L0_attn_conv_w, L0_attn_conv_b, L0_attn_theta, L0_attn_decay_slopes, L0_attn_anchor_slopes, L0_attn_score_scale, L0_attn_deriv_logits, L0_attn_norm_scale, L0_attn_W_re, L0_attn_W_im, L0_attn_out_proj_w, L0_xattn_Wq, L0_xattn_bq, L0_xattn_Wk, L0_xattn_bk, L0_xattn_Wv, L0_xattn_bv, L0_xattn_Wo, L0_xattn_bo, L0_ffn_W_Q, L0_ffn_W_K, L0_ffn_W_O, L0_ffn_W_inv, L0_ffn_V_fwd, L0_ffn_W_fwd, L0_ffn_U_fwd, L0_ffn_b_fwd, L0_ffn_V_inv, L0_ffn_W_inv_exp, L0_ffn_U_inv, L0_ffn_b_inv, L0_ffn_router_w1, L0_ffn_router_b1, L0_ffn_router_w2, L0_ffn_router_b2, L0_ffn_alpha_bi, L0_ffn_expert_bias):
    import jax
    import jax.numpy as jnp

    def _L0_attn_ref(x, in_proj_w, conv_w, conv_b, theta, decay_slopes, anchor_slopes, score_scale, deriv_logits, norm_scale, W_re, W_im, out_proj_w):
        import jax, jax.numpy as jnp
        import numpy as np
        B, L, D = (2, 512, 256)
        K, M, A = (32, 4, 4)
        H = D // K
        CK = 4
        TOTAL = 2 * D + K

        def _glorot(k, shape):
            lim = np.sqrt(6.0 / (shape[0] + shape[1]))
            return jax.random.uniform(k, shape, jnp.float32, -lim, lim)
        b, l, d = x.shape
        z = x @ in_proj_w
        zp = jnp.pad(z, ((0, 0), (CK - 1, 0), (0, 0)))
        z = jax.lax.conv_general_dilated(zp, conv_w, (1,), 'VALID', dimension_numbers=('NWC', 'WIO', 'NWC'), feature_group_count=TOTAL) + conv_b
        x_val = z[..., :D].reshape(b, l, K, H)
        x_gate = jax.nn.silu(z[..., D:2 * D])
        s_raw = z[..., -K:].reshape(b, l, K, 1)
        pos = jnp.arange(l, dtype=jnp.float32)
        d_slopes = jax.nn.softplus(decay_slopes).reshape(1, 1, K - A, 1)
        dist_d = jnp.maximum(jnp.float32(l - 1) - pos, 0.0)[None, :, None, None]
        w_decay = jnp.exp(-d_slopes * dist_d)
        a_slopes = jax.nn.softplus(anchor_slopes).reshape(1, 1, A, 1)
        w_anchor = jnp.exp(-a_slopes * pos[None, :, None, None])
        time_weight = jnp.concatenate([w_decay, w_anchor], axis=2)
        p = jnp.exp(jnp.clip(score_scale[None, None, :, None] * s_raw, -20.0, 20.0))
        x5 = x_val[..., None]
        phi = x5 * theta
        cos_b, sin_b = (jnp.cos(phi), jnp.sin(phi))
        w = jax.nn.softmax(deriv_logits)
        poly = w[0] + w[1] * x5 - w[2] * jnp.square(x5)
        re_m = poly * cos_b
        im_m = poly * sin_b
        p_w = (p * time_weight)[..., None]
        flat = (b, l, K * H * M)
        merged = jnp.concatenate([(p_w * re_m).reshape(flat), (p_w * im_m).reshape(flat), jnp.broadcast_to(p_w, (b, l, K, H, M)).reshape(flat)], axis=-1)
        num_re, num_im, den = jnp.split(jnp.cumsum(merged, axis=1), 3, axis=-1)
        inv_den = 1.0 / jnp.maximum(den, jnp.float32(0.0001))
        re = (num_re * inv_den).reshape(b, l, K, H * M)
        im = (num_im * inv_den).reshape(b, l, K, H * M)
        mean_sq = (jnp.sum(jnp.square(re), -1) + jnp.sum(jnp.square(im), -1)) / (2.0 * H * M)
        rs = jax.lax.rsqrt(mean_sq[..., None] + 1e-05)
        y = re * rs * norm_scale[:H * M] @ W_re + im * rs * norm_scale[H * M:] @ W_im
        y = y.reshape(b, l, D)
        return y * x_gate @ out_proj_w

    def _L0_xattn_ref(query, key, value, Wq, bq, Wk, bk, Wv, bv, Wo, bo):
        import jax, jax.numpy as jnp
        import numpy as np
        import math
        D_MODEL = 256
        NHEAD = 16
        FACTOR = 1
        B, L = (2, 1024)

        def _autocorr_forward(query, key, value, Wq, bq, Wk, bk, Wv, bv, Wo, bo):
            Bq, Lq, d = query.shape
            Lk = key.shape[1]
            H = NHEAD
            Dk = d // H
            Q = (query @ Wq + bq).reshape(Bq, Lq, H, Dk).transpose(0, 2, 1, 3)
            K = (key @ Wk + bk).reshape(Bq, Lk, H, Dk).transpose(0, 2, 1, 3)
            V = (value @ Wv + bv).reshape(Bq, Lk, H, Dk).transpose(0, 2, 1, 3)
            if Lk > Lq:
                K = K[:, :, :Lq, :]
                V = V[:, :, :Lq, :]
            elif Lq > Lk:
                pad = [(0, 0), (0, 0), (0, Lq - Lk), (0, 0)]
                K = jnp.pad(K, pad)
                V = jnp.pad(V, pad)
            Lloc = Lq
            Qf = jnp.fft.rfft(Q, axis=2)
            Kf = jnp.fft.rfft(K, axis=2)
            corr = jnp.fft.irfft(Qf * jnp.conj(Kf), n=Lloc, axis=2)
            corr_mean = corr.mean(axis=-1)
            top_k = min(max(1, int(FACTOR * math.log(Lloc + 1))), Lloc)
            w, idx = jax.lax.top_k(corr_mean, top_k)
            w = jax.nn.softmax(w, axis=-1)
            ar = jnp.arange(Lloc)
            shifted = (ar[None, None, None, :] + idx[..., None]) % Lloc
            rolled = jnp.take_along_axis(V[:, :, None, :, :], shifted[..., None], axis=3)
            out = jnp.einsum('bhk,bhkld->bhld', w, rolled)
            out = out.transpose(0, 2, 1, 3).reshape(Bq, Lq, d)
            return out @ Wo + bo
        return _autocorr_forward(query, key, value, Wq, bq, Wk, bk, Wv, bv, Wo, bo)

    def _L0_ffn_ref(x, W_Q, W_K, W_O, W_inv, V_fwd, W_fwd, U_fwd, b_fwd, V_inv, W_inv_exp, U_inv, b_inv, router_w1, router_b1, router_w2, router_b2, alpha_bi, expert_bias):
        import jax, jax.numpy as jnp
        import numpy as np
        B, T, D, R, KEXP = (4, 1024, 256, 64, 8)
        RH = max(D, 32)
        SCALE = 0.02

        def _fused_branch(Q_side, K_side, V, W, U, b, router_w1, router_b1, router_w2, router_b2, expert_bias):
            xV = jnp.einsum('btd,kdr->btkr', Q_side, V)
            yW = jnp.einsum('btd,kdr->btkr', K_side, W)
            cum_yW = jnp.cumsum(yW, axis=1)
            prod = xV * cum_yW
            h = jax.nn.gelu(Q_side @ router_w1.T + router_b1, approximate=False)
            logits = h @ router_w2.T + router_b2 + expert_bias
            weights = jax.nn.softmax(logits, axis=-1)
            out = jnp.einsum('btkr,kdr->btd', prod * weights[..., None], U)
            out = out + weights @ b
            n_valid = jnp.arange(1, Q_side.shape[1] + 1, dtype=Q_side.dtype)
            return out / n_valid[None, :, None]
        Q = x @ W_Q.T
        K = x @ W_K.T
        invQ = Q @ W_inv.T
        invK = K @ W_inv.T
        fwd = _fused_branch(Q, K, V_fwd, W_fwd, U_fwd, b_fwd, router_w1, router_b1, router_w2, router_b2, expert_bias)
        inv = _fused_branch(invQ, invK, W_inv_exp, V_inv, U_inv, b_inv, router_w1, router_b1, router_w2, router_b2, expert_bias)
        out = fwd + alpha_bi * inv
        return out @ W_O.T
    x = _layernorm(x + _L0_attn_ref(x, L0_attn_in_proj_w, L0_attn_conv_w, L0_attn_conv_b, L0_attn_theta, L0_attn_decay_slopes, L0_attn_anchor_slopes, L0_attn_score_scale, L0_attn_deriv_logits, L0_attn_norm_scale, L0_attn_W_re, L0_attn_W_im, L0_attn_out_proj_w), axis=-1)
    x = _layernorm(x + _L0_xattn_ref(x, ctx_1024, ctx_1024, L0_xattn_Wq, L0_xattn_bq, L0_xattn_Wk, L0_xattn_bk, L0_xattn_Wv, L0_xattn_bv, L0_xattn_Wo, L0_xattn_bo), axis=-1)
    x = _layernorm(x + _L0_ffn_ref(x, L0_ffn_W_Q, L0_ffn_W_K, L0_ffn_W_O, L0_ffn_W_inv, L0_ffn_V_fwd, L0_ffn_W_fwd, L0_ffn_U_fwd, L0_ffn_b_fwd, L0_ffn_V_inv, L0_ffn_W_inv_exp, L0_ffn_U_inv, L0_ffn_b_inv, L0_ffn_router_w1, L0_ffn_router_b1, L0_ffn_router_w2, L0_ffn_router_b2, L0_ffn_alpha_bi, L0_ffn_expert_bias), axis=-1)
    return x

_drawn_inputs = setup_inputs


def setup_inputs(seed=0):
    import zlib

    import numpy as np

    out = dict(_drawn_inputs(seed))
    spreads = {'L0_attn_conv_b': (0.0, 0.1),
     'L0_attn_score_scale': (1.0, 0.6),
     'L0_attn_norm_scale': (1.0, 0.554),
     'L0_xattn_bq': (0.0, 2.0),
     'L0_xattn_bk': (0.0, 2.0),
     'L0_xattn_bv': (0.0, 0.1),
     'L0_xattn_bo': (0.0, 0.1),
     'L0_ffn_b_fwd': (0.0, 2.0),
     'L0_ffn_b_inv': (0.0, 2.0),
     'L0_ffn_router_b1': (0.0, 2.0),
     'L0_ffn_router_b2': (0.0, 2.0),
     'L0_ffn_expert_bias': (0.0, 2.0)}
    factors = {'L0_attn_theta': 3.36,
     'L0_attn_decay_slopes': 24.016,
     'L0_attn_anchor_slopes': 64.0,
     'L0_attn_W_im': 4.282,
     'L0_ffn_W_Q': 8.0,
     'L0_ffn_W_K': 8.0,
     'L0_ffn_W_O': 8.0,
     'L0_ffn_W_inv': 8.0,
     'L0_ffn_V_fwd': 8.0,
     'L0_ffn_W_fwd': 8.0,
     'L0_ffn_U_fwd': 8.0,
     'L0_ffn_V_inv': 8.0,
     'L0_ffn_W_inv_exp': 8.0,
     'L0_ffn_U_inv': 8.0,
     'L0_ffn_router_w1': 8.0,
     'L0_ffn_router_w2': 8.0}
    for name, (base, spread) in spreads.items():
        noise = np.random.default_rng([zlib.crc32(name.encode()), seed]).standard_normal(out[name].shape)
        drawn = base * np.exp(spread * noise) if base else spread * noise
        out[name] = jnp.asarray(drawn.astype(out[name].dtype))
    for name, factor in factors.items():
        out[name] = (out[name] * factor).astype(out[name].dtype)
    return out
```

```python
import concourse.bass as bass
from concourse import mybir
from contextlib import ExitStack
import math
import numpy as np

F32 = mybir.dt.float32
I32 = mybir.dt.int32
ALU = mybir.AluOpType
ACT = mybir.ActivationFunctionType
AX = mybir.AxisListType

P = 128
B, L, D = 16, 256, 256
SEQ = 2
T = SEQ * L
NCHUNK = B // SEQ
NQ = T // P
DT = D // P
HEADS, HD, M, ANCHORS, TAPS = 32, 8, 4, 4, 4
NZ = 6
XH, XD = 16, 16
TOPK = int(math.log(L + 1))
KEXP, R = 8, 64
NJ = 2 * KEXP * R // P
UNITS = 2 * M
EPS = 1e-5

C_ID, C_BLK, C_HM, C_POS, C_RN, C_M0, C_E8, C_END = 0, 128, 256, 272, 528, 530, 532, 660


class Steps:

    def __init__(self, names):
        self.names = [n if isinstance(n, tuple) else (n,) for n in names]
        self.pos = {n: k + 1 for k, n in enumerate(self.names)}
        self.per = len(self.names)
        self.next = 0
        assert len(self.pos) == self.per

    def tick(self, *name):
        assert self.names[self.next % self.per] == name, (self.names[self.next % self.per], name)
        self.next += 1
        return 1

    def at(self, i, *name):
        return i * self.per + self.pos[name]


Z_ORDER = [4, 0, 5, 1, 2, 3]
PE_A = Steps([("xT", 0), ("xT", 1)] + [("z", j) for j in Z_ORDER]
             + [("sum", u) for u in range(UNITS)] + [("out", 0), ("out", 1)])
VEC_A = Steps(
    sum([[("tap", 4 + h, 2), ("tap", 4 + h, 1), ("tap", 4 + h, 0), ("clip", h), ("expo", h),
          ("tap", h, 2), ("tap", h, 1), ("tap", h, 0), ("turns", 4 * h), ("frac", 4 * h),
          ("turns", 4 * h + 1), ("frac", 4 * h + 1), ("p1", h), ("p2", h), ("g", h),
          ("den", h), ("guard", h)][(0 if h == 0 else 0):]
         for h in range(1)], [])
    + [("tap", 5, 2), ("tap", 5, 1), ("tap", 5, 0), ("clip", 1), ("expo", 1),
       ("tap", 1, 2), ("tap", 1, 1), ("tap", 1, 0), ("p1", 1), ("p2", 1), ("g", 1),
       ("den", 1), ("guard", 1)]
    + [("tap", j, t) for j in (2, 3) for t in (2, 1, 0)]
    + sum([[("im", u), ("re", u)] + ([("turns", u + 2), ("frac", u + 2)] if u + 2 < UNITS else [])
           + [("scan", u)] + ([("w", u // M), ("gf", u // M), ("y", u // M)] if u % M == M - 1 else [])
           for u in range(UNITS)], [])
    + [("res", 0), ("res", 1)] + [("stats", q) for q in range(NQ)] + [("aggr", q) for q in range(NQ)]
    + [("norm", q) for q in range(NQ)])
ACT_A = Steps(
    [("xT", 0), ("xT", 1), ("z", 4), ("z", 0), ("exp", 0), ("z", 5), ("z", 1), ("exp", 1), ("z", 2), ("z", 3),
     ("silu", 0), ("silu", 1), ("e", 0), ("e", 1)]
    + [(n, u) for u in range(2) for n in ("half", "cos", "sin")]
    + sum([([(n, u + 2) for n in ("half", "cos", "sin")] if u + 2 < UNITS else []) + [("sq", u)]
           + ([("ln", u // M), ("f", u // M)] if u % M == M - 1 else []) for u in range(UNITS)], []))
POOL_A = Steps([("var",), ("rstd",)])

SPEC = ["qa", "qb", "ka", "kb", "va", "vb"]
PE_B = Steps([("xf", 0), ("xf", 1), ("cf", 0), ("cf", 1)] + [(s,) for s in SPEC]
             + ["corr", "wt", "wf", ("ot", 0), ("ot", 1), ("out", 0), ("out", 1)])
ACT_B = Steps([("xf", 0), ("xf", 1), ("cf", 0), ("cf", 1)] + [(s,) for s in SPEC]
              + ["exp", "wt", ("ot", 0), ("ot", 1)])
POOL_B = Steps(["res", "bq", "bk", "bv", "var", "rstd"])
VEC_B = Steps(["aabb", "ab", "ba", "heads", "ca", "cb0", "cb1", "cb2",
               "corr", "top", "negmax", "above", "equal", "order", "first", "also", "keep", "weight",
               "inv", "wn", "w1", "w2", "w4", "w3a", "w3", "oa", "ob", "o", ("res", 0), ("res", 1)]
              + [("stats", q) for q in range(NQ)] + [("aggr", q) for q in range(NQ)]
              + [("norm", q) for q in range(NQ)])

PE_C = Steps([("xT", 0), ("xT", 1)] + [("h", n) for n in range(4)] + ["logit", "wT"]
             + sum([[("w", j), ("c", j), ("x", j)] for j in range(NJ)], []) + [("out", 0), ("out", 1)])
ACT_C = Steps([("xT", 0), ("xT", 1)] + [("h", n) for n in range(4)] + ["exp", "wT"]
              + sum([[("w", j), ("c", j)] for j in range(NJ)], []))
POOL_C = Steps([("cw", j) for j in range(NJ)] + ["var", "rstd"])
VEC_C = Steps(["cum", "logit", "max", "sub", "sum", "inv", "weight"] + [("prod", j) for j in range(NJ)]
              + [("res", 0), ("res", 1)] + [("stats", q) for q in range(NQ)]
              + [("aggr", q) for q in range(NQ)] + [("norm", q) for q in range(NQ)])

BANK_A = {("xT", 0): 0, ("xT", 1): 1, ("z", 4): 2, ("z", 0): 0, ("z", 5): 1, ("z", 1): 2, ("z", 2): 0,
          ("z", 3): 1, ("S", 0): 2, ("Y", 0): 0, ("S", 1): 1, ("Y", 1): 2, ("out", 0): 0, ("out", 1): 1}
BANK_B = {("xf", 0): 3, ("xf", 1): 4, ("cf", 0): 3, ("cf", 1): 4, ("qa",): 3, ("qb",): 4, ("ka",): 3,
          ("kb",): 4, ("va",): 3, ("vb",): 4, ("corr",): 3, ("wt",): 4, ("wf",): 3, ("ot", 0): 4,
          ("ot", 1): 3, ("out", 0): 4, ("out", 1): 3}
BANK_C = {("xT", 0): 5, ("xT", 1): 6, ("h", 0): 7, ("h", 1): 5, ("h", 2): 6, ("h", 3): 7, ("logit",): 5,
          ("wT",): 6}
for _j in range(NJ):
    BANK_C.update({("w", _j): 7, ("c", _j): 5, ("x", _j): 6})
BANK_C.update({("out", 0): 7, ("out", 1): 5})


def before(banks, group):
    order = list(banks)
    k = order.index(group)
    mine = [g for g in order if banks[g] == banks[group]]
    n = mine.index(group)
    return (mine[n - 1], False) if n else (mine[-1], True)


def decoder_kernel(nc, x, ctx_in, in_proj, conv_w, conv_b, theta, decay, anchor, score, deriv, norm_sc,
                   w_re, w_im, out_proj, wq, bq, wk, bk, wv, bv, wo, bo, f_q, f_k, f_o, f_inv, v_fwd,
                   w_fwd, u_fwd, b_fwd, v_inv, w_inv, u_inv, b_inv, r_w1, r_b1, r_w2, r_b2, alpha, ebias,
                   consts, dft, idft, expand, select, out):
    ctx = ExitStack()
    with ctx:
        def sb(name, shape, dt=F32):
            return ctx.enter_context(nc.sbuf_tensor(name, shape, dt))

        def sem(name):
            return ctx.enter_context(nc.semaphore(name))

        ctx.enter_context(nc.allow_non_contiguous_dma("small weights, once"))
        cst = sb("cst", [P, C_END])
        ident = cst[:, C_ID:C_ID + P]
        blk = cst[:, C_BLK:C_BLK + P]
        headm = cst[:, C_HM:C_HM + 16]
        pos = cst[:, C_POS:C_POS + L]
        rn = cst[:, C_RN:C_RN + 2]
        m0, m1 = cst[:, C_M0:C_M0 + 1], cst[:, C_M0 + 1:C_M0 + 2]
        e8 = cst[0:HD, C_E8:C_E8 + P]
        e32 = sb("e32", [HEADS, 2, P])
        sel = sb("sel", [2 * KEXP, NJ, P])
        win = sb("win", [P, DT, NZ * P])
        wopj = sb("wopj", [P, DT, D])
        mask = sb("mask", [P, 2 * T], mybir.dt.bfloat16)
        cw = sb("cw", [P, NZ, TAPS])
        cb = sb("cb", [P, NZ])
        thn = sb("thn", [P, 2, M])
        ss = sb("ss", [P, 2])
        lt = sb("lt", [P, 2, L])
        dw = sb("dw", [P, 4])
        wy = sb("wy", [P, 2, M, P])
        wqs, wks, wvs, wos = (sb(n, [P, DT, D]) for n in ("wqs", "wks", "wvs", "wos"))
        bos = sb("bos", [P, D])
        bqkv = sb("bqkv", [1, 3, D])
        fdft = sb("fdft", [P, 2, L])
        fidft = sb("fidft", [P, 2, L])
        mv = sb("mv", [P, DT, 2, KEXP * R])
        mw = sb("mw", [P, DT, 2, KEXP * R])
        mr = sb("mr", [P, DT, 2, D])
        up = sb("up", [P, NJ, D])
        bp = sb("bp", [2 * KEXP, D])
        w2t = sb("w2t", [P, DT, KEXP])
        rb1 = sb("rb1", [P, DT])
        rb2 = sb("rb2", [P, 2, KEXP])
        acol = sb("acol", [P, 2])
        half_ = sb("half_", [P, NQ])
        eps_ = sb("eps_", [P, NQ])
        seen = sb("seen", [P, 3])
        xa = sb("xa", [P, NQ, D])
        xt = sb("xt", [P, DT, T])
        zc = sb("zc", [P, NZ, T])
        g = sb("g", [P, 2, T])
        frac = sb("frac", [P, 2, T])
        hq = sb("hq", [P, 2, T])
        kturn = hq[:, :, :].bitcast(I32)
        den = zc[:, 4:6, :]
        sc = sb("sc", [P, 4, 2, T])
        sq = sb("sq", [P, 2, 2, T])
        xs_a = sb("xs_a", [P, NQ, D])
        x1 = sb("x1", [P, NQ, D])
        cin = sb("cin", [P, NQ, D])
        spec = sb("spec", [P, 4, T])
        qkv = sb("qkv", [P, 6, T])
        x2 = sb("x2", [P, NQ, D])
        BH = SEQ * XH
        rsum = sb("rsum", [P, 4, BH])
        cspec = sb("cspec", [P, 4, BH])
        cor = sb("cor", [BH, 5, L])
        sm = sb("sm", [BH, 16])
        wtt = sb("wtt", [P, 2, BH])
        wspec = sb("wspec", [P, 4, BH])
        x2t = sb("x2t", [P, DT, T])
        cum = sb("cum", [P, DT, T])
        prod = sb("prod", [P, NJ, T])
        hT = prod[:, 0:4, :]
        lg = sb("lg", [P, NQ * 2, KEXP])
        ls = sb("ls", [P, 2, NQ * 2])
        wT = sb("wT", [2 * KEXP, T])
        ws = sb("ws", [P, 2, T])
        cs = sb("cs", [P, 2, T])
        xs_c = sb("xs_c", [P, NQ, D])
        st = [sb(f"st{n}", [P, NQ, 6]) for n in "abc"]
        mvr = [sb(f"mvr{n}", [P, NQ, 2]) for n in "abc"]
        rs = [sb(f"rs{n}", [P, 2, NQ]) for n in "abc"]
        fq = spec[:, 0, :].rearrange("p (t n) -> p t n", t=DT)
        fk = spec[:, 1, :].rearrange("p (t n) -> p t n", t=DT)
        fo = spec[:, 2, :].rearrange("p (t n) -> p t n", t=DT)
        fi = spec[:, 3, :].rearrange("p (t n) -> p t n", t=DT)
        raw_v = [prod[:, 2 * n:2 * n + 2, :] for n in range(4)]
        raw_u = [qkv[:, 2 * n:2 * n + 2, :] for n in range(2)]
        fr = qkv[:, 4, :].rearrange("p (t n) -> p t n", t=DT)
        fot = qkv[:, 5, :].rearrange("p (t n) -> p t n", t=DT)
        fit = x2t[:, 0, :].rearrange("p (t n) -> p t n", t=DT)
        frt = x2t[:, 1, :].rearrange("p (t n) -> p t n", t=DT)
        nqt = cum[:, 0, :].rearrange("p (t n) -> p t n", t=DT)
        nkt = cum[:, 1, :].rearrange("p (t n) -> p t n", t=DT)
        rw2 = xs_c[0:KEXP, 0, :]
        b16 = xs_c[0:2 * KEXP, 1, :]
        bt = xs_c[:, 2, 0:DT * 2 * KEXP].rearrange("p (t n) -> p t n", t=DT)
        c32 = x1[0:HEADS, 0, 0:8]
        c32t = x1[0:HEADS, 1, 0:16]
        y8 = x1[0:HD, 2, 0:2 * M * HD].rearrange("p (c m n) -> p c m n", c=2, m=M)
        y8s = x1[0:HD, 3, 0:2 * M * HD].rearrange("p (c m n) -> p c m n", c=2, m=M)
        n8 = x1[0:HD, 3, 64:64 + 2 * M].rearrange("p (c m) -> p c m", c=2)
        col7 = x1[:, 1, 32:48].rearrange("p (a b) -> p a b", a=2)
        ybase = x1[:, 2, 64:64 + 2 * M * HD]
        dl = x1[:, 1, 64:72]
        lns = x1[:, 1, 80:84]

        ps = ctx.enter_context(nc.psum_tensor("ps", [P, 8, T], F32))

        pe_a, act_a, vec_a, pool_a = (sem(n) for n in ("pe_a", "act_a", "vec_a", "pool_a"))
        pe_b, act_b, vec_b, pool_b = (sem(n) for n in ("pe_b", "act_b", "vec_b", "pool_b"))
        pe_c, act_c, vec_c, pool_c = (sem(n) for n in ("pe_c", "act_c", "vec_c", "pool_c"))
        xa_in, xr_in, ctx_loaded, stored = (sem(n) for n in ("xa_in", "xr_in", "ctx_loaded", "stored"))
        w_attn, w_x, w_raw = (sem(n) for n in ("w_attn", "w_x", "w_raw"))
        pe_s, vec_s, act_s, chain = (sem(n) for n in ("pe_s", "vec_s", "act_s", "chain"))
        ready = sem("ready")
        block = ctx.enter_context(nc.Block())

        def tok(ap, i):
            return ap[i * SEQ:(i + 1) * SEQ] if isinstance(i, int) else ap[bass.ds(i * SEQ, SEQ)]

        def rows(ap, i):
            return tok(ap, i).rearrange("b (h p) d -> p (b h) d", p=P)

        def bb(ap, shape):
            return ap.broadcast_to(shape)

        n_attn = n_x = n_raw = 0

        LOADS_A, LOADS_X, LOADS_RAW = [], [], []
        LOADS_A += [(cst[:, :], consts), (e32[:, :, :], expand)]
        LOADS_A += [(win[:, :, 0:2 * D], in_proj[:, 0:2 * D].rearrange("(t p) n -> p t n", p=P)),
                    (g[:, 0, 0:DT * HEADS].rearrange("p (t n) -> p t n", t=DT),
                     in_proj[:, 2 * D:2 * D + HEADS].rearrange("(t p) n -> p t n", p=P)),
                    (wopj[:, :, :], out_proj.rearrange("(t p) n -> p t n", p=P))]
        for j in range(4):
            LOADS_A += [(cw[:, j, :], conv_w[:, 0, j * P:(j + 1) * P].rearrange("a p -> p a"))]
        LOADS_A += [(cb[:, 0:4], conv_b[0:2 * D].rearrange("(t p) -> p t", p=P)),
                    (thn[:, :, :], theta[0, 0].rearrange("(t k) h m -> (k h) t m", t=2)),
                    (c32[:, 0:4], conv_w[:, 0, 2 * D:].rearrange("a p -> p a")),
                    (c32[:, 4:5], conv_b[2 * D:].rearrange("(p a) -> p a", a=1)),
                    (c32[:, 5:6], score.rearrange("(p a) -> p a", a=1)),
                    (c32[0:HEADS - ANCHORS, 6:7], decay.rearrange("(p a) -> p a", a=1)),
                    (c32[HEADS - ANCHORS:HEADS, 6:7], anchor.rearrange("(p a) -> p a", a=1)),
                    (y8[:, 0, :, :], w_re.rearrange("(h m) n -> h m n", m=M)),
                    (y8[:, 1, :, :], w_im.rearrange("(h m) n -> h m n", m=M)),
                    (n8[:, :, :], norm_sc.rearrange("(c h m) -> h c m", c=2, m=M)),
                    (dl[:, 0:3], deriv.rearrange("(a n) -> a n", a=1).broadcast_to([P, 3]))]
        for dst, src in ((wqs, wq), (wks, wk), (wvs, wv), (wos, wo)):
            LOADS_X += [(dst[:, :, :], src.rearrange("(t p) n -> p t n", p=P))]
        LOADS_X += [(fdft[:, :, :], dft.rearrange("(t p) n -> p t n", p=P)),
                    (fidft[:, :, :], idft.rearrange("t p n -> p t n")),
                    (bos[:, :], bo.rearrange("(a n) -> a n", a=1).broadcast_to([P, D]))]
        for n, src in enumerate((bq, bk, bv)):
            LOADS_X += [(bqkv[:, n, :], src.rearrange("(a n) -> a n", a=1))]
        for dst, src in ((fq, f_q), (fk, f_k), (fo, f_o), (fi, f_inv), (fr, r_w1)):
            LOADS_RAW += [(dst, src.rearrange("(t p) n -> p t n", p=P))]
        for dst, src in list(zip(raw_v, (v_fwd, w_fwd, w_inv, v_inv))) + list(zip(raw_u, (u_fwd, u_inv))):
            for t in range(DT):
                LOADS_RAW += [(dst[:, t, :].rearrange("p (k r) -> p k r", k=KEXP),
                               src[:, t * P:(t + 1) * P, :].rearrange("k p r -> p k r"))]
        LOADS_RAW += [(rw2, r_w2), (b16[0:KEXP, :], b_fwd), (b16[KEXP:2 * KEXP, :], b_inv),
                      (sel[:, :, :], select), (rb1[:, :], r_b1.rearrange("(t p) -> p t", p=P)),
                      (rb2[:, 0, :], r_b2.rearrange("(a n) -> a n", a=1).broadcast_to([P, KEXP])),
                      (rb2[:, 1, :], ebias.rearrange("(a n) -> a n", a=1).broadcast_to([P, KEXP])),
                      (acol[:, 0:1], alpha.rearrange("(a n) -> a n", a=1).broadcast_to([P, 1]))]

        @block.sync
        def _(sp):
            for dst, src in LOADS_A:
                sp.dma_start(dst, src).then_inc(w_attn, 16)

            def load_x(i):
                if not isinstance(i, int) or i > 0:
                    sp.wait_ge(pe_a, PE_A.at(i - 1, "xT", 1))
                sp.dma_start(xa[:, :, :], rows(x, i)).then_inc(xa_in, 16)

            def load_residual(i):
                if not isinstance(i, int) or i > 0:
                    sp.wait_ge(vec_a, VEC_A.at(i - 1, "norm", NQ - 1))
                sp.dma_start(xs_a[:, :, :], rows(x, i)).then_inc(xr_in, 16)

            def load_ctx(i):
                if not isinstance(i, int) or i > 0:
                    sp.wait_ge(pe_b, PE_B.at(i - 1, "cf", 1))
                sp.dma_start(cin[:, :, :], rows(ctx_in, i)).then_inc(ctx_loaded, 16)

            def store(i):
                sp.wait_ge(vec_c, VEC_C.at(i, "norm", NQ - 1))
                sp.dma_start(rows(out, i), xs_c[:, :, :]).then_inc(stored, 16)

            load_x(0)
            load_residual(0)
            for dst, src in LOADS_X:
                sp.dma_start(dst, src).then_inc(w_x, 16)
            load_ctx(0)
            for dst, src in LOADS_RAW:
                sp.dma_start(dst, src).then_inc(w_raw, 16)
            load_x(1)
            load_residual(1)
            load_ctx(1)
            load_x(2)
            load_residual(2)
            load_ctx(2)
            load_x(3)
            load_residual(3)
            store(0)
            with sp.Fori(3, NCHUNK - 1) as i:
                load_ctx(i)
                load_x(i + 1)
                load_residual(i + 1)
                store(i - 2)
            load_ctx(NCHUNK - 1)
            store(NCHUNK - 3)
            store(NCHUNK - 2)
            store(NCHUNK - 1)
            sp.wait_ge(stored, 16 * NCHUNK)

        NS = 0

        SETUP = ([("col", 0), ("col", 1), ("y", 0), ("ot", 0), ("ot", 1), ("it", 0), ("it", 1),
                  ("rt", 0), ("rt", 1), ("w2", 0), ("bt", 0), ("nq", 0), ("nq", 1), ("nk", 0), ("nk", 1)]
                 + [(m, br, t) for m in ("mv", "mw", "mr") for br in range(2) for t in range(DT)]
                 + [("up", j) for j in range(NJ)] + [("bp", 0)])

        def s_at(*name):
            return SETUP.index(name) + 1

        @block.tensor
        def _(pe):
            mm = nc.tensor.matmul

            def group(*name):
                k = SETUP.index(name)
                if k >= 8:
                    pe.wait_ge(vec_s, k - 7)
                return ps[:, k % 8, :]

            pe.wait_ge(w_attn, 16 * len(LOADS_A))
            pe.wait_ge(chain, SETUP_COL)
            for h in range(2):
                o = group("col", h)
                mm(o[:, 0:8], e32[:, h, :], c32t[:, 0:8], start=True, stop=True).then_inc(pe_s, 1)
            o = group("y", 0)
            mm(o[:, 0:2 * M * HD], e8, y8s.rearrange("p c m n -> p (c m n)"), start=True, stop=True)\
                .then_inc(pe_s, 1)
            pe.wait_ge(w_raw, 16 * len(LOADS_RAW))
            for name, src in (("ot", fo), ("it", fi), ("rt", fr)):
                for t in range(DT):
                    o = group(name, t)
                    for r in range(DT):
                        last = nc.tensor.transpose(o[:, r * P:(r + 1) * P], src[:, r, t * P:(t + 1) * P], ident)
                    last.then_inc(pe_s, 1)
            o = group("w2", 0)
            for t in range(DT):
                last = nc.tensor.transpose(o[:, t * KEXP:(t + 1) * KEXP], rw2[:, t * P:(t + 1) * P],
                                           ident[0:KEXP, 0:KEXP])
            last.then_inc(pe_s, 1)
            o = group("bt", 0)
            for t in range(DT):
                last = nc.tensor.transpose(o[:, t * 16:(t + 1) * 16], b16[:, t * P:(t + 1) * P], ident[0:16, 0:16])
            last.then_inc(pe_s, 1)

            def product(dst, lhs, rhs):
                for t in range(DT):
                    last = mm(dst, lhs(t), rhs(t), start=(t == 0), stop=(t == DT - 1))
                return last

            pe.wait_ge(vec_s, s_at("it", 1))
            for name, w in (("nq", fq), ("nk", fk)):
                for t in range(DT):
                    o = group(name, t)
                    product(o[:, 0:D], lambda r: fit[:, r, t * P:(t + 1) * P], lambda r: w[:, r, :])\
                        .then_inc(pe_s, 1)
            for name, lhs, rhs in (("mv", (fq, nqt), (raw_v[0], raw_v[2])),
                                   ("mw", (fk, nkt), (raw_v[1], raw_v[3])), ("mr", (fq, nqt), (frt, frt))):
                for br in range(2):
                    if name == "mv" and br == 1:
                        pe.wait_ge(vec_s, s_at("nk", 1))
                    for t in range(DT):
                        o = group(name, br, t)
                        n = rhs[br][:, 0, :].free_size() if False else (D if name == "mr" else KEXP * R)
                        product(o[:, 0:n], lambda r: lhs[br][:, r, t * P:(t + 1) * P],
                                lambda r: rhs[br][:, r, :]).then_inc(pe_s, 1)
            for j in range(NJ):
                o = group("up", j)
                u, c = raw_u[j // 4], (j % 4) * P
                product(o[:, 0:D], lambda r: u[:, r, c:c + P], lambda r: fot[:, r, :]).then_inc(pe_s, 1)
            o = group("bp", 0)
            product(o[0:16, 0:D], lambda r: bt[:, r, :], lambda r: fot[:, r, :]).then_inc(pe_s, 1)
            pe.wait_ge(ready, 1)

            def free_a(i, *name):
                prev, old = before(BANK_A, name)
                if old:
                    if isinstance(i, int) and i == 0:
                        return ps[:, BANK_A[name], :]
                    i = i - 1
                kind, n = prev
                if kind == "xT":
                    pe.wait_ge(act_a, ACT_A.at(i, "xT", n))
                elif kind == "z":
                    pe.wait_ge(vec_a, VEC_A.at(i, "tap", n, 0))
                elif kind == "S":
                    pe.wait_ge(vec_a, VEC_A.at(i, "w", n))
                elif kind == "Y":
                    pe.wait_ge(vec_a, VEC_A.at(i, "y", n))
                else:
                    pe.wait_ge(vec_a, VEC_A.at(i, "res", n))
                return ps[:, BANK_A[name], :]

            def free_b(i, *name):
                prev, old = before(BANK_B, name)
                if old:
                    if isinstance(i, int) and i == 0:
                        return ps[:, BANK_B[name], :]
                    i = i - 1
                if prev[0] in ("corr", "out"):
                    pe.wait_ge(vec_b, VEC_B.at(i, *(prev if prev[0] == "corr" else ("res", prev[1]))))
                elif prev[0] == "wf":
                    pe.wait_ge(vec_b, VEC_B.at(i, "w3"))
                else:
                    pe.wait_ge(act_b, ACT_B.at(i, *prev))
                return ps[:, BANK_B[name], :]

            def free_c(i, *name):
                prev, old = before(BANK_C, name)
                if old:
                    if isinstance(i, int) and i == 0:
                        return ps[:, BANK_C[name], :]
                    i = i - 1
                if prev[0] == "logit":
                    pe.wait_ge(vec_c, VEC_C.at(i, "logit"))
                elif prev[0] == "x":
                    pe.wait_ge(vec_c, VEC_C.at(i, "prod", prev[1]))
                elif prev[0] == "out":
                    pe.wait_ge(vec_c, VEC_C.at(i, "res", prev[1]))
                else:
                    pe.wait_ge(act_c, ACT_C.at(i, *prev))
                return ps[:, BANK_C[name], :]

            def a_project(i):
                pe.wait_ge(xa_in, 16 * i + 16)
                for t in range(DT):
                    o = free_a(i, "xT", t)
                    for q in range(NQ):
                        last = nc.tensor.transpose(o[:, q * P:(q + 1) * P], xa[:, q, t * P:(t + 1) * P], ident)
                    last.then_inc(pe_a, PE_A.tick("xT", t))
                for j in Z_ORDER:
                    o = free_a(i, "z", j)
                    pe.wait_ge(act_a, ACT_A.at(i, "xT", 1))
                    for t in range(DT):
                        last = mm(o, win[:, t, j * P:(j + 1) * P], xt[:, t, :], start=(t == 0), stop=(t == DT - 1))
                    last.then_inc(pe_a, PE_A.tick("z", j))

            def a_sums(i, u):
                h, m = divmod(u, M)
                if m == 0:
                    free_a(i, "S", h)
                    free_a(i, "Y", h)
                s, y = ps[:, BANK_A[("S", h)], :], ps[:, BANK_A[("Y", h)], :]
                pe.wait_ge(vec_a, VEC_A.at(i, "scan", u))
                for c in range(2):
                    mm(y, wy[:, 1 - c, m, :], sc[:, u % 4, c, :], start=(m == 0 and c == 0), stop=(m == M - 1 and c == 1))
                pe.wait_ge(act_a, ACT_A.at(i, "sq", u))
                for c in range(2):
                    last = mm(s, blk, sq[:, u % 2, c, :], start=(m == 0 and c == 0), stop=(m == M - 1 and c == 1))
                last.then_inc(pe_a, PE_A.tick("sum", u))

            def a_out(i):
                pe.wait_ge(vec_a, VEC_A.at(i, "y", 1))
                for n in range(2):
                    o = free_a(i, "out", n)
                    for q in range(2 * n, 2 * n + 2):
                        for t in range(DT):
                            last = mm(o[:, (q % 2) * D:(q % 2 + 1) * D], zc[:, 2 + t, q * P:(q + 1) * P],
                                      wopj[:, t, :], start=(t == 0), stop=(t == DT - 1))
                    last.then_inc(pe_a, PE_A.tick("out", n))

            def b_spectra(i):
                pe.wait_ge(vec_a, VEC_A.at(i, "norm", NQ - 1))
                if not isinstance(i, int) or i > 0:
                    pe.wait_ge(pe_b, PE_B.at(i - 1, "ot", 1)) if False else None
                for name, src in (("xf", x1), ("cf", cin)):
                    if name == "cf":
                        pe.wait_ge(ctx_loaded, 16 * i + 16)
                    for t in range(DT):
                        o = free_b(i, name, t)
                        for b in range(SEQ):
                            for h in range(2):
                                last = mm(o[:, b * L:(b + 1) * L], src[:, 2 * b + h, t * P:(t + 1) * P],
                                          fdft[:, h, :], start=(h == 0), stop=(h == 1))
                        last.then_inc(pe_b, PE_B.tick(name, t))
                for k, name in enumerate(SPEC):
                    o = free_b(i, name)
                    first = 0 if name[0] == "q" else 2
                    w = {"q": wqs, "k": wks, "v": wvs}[name[0]]
                    pe.wait_ge(act_b, ACT_B.at(i, "xf" if first == 0 else "cf", 1))
                    for b in range(SEQ):
                        for t in range(DT):
                            c = b * L + (k % 2) * P
                            last = mm(o[:, b * D:(b + 1) * D], spec[:, first + t, c:c + P], w[:, t, :],
                                      start=(t == 0), stop=(t == DT - 1))
                    last.then_inc(pe_b, PE_B.tick(name))

            def b_corr(i):
                o = free_b(i, "corr")
                pe.wait_ge(vec_b, VEC_B.at(i, "cb2"))
                for part in range(2):
                    last = mm(o[0:BH, 0:L], cspec[:, part, :], fidft[:, part, :], start=(part == 0), stop=(part == 1))
                last.then_inc(pe_b, PE_B.tick("corr"))

            def b_weights(i):
                o = free_b(i, "wt")
                pe.wait_ge(vec_b, VEC_B.at(i, "wn"))
                for h in range(2):
                    last = mm(o[:, h * BH:(h + 1) * BH], cor[:, 0, h * P:(h + 1) * P], ident[0:BH, 0:BH],
                              start=True, stop=True)
                last.then_inc(pe_b, PE_B.tick("wt"))
                o = free_b(i, "wf")
                pe.wait_ge(act_b, ACT_B.at(i, "wt"))
                for part in range(2):
                    for h in range(2):
                        last = mm(o[:, part * BH:(part + 1) * BH], fdft[:, h, part * P:(part + 1) * P], wtt[:, h, :],
                                  start=(h == 0), stop=(h == 1))
                last.then_inc(pe_b, PE_B.tick("wf"))

            def b_back(i):
                for t in range(DT):
                    o = free_b(i, "ot", t)
                    pe.wait_ge(vec_b, VEC_B.at(i, "o"))
                    for b in range(SEQ):
                        for part in range(2):
                            c = b * D + t * P
                            last = mm(o[:, b * L:(b + 1) * L], qkv[:, part, c:c + P], fidft[:, part, :],
                                      start=(part == 0), stop=(part == 1))
                    last.then_inc(pe_b, PE_B.tick("ot", t))

            def b_out(i):
                for n in range(2):
                    o = free_b(i, "out", n)
                    pe.wait_ge(act_b, ACT_B.at(i, "ot", 1))
                    for q in range(2 * n, 2 * n + 2):
                        for t in range(DT):
                            last = mm(o[:, (q % 2) * D:(q % 2 + 1) * D], spec[:, t, q * P:(q + 1) * P],
                                      wos[:, t, :], start=(t == 0), stop=(t == DT - 1))
                    last.then_inc(pe_b, PE_B.tick("out", n))

            def c_router(i):
                pe.wait_ge(vec_b, VEC_B.at(i, "norm", NQ - 1))
                for t in range(DT):
                    o = free_c(i, "xT", t)
                    for q in range(NQ):
                        last = nc.tensor.transpose(o[:, q * P:(q + 1) * P], x2[:, q, t * P:(t + 1) * P], ident)
                    last.then_inc(pe_c, PE_C.tick("xT", t))
                for n in range(4):
                    br, r = divmod(n, 2)
                    o = free_c(i, "h", n)
                    pe.wait_ge(act_c, ACT_C.at(i, "xT", 1))
                    for t in range(DT):
                        last = mm(o, mr[:, t, br, r * P:(r + 1) * P], x2t[:, t, :], start=(t == 0), stop=(t == 1))
                    last.then_inc(pe_c, PE_C.tick("h", n))

            def c_logits(i):
                o = free_c(i, "logit")
                pe.wait_ge(act_c, ACT_C.at(i, "h", 3))
                for q in range(NQ):
                    for br in range(2):
                        c = (q * 2 + br) * KEXP
                        for r in range(DT):
                            last = mm(o[:, c:c + KEXP], hT[:, 2 * br + r, q * P:(q + 1) * P], w2t[:, r, :],
                                      start=(r == 0), stop=(r == 1))
                last.then_inc(pe_c, PE_C.tick("logit"))

            def c_weights(i):
                o = free_c(i, "wT")
                pe.wait_ge(vec_c, VEC_C.at(i, "weight"))
                for q in range(NQ):
                    last = nc.tensor.transpose(o[0:16, q * P:(q + 1) * P],
                                               lg[:, 2 * q:2 * q + 2, :].rearrange("p a b -> p (a b)"), ident)
                last.then_inc(pe_c, PE_C.tick("wT"))

            def c_tile(i, j):
                br, c = j // 4, (j % 4) * P
                o = free_c(i, "w", j)
                pe.wait_ge(act_c, ACT_C.at(i, "wT"))
                mm(o, sel[:, j, :], wT[:, :], start=True, stop=True).then_inc(pe_c, PE_C.tick("w", j))
                o = free_c(i, "c", j)
                pe.wait_ge(vec_c, VEC_C.at(i, "cum"))
                for t in range(DT):
                    last = mm(o, mw[:, t, br, c:c + P], cum[:, t, :], start=(t == 0), stop=(t == 1))
                last.then_inc(pe_c, PE_C.tick("c", j))
                o = free_c(i, "x", j)
                for t in range(DT):
                    last = mm(o, mv[:, t, br, c:c + P], x2t[:, t, :], start=(t == 0), stop=(t == 1))
                last.then_inc(pe_c, PE_C.tick("x", j))

            def c_out(i):
                for n in range(2):
                    o = free_c(i, "out", n)
                    pe.wait_ge(vec_c, VEC_C.at(i, "prod", NJ - 1))
                    for q in range(2 * n, 2 * n + 2):
                        d = o[:, (q % 2) * D:(q % 2 + 1) * D]
                        for j in range(NJ):
                            mm(d, prod[:, j, q * P:(q + 1) * P], up[:, j, :], start=(j == 0), stop=False)
                        last = mm(d, wT[:, q * P:(q + 1) * P], bp[:, :], start=False, stop=True)
                    last.then_inc(pe_c, PE_C.tick("out", n))

            def turn(a, b, c):
                if a is not None:
                    a_project(a)
                if b is not None:
                    b_spectra(b)
                if c is not None:
                    c_router(c)
                    c_logits(c)
                    c_weights(c)
                for u in range(UNITS):
                    if b is not None and u == 2:
                        b_corr(b)
                    if b is not None and u == 4:
                        b_weights(b)
                    if b is not None and u == 6:
                        b_back(b)
                        b_out(b)
                    if c is not None:
                        c_tile(c, u)
                    if a is not None:
                        a_sums(a, u)
                if c is not None:
                    c_out(c)
                if a is not None:
                    a_out(a)

            turn(0, None, None)
            turn(1, 0, None)
            turn(2, 1, 0)
            with pe.Fori(3, NCHUNK) as i:
                turn(i, i - 1, i - 2)
            turn(None, NCHUNK - 1, NCHUNK - 2)
            turn(None, None, NCHUNK - 1)

        @block.scalar
        def _(act):
            A = nc.scalar.activation
            act.wait_ge(chain, 2)
            A(c32t[:, 9:10], c32t[:, 8:9], ACT.Exp).then_inc(act_s, 1)
            act.wait_ge(chain, 3)
            A(c32t[:, 11:12], c32t[:, 10:11], ACT.Ln).then_inc(act_s, 1)
            act.wait_ge(chain, SETUP_DERIV)
            A(dl[:, 4:7], dl[:, 0:3], ACT.Exp).then_inc(act_s, 1)
            act.wait_ge(ready, 1)

            def a_front(i):
                for t in range(DT):
                    act.wait_ge(pe_a, PE_A.at(i, "xT", t))
                    if t == 0 and (not isinstance(i, int) or i > 0):
                        pass
                    A(xt[:, t, :], ps[:, BANK_A[("xT", t)], :], ACT.Copy).then_inc(act_a, ACT_A.tick("xT", t))

                def z(j):
                    act.wait_ge(pe_a, PE_A.at(i, "z", j))
                    if not isinstance(i, int) or i > 0:
                        if j in (2, 3):
                            act.wait_ge(pe_a, PE_A.at(i - 1, "out", 1))
                        elif j < 2:
                            act.wait_ge(vec_a, VEC_A.at(i - 1, "frac", UNITS - 1))
                        else:
                            act.wait_ge(vec_a, VEC_A.at(i - 1, "gf", j - 4))
                    A(zc[:, j, :], ps[:, BANK_A[("z", j)], :], ACT.Identity, bias=cb[:, j:j + 1],
                      scale=cw[:, j, 3:4]).then_inc(act_a, ACT_A.tick("z", j))

                def p(h):
                    act.wait_ge(vec_a, VEC_A.at(i, "expo", h))
                    A(zc[:, 4 + h, :], zc[:, 4 + h, :], ACT.Exp).then_inc(act_a, ACT_A.tick("exp", h))

                z(4)
                z(0)
                p(0)
                z(5)
                z(1)
                p(1)
                z(2)
                z(3)
                for h in range(2):
                    act.wait_ge(vec_a, VEC_A.at(i, "tap", 2 + h, 0))
                    A(zc[:, 2 + h, :], zc[:, 2 + h, :], ACT.Silu).then_inc(act_a, ACT_A.tick("silu", h))
                for h in range(2):
                    act.wait_ge(vec_a, VEC_A.at(i, "guard", h))
                    A(den[:, h, :], den[:, h, :], ACT.Square, scale=math.sqrt(EPS)).then_inc(act_a, ACT_A.tick("e", h))

            def a_angles(i, u):
                act.wait_ge(vec_a, VEC_A.at(i, "frac", u))
                if u >= 2:
                    act.wait_ge(vec_a, VEC_A.at(i, "re", u - 2))
                elif not isinstance(i, int) or i > 0:
                    act.wait_ge(vec_a, VEC_A.at(i - 1, "re", UNITS - 2 + u))
                A(hq[:, u % 2, :], frac[:, u % 2, :], ACT.Sin, scale=math.pi).then_inc(act_a, ACT_A.tick("half", u))
                act.wait_ge(act_a, ACT_A.at(i, "half", u))
                A(hq[:, u % 2, :], hq[:, u % 2, :], ACT.Square, scale=math.sqrt(2.0)).then_inc(act_a, ACT_A.tick("cos", u))
                if u >= 4:
                    pe_i, pe_u = i, u - 4
                else:
                    pe_i, pe_u = i - 1, u + 4
                if u >= 4 or not isinstance(i, int) or i > 0:
                    pass
                    act.wait_ge(pe_a, PE_A.at(pe_i, "sum", pe_u))
                A(sc[:, u % 4, 0, :], frac[:, u % 2, :], ACT.Sin, scale=2.0 * math.pi)\
                    .then_inc(act_a, ACT_A.tick("sin", u))

            def a_squares(i, u):
                act.wait_ge(vec_a, VEC_A.at(i, "scan", u))
                if u >= 2:
                    act.wait_ge(pe_a, PE_A.at(i, "sum", u - 2))
                elif not isinstance(i, int) or i > 0:
                    act.wait_ge(pe_a, PE_A.at(i - 1, "sum", UNITS - 2 + u))
                A(sq[:, u % 2, :, :], sc[:, u % 4, :, :], ACT.Square, scale=1.0 / math.sqrt(2.0 * HD * M))\
                    .then_inc(act_a, ACT_A.tick("sq", u))

            def a_norm(i, h):
                act.wait_ge(vec_a, VEC_A.at(i, "w", h))
                A(den[:, h, :], den[:, h, :], ACT.Ln).then_inc(act_a, ACT_A.tick("ln", h))
                act.wait_ge(act_a, ACT_A.at(i, "ln", h))
                A(den[:, h, :], den[:, h, :], ACT.Exp, scale=-0.5).then_inc(act_a, ACT_A.tick("f", h))

            def b_spectra(i):
                for name, first in (("xf", 0), ("cf", 2)):
                    for t in range(DT):
                        act.wait_ge(pe_b, PE_B.at(i, name, t))
                        if t == 0 and first == 0 and (not isinstance(i, int) or i > 0):
                            act.wait_ge(pe_b, PE_B.at(i - 1, "out", 1))
                            act.wait_ge(vec_b, VEC_B.at(i - 1, "o"))
                        A(spec[:, first + t, :], ps[:, BANK_B[(name, t)], :], ACT.Copy)\
                            .then_inc(act_b, ACT_B.tick(name, t))
                for k, name in enumerate(SPEC):
                    act.wait_ge(pe_b, PE_B.at(i, name))
                    if k == 0 and (not isinstance(i, int) or i > 0):
                        act.wait_ge(pe_b, PE_B.at(i - 1, "ot", 1))
                    A(qkv[:, k, :], ps[:, BANK_B[(name,)], :], ACT.Copy).then_inc(act_b, ACT_B.tick(name))

            def b_exp(i):
                act.wait_ge(vec_b, VEC_B.at(i, "negmax"))
                A(cor[:, 4, :], cor[:, 0, :], ACT.Exp, bias=sm[:, 8:9]).then_inc(act_b, ACT_B.tick("exp"))

            def b_wt(i):
                act.wait_ge(pe_b, PE_B.at(i, "wt"))
                A(wtt[:, :, :], ps[:, BANK_B[("wt",)], 0:2 * BH].rearrange("p (a b) -> p a b", a=2), ACT.Copy)\
                    .then_inc(act_b, ACT_B.tick("wt"))

            def b_back(i):
                for t in range(DT):
                    act.wait_ge(pe_b, PE_B.at(i, "ot", t))
                    if t == 0:
                        act.wait_ge(vec_b, VEC_B.at(i, "o"))
                    A(spec[:, t, :], ps[:, BANK_B[("ot", t)], :], ACT.Copy).then_inc(act_b, ACT_B.tick("ot", t))

            def c_front(i):
                for t in range(DT):
                    act.wait_ge(pe_c, PE_C.at(i, "xT", t))
                    A(x2t[:, t, :], ps[:, BANK_C[("xT", t)], :], ACT.Copy).then_inc(act_c, ACT_C.tick("xT", t))
                for n in range(4):
                    act.wait_ge(pe_c, PE_C.at(i, "h", n))
                    if n == 0 and (not isinstance(i, int) or i > 0):
                        act.wait_ge(pe_c, PE_C.at(i - 1, "out", 1))
                    A(hT[:, n, :], ps[:, BANK_C[("h", n)], :], ACT.Gelu, bias=rb1[:, n % 2:n % 2 + 1])\
                        .then_inc(act_c, ACT_C.tick("h", n))

            def c_exp(i):
                act.wait_ge(vec_c, VEC_C.at(i, "sub"))
                A(lg[:, :, :], lg[:, :, :], ACT.Exp).then_inc(act_c, ACT_C.tick("exp"))
                act.wait_ge(pe_c, PE_C.at(i, "wT"))
                if not isinstance(i, int) or i > 0:
                    pass
                A(wT[:, :], ps[0:16, BANK_C[("wT",)], :], ACT.Copy).then_inc(act_c, ACT_C.tick("wT"))

            def c_tile(i, j):
                act.wait_ge(pe_c, PE_C.at(i, "w", j))
                if j >= 2:
                    act.wait_ge(pool_c, POOL_C.at(i, "cw", j - 2))
                elif not isinstance(i, int) or i > 0:
                    act.wait_ge(pool_c, POOL_C.at(i - 1, "cw", NJ - 2 + j))
                A(ws[:, j % 2, :], ps[:, BANK_C[("w", j)], :], ACT.Copy).then_inc(act_c, ACT_C.tick("w", j))
                act.wait_ge(pe_c, PE_C.at(i, "c", j))
                if j >= 2:
                    act.wait_ge(vec_c, VEC_C.at(i, "prod", j - 2))
                elif not isinstance(i, int) or i > 0:
                    act.wait_ge(vec_c, VEC_C.at(i - 1, "prod", NJ - 2 + j))
                A(cs[:, j % 2, :], ps[:, BANK_C[("c", j)], :], ACT.Copy).then_inc(act_c, ACT_C.tick("c", j))

            def turn(a, b, c):
                if a is not None:
                    a_front(a)
                if b is not None:
                    b_spectra(b)
                if c is not None:
                    c_front(c)
                    c_exp(c)
                if a is not None:
                    a_angles(a, 0)
                    a_angles(a, 1)
                for u in range(UNITS):
                    if b is not None and u == 2:
                        b_exp(b)
                    if b is not None and u == 4:
                        b_wt(b)
                    if b is not None and u == 6:
                        b_back(b)
                    if c is not None:
                        c_tile(c, u)
                    if a is not None:
                        if u + 2 < UNITS:
                            a_angles(a, u + 2)
                        a_squares(a, u)
                        if u % M == M - 1:
                            a_norm(a, u // M)

            turn(0, None, None)
            turn(1, 0, None)
            turn(2, 1, 0)
            with act.Fori(3, NCHUNK) as i:
                turn(i, i - 1, i - 2)
            turn(None, NCHUNK - 1, NCHUNK - 2)
            turn(None, None, NCHUNK - 1)

        @block.gpsimd
        def _(pool):
            G = nc.gpsimd
            pool.wait_ge(ready, 1)

            def rstd(i, k, vec, VEC, own, OWN):
                pool.wait_ge(vec, VEC.at(i, "aggr", NQ - 1))
                G.tensor_tensor(rs[k][:, 0, :], mvr[k][:, :, 1], eps_[:, :], ALU.add)\
                    .then_inc(own, OWN.tick("var"))
                pool.wait_ge(own, OWN.at(i, "var"))
                G.tensor_tensor(rs[k][:, 1, :], rs[k][:, 0, :], half_[:, :], ALU.pow)\
                    .then_inc(own, OWN.tick("rstd"))

            def b_front(i):
                pool.wait_ge(vec_a, VEC_A.at(i, "norm", NQ - 1))
                pool.wait_ge(pe_b, PE_B.at(i, "xf", 1))
                G.tensor_tensor(x1[:, :, :], x1[:, :, :], bos[:, :].unsqueeze(1).broadcast_to([P, NQ, D]), ALU.add)\
                    .then_inc(pool_b, POOL_B.tick("res"))
                for n, name in enumerate(("q", "k", "v")):
                    pool.wait_ge(act_b, ACT_B.at(i, name + "a"))
                    row = qkv[0:1, 2 * n, :].rearrange("p (b d) -> p b d", b=SEQ)
                    G.tensor_tensor(row, row, bqkv[:, n, :].unsqueeze(1).broadcast_to([1, SEQ, D]), ALU.add)\
                        .then_inc(pool_b, POOL_B.tick("b" + name))

            def c_tile(i, j):
                pool.wait_ge(act_c, ACT_C.at(i, "c", j))
                G.tensor_tensor(cs[:, j % 2, :], cs[:, j % 2, :], ws[:, j % 2, :], ALU.mult)\
                    .then_inc(pool_c, POOL_C.tick("cw", j))

            def turn(a, b, c):
                if b is not None:
                    b_front(b)
                if c is not None:
                    for j in range(NJ):
                        c_tile(c, j)
                        if j == NJ - 1:
                            rstd(c, 2, vec_c, VEC_C, pool_c, POOL_C)
                if b is not None:
                    rstd(b, 1, vec_b, VEC_B, pool_b, POOL_B)
                if a is not None:
                    rstd(a, 0, vec_a, VEC_A, pool_a, POOL_A)

            turn(0, None, None)
            turn(1, 0, None)
            turn(2, 1, 0)
            with pool.Fori(3, NCHUNK) as i:
                turn(i, i - 1, i - 2)
            turn(None, NCHUNK - 1, NCHUNK - 2)
            turn(None, None, NCHUNK - 1)

        @block.vector
        def _(dve):
            V = nc.vector
            TS, TT, STT = V.tensor_scalar, V.tensor_tensor, V.scalar_tensor_tensor
            count = [0]

            def link(ins):
                ins.then_inc(chain, 1)
                count[0] += 1
                dve.wait_ge(chain, count[0])

            dve.wait_ge(w_attn, 16 * len(LOADS_A))
            slope, e, u1 = c32[:, 6:7], c32t[:, 9:10], c32t[:, 10:11]
            link(TS(c32t[:, 12:13], slope, -1.0, None, ALU.mult))
            V.memset(mask[:, :], 1.0)
            V.memset(half_[:, :], -0.5)
            V.memset(eps_[:, :], EPS)
            V.tensor_copy(c32t[:, 0:6], c32[:, 0:6])
            link(TT(c32t[:, 8:9], slope, c32t[:, 12:13], ALU.min))
            dve.wait_ge(act_s, 1)
            link(TS(u1, e, 1.0, None, ALU.add))
            link(TS(c32t[:, 12:13], u1, 1.0, None, ALU.subtract))
            link(TS(c32t[:, 13:14], u1, 1.0, None, ALU.is_equal))
            link(TT(c32t[:, 12:13], c32t[:, 12:13], c32t[:, 13:14], ALU.add))
            link(V.reciprocal(c32t[:, 12:13], c32t[:, 12:13]))
            dve.wait_ge(act_s, 2)
            link(TT(c32t[:, 14:15], c32t[:, 11:12], c32t[:, 13:14], ALU.add))
            link(TT(c32t[:, 14:15], c32t[:, 14:15], e, ALU.mult))
            link(TT(c32t[:, 14:15], c32t[:, 14:15], c32t[:, 12:13], ALU.mult))
            link(TS(c32t[:, 15:16], slope, 0.0, None, ALU.max))
            link(V.memset(c32t[:, 7:8], 0.0))
            link(TT(c32t[:, 6:7], c32t[:, 14:15], c32t[:, 15:16], ALU.add))
            link(TT(y8s[:, :, :, :], y8[:, :, :, :], n8.unsqueeze(3).broadcast_to([HD, 2, M, HD]), ALU.mult))
            link(TS(y8s[:, 0, :, :], y8s[:, 0, :, :], -1.0, None, ALU.mult))
            assert count[0] == SETUP_COL
            link(V.tensor_reduce(dl[:, 3:4], dl[:, 0:3], AX.X, ALU.max))
            link(TS(dl[:, 0:3], dl[:, 0:3], dl[:, 3:4], None, ALU.subtract))
            assert count[0] == SETUP_DERIV
            dve.wait_ge(act_s, 3)
            link(V.tensor_reduce(dl[:, 3:4], dl[:, 4:7], AX.X, ALU.add))
            link(V.reciprocal(dl[:, 3:4], dl[:, 3:4]))
            link(TS(dw[:, 0:3], dl[:, 4:7], dl[:, 3:4], None, ALU.mult))
            link(TS(dw[:, 2:3], dw[:, 2:3], -1.0, None, ALU.mult))
            link(TS(thn[:, :, :], thn[:, :, :], 1.0 / (2.0 * math.pi), None, ALU.mult))
            link(V.memset(mask[:, :].rearrange("p (s l) -> p s l", l=L)[:, :, 0:1], 0.0))
            sraw = g[:, 0, 0:DT * HEADS].rearrange("p (t n) -> p t n", t=DT)
            for t in range(DT):
                link(V.tensor_copy(win[:, t, 2 * D:].rearrange("p (k h) -> p k h", h=HD),
                                   sraw[:, t, :].unsqueeze(2).broadcast_to([P, HEADS, HD])))
            evs = [0]

            def evac(*name):
                k = SETUP.index(name)
                assert k == evs[0]
                evs[0] += 1
                dve.wait_ge(pe_s, k + 1)
                return ps[:, k % 8, :]

            for h in range(2):
                V.tensor_copy(col7[:, h, :], evac("col", h)[:, 0:8]).then_inc(vec_s, 1)
            V.tensor_copy(ybase, evac("y", 0)[:, 0:2 * M * HD]).then_inc(vec_s, 1)
            dve.wait_ge(vec_s, 3)
            V.tensor_copy(ss[:, :], col7[:, :, 5])
            for h in range(2):
                V.tensor_copy(cw[:, 4 + h, :], col7[:, h, 0:4])
            link(V.tensor_copy(cb[:, 4:6], col7[:, :, 4]))
            link(TS(lns[:, 0:2], col7[:, :, 6], -(L - 1.0), None, ALU.mult))
            link(TS(lns[:, 2:4], col7[:, :, 6], -1.0, None, ALU.mult))
            for h in range(2):
                link(TS(lt[:, h, :], pos, col7[:, h, 6:7], lns[:, h:h + 1], ALU.mult, ALU.add))
            a0 = (HEADS // 2 - ANCHORS) * HD
            link(TS(lt[a0:P, 1, :], pos[a0:P, :], lns[a0:P, 3:4], None, ALU.mult))
            for c in range(2):
                for m in range(M):
                    k = (c * M + m) * HD
                    link(TT(wy[:, c, m, :].rearrange("p (k n) -> p k n", n=HD),
                            ybase[:, k:k + HD].unsqueeze(1).broadcast_to([P, 16, HD]),
                            headm.unsqueeze(2).broadcast_to([P, 16, HD]), ALU.mult))
            dve.wait_ge(w_x, 16 * len(LOADS_X))
            dve.wait_ge(w_raw, 16 * len(LOADS_RAW))
            link(TS(bqkv[:, :, :], bqkv[:, :, :], float(L), None, ALU.mult))
            link(TT(rb2[:, 0, :], rb2[:, 0, :], rb2[:, 1, :], ALU.add))
            link(V.tensor_copy(rb2[:, 1, :], rb2[:, 0, :]))
            link(V.memset(acol[:, 1:2], 1.0))
            link(TS(dl[0:16, 0:1], cst[0:16, C_HM:C_HM + 1], 1.0, None, ALU.mult))
            link(TS(dl[0:16, 1:2], acol[0:16, 0:1], 1.0, None, ALU.subtract))
            link(TS(dl[0:16, 0:1], dl[0:16, 0:1], -1.0, 1.0, ALU.mult, ALU.add))
            link(TT(dl[0:16, 2:3], dl[0:16, 0:1], dl[0:16, 1:2], ALU.mult))
            link(TT(acol[0:16, 1:2], acol[0:16, 1:2], dl[0:16, 2:3], ALU.add))
            for name, dst in (("ot", fot), ("it", fit), ("rt", frt)):
                for t in range(DT):
                    V.tensor_copy(dst[:, t, :], evac(name, t)[:, 0:D]).then_inc(vec_s, 1)
            V.tensor_copy(w2t[:, :, :], evac("w2", 0)[:, 0:DT * KEXP].rearrange("p (t n) -> p t n", t=DT))\
                .then_inc(vec_s, 1)
            V.tensor_copy(bt, evac("bt", 0)[:, 0:DT * 16].rearrange("p (t n) -> p t n", t=DT)).then_inc(vec_s, 1)
            for name, dst in (("nq", nqt), ("nk", nkt)):
                for t in range(DT):
                    V.tensor_copy(dst[:, t, :], evac(name, t)[:, 0:D]).then_inc(vec_s, 1)
            for name, dst in (("mv", mv), ("mw", mw), ("mr", mr)):
                for br in range(2):
                    for t in range(DT):
                        V.tensor_copy(dst[:, t, br, :], evac(name, br, t)[:, 0:(D if name == "mr" else T)])\
                            .then_inc(vec_s, 1)
            for j in range(NJ):
                TS(up[:, j, :], evac("up", j)[:, 0:D], acol[:, 0:1] if j >= NJ // 2 else 1.0, None, ALU.mult)\
                    .then_inc(vec_s, 1)
            TS(bp[:, :], evac("bp", 0)[0:16, 0:D], acol[0:16, 1:2], None, ALU.mult).then_inc(vec_s, 1)
            dve.wait_ge(vec_s, len(SETUP))
            V.memset(dw[:, 3:4], 0.0).then_inc(ready, 1)

            def a_tap(i, j, tap):
                s = TAPS - 1 - tap
                o = zc[:, j, :].rearrange("p (b l) -> p b l", b=SEQ)
                z = ps[:, BANK_A[("z", j)], :].rearrange("p (b l) -> p b l", b=SEQ)
                if tap == 2:
                    dve.wait_ge(act_a, ACT_A.at(i, "z", j))
                else:
                    dve.wait_ge(vec_a, VEC_A.at(i, "tap", j, tap + 1))
                STT(o[:, :, s:L], z[:, :, 0:L - s], cw[:, j, tap:tap + 1], o[:, :, s:L], ALU.mult, ALU.add)\
                    .then_inc(vec_a, VEC_A.tick("tap", j, tap))

            def a_exponent(i, h):
                z = zc[:, 4 + h, :]
                dve.wait_ge(vec_a, VEC_A.at(i, "tap", 4 + h, 0))
                TS(z, z, ss[:, h:h + 1], 20.0, ALU.mult, ALU.min).then_inc(vec_a, VEC_A.tick("clip", h))
                dve.wait_ge(vec_a, VEC_A.at(i, "clip", h))
                z3 = z.rearrange("p (b l) -> p b l", b=SEQ)
                STT(z3, z3, -20.0, lt[:, h, :].unsqueeze(1).broadcast_to([P, SEQ, L]), ALU.max, ALU.add)\
                    .then_inc(vec_a, VEC_A.tick("expo", h))

            def a_fraction(i, u):
                h, m = divmod(u, M)
                if m == 0:
                    dve.wait_ge(vec_a, VEC_A.at(i, "tap", h, 0))
                if u >= 2:
                    dve.wait_ge(act_a, ACT_A.at(i, "sin", u - 2))
                    dve.wait_ge(vec_a, VEC_A.at(i, "re", u - 2))
                elif not isinstance(i, int) or i > 0:
                    dve.wait_ge(act_a, ACT_A.at(i - 1, "sin", UNITS - 2 + u))
                TS(kturn[:, u % 2, :], zc[:, h, :], thn[:, h, m:m + 1], None, ALU.mult)\
                    .then_inc(vec_a, VEC_A.tick("turns", u))
                dve.wait_ge(vec_a, VEC_A.at(i, "turns", u))
                STT(frac[:, u % 2, :], zc[:, h, :], thn[:, h, m:m + 1], kturn[:, u % 2, :], ALU.mult, ALU.subtract)\
                    .then_inc(vec_a, VEC_A.tick("frac", u))

            def a_poly(i, h):
                z = zc[:, h, :]
                dve.wait_ge(vec_a, VEC_A.at(i, "tap", h, 0))
                if not isinstance(i, int) or i > 0:
                    dve.wait_ge(vec_a, VEC_A.at(i - 1, "re", M * h + M - 1))
                TS(g[:, h, :], z, dw[:, 2:3], dw[:, 1:2], ALU.mult, ALU.add).then_inc(vec_a, VEC_A.tick("p1", h))
                dve.wait_ge(vec_a, VEC_A.at(i, "p1", h))
                TT(g[:, h, :], g[:, h, :], z, ALU.mult).then_inc(vec_a, VEC_A.tick("p2", h))
                dve.wait_ge(vec_a, VEC_A.at(i, "p2", h))
                dve.wait_ge(act_a, ACT_A.at(i, "exp", h))
                STT(g[:, h, :], g[:, h, :], dw[:, 0:1], zc[:, 4 + h, :], ALU.add, ALU.mult)\
                    .then_inc(vec_a, VEC_A.tick("g", h))

            def a_den(i, h):
                dve.wait_ge(vec_a, VEC_A.at(i, "g", h))
                V.tensor_tensor_scan(den[:, h, :], mask[:, 0:T], den[:, h, :], 0.0, ALU.mult, ALU.add)\
                    .then_inc(vec_a, VEC_A.tick("den", h))
                dve.wait_ge(vec_a, VEC_A.at(i, "den", h))
                TS(den[:, h, :], den[:, h, :], 1e-4, None, ALU.max).then_inc(vec_a, VEC_A.tick("guard", h))

            def a_moments(i, u):
                h, s = u // M, u % 4
                dve.wait_ge(act_a, ACT_A.at(i, "sin", u))
                if u % M == 0:
                    dve.wait_ge(vec_a, VEC_A.at(i, "g", h))
                TT(sc[:, s, 0, :], sc[:, s, 0, :], g[:, h, :], ALU.mult).then_inc(vec_a, VEC_A.tick("im", u))
                STT(sc[:, s, 1, :], hq[:, u % 2, :], 1.0, g[:, h, :], ALU.subtract, ALU.mult)\
                    .then_inc(vec_a, VEC_A.tick("re", u))

            def a_scan(i, u):
                flat = sc[:, u % 4, :, :].rearrange("p c t -> p (c t)")
                dve.wait_ge(vec_a, VEC_A.at(i, "re", u))
                V.tensor_tensor_scan(flat, mask[:, 0:2 * T], flat, 0.0, ALU.mult, ALU.add)\
                    .then_inc(vec_a, VEC_A.tick("scan", u))

            def a_heads(i, h):
                last = M * h + M - 1
                dve.wait_ge(pe_a, PE_A.at(i, "sum", last))
                dve.wait_ge(act_a, ACT_A.at(i, "e", h))
                TT(den[:, h, :], ps[:, BANK_A[("S", h)], :], den[:, h, :], ALU.add).then_inc(vec_a, VEC_A.tick("w", h))
                dve.wait_ge(act_a, ACT_A.at(i, "f", h))
                TT(zc[:, 2 + h, :], zc[:, 2 + h, :], den[:, h, :], ALU.mult).then_inc(vec_a, VEC_A.tick("gf", h))
                dve.wait_ge(vec_a, VEC_A.at(i, "gf", h))
                TT(zc[:, 2 + h, :], zc[:, 2 + h, :], ps[:, BANK_A[("Y", h)], :], ALU.mult)\
                    .then_inc(vec_a, VEC_A.tick("y", h))

            def layer_norm(i, k, xs, dst, vec, VEC, pool, POOL):
                for q in range(NQ):
                    dve.wait_ge(vec, VEC.at(i, "res", q // 2))
                    V.bn_stats(st[k][:, q, :], xs[:, q, :]).then_inc(vec, VEC.tick("stats", q))
                dve.wait_ge(vec, VEC.at(i, "stats", NQ - 1))
                V.tensor_copy(seen[:, k:k + 1], st[k][:, 0, 0:1])
                for q in range(NQ):
                    V.bn_aggr(mvr[k][:, q, :], st[k][:, q, :]).then_inc(vec, VEC.tick("aggr", q))
                dve.wait_ge(pool, POOL.at(i, "rstd"))
                for q in range(NQ):
                    TS(dst[:, q, :], xs[:, q, :], mvr[k][:, q, 0:1], rs[k][:, 1, q:q + 1], ALU.subtract, ALU.mult)\
                        .then_inc(vec, VEC.tick("norm", q))

            def a_finish(i):
                for n in range(2):
                    dve.wait_ge(pe_a, PE_A.at(i, "out", n))
                    if n == 0:
                        dve.wait_ge(xr_in, 16 * i + 16)
                    o = xs_a[:, 2 * n:2 * n + 2, :]
                    TT(o, o, ps[:, BANK_A[("out", n)], :].rearrange("p (q d) -> p q d", q=2), ALU.add)\
                        .then_inc(vec_a, VEC_A.tick("res", n))
                layer_norm(i, 0, xs_a, x1, vec_a, VEC_A, pool_a, POOL_A)

            def b_products(i):
                dve.wait_ge(act_b, ACT_B.at(i, "kb"))
                dve.wait_ge(pool_b, POOL_B.at(i, "bk"))
                dve.wait_ge(pe_b, PE_B.at(i, "vb"))
                TT(spec[:, 0:2, :], qkv[:, 0:2, :], qkv[:, 2:4, :], ALU.mult).then_inc(vec_b, VEC_B.tick("aabb"))
                TT(spec[:, 2, :], qkv[:, 0, :], qkv[:, 3, :], ALU.mult).then_inc(vec_b, VEC_B.tick("ab"))
                TT(spec[:, 3, :], qkv[:, 1, :], qkv[:, 2, :], ALU.mult).then_inc(vec_b, VEC_B.tick("ba"))
                dve.wait_ge(vec_b, VEC_B.at(i, "ba"))
                V.tensor_reduce(rsum[:, :, :], spec[:, :, :].rearrange("p a (h d) -> p a h d", d=XD), AX.X, ALU.add)\
                    .then_inc(vec_b, VEC_B.tick("heads"))
                aa, bb_, ab, ba = (rsum[:, n, :] for n in range(4))
                dve.wait_ge(vec_b, VEC_B.at(i, "heads"))
                if not isinstance(i, int) or i > 0:
                    pass
                STT(cspec[:, 0, :], bb_, m0, aa, ALU.mult, ALU.add).then_inc(vec_b, VEC_B.tick("ca"))
                TT(cspec[:, 2, :], ba, ab, ALU.subtract).then_inc(vec_b, VEC_B.tick("cb0"))
                TS(cspec[:, 3, :], bb_, m1, None, ALU.mult).then_inc(vec_b, VEC_B.tick("cb1"))
                dve.wait_ge(vec_b, VEC_B.at(i, "cb1"))
                STT(cspec[:, 1, :], cspec[:, 2, :], m0, cspec[:, 3, :], ALU.mult, ALU.add)\
                    .then_inc(vec_b, VEC_B.tick("cb2"))

            def b_topk(i):
                c, top = cor[:, 0, :], sm[:, 0:8]
                above, equal, order = cor[:, 1, :], cor[:, 2, :], cor[:, 3, :]
                dve.wait_ge(pe_b, PE_B.at(i, "corr"))
                TS(c, ps[0:BH, BANK_B[("corr",)], 0:L], 1.0 / XD, None, ALU.mult).then_inc(vec_b, VEC_B.tick("corr"))
                dve.wait_ge(vec_b, VEC_B.at(i, "corr"))
                V.tensor_copy(sm[:, 12:13], cor[:, 0, 0:1])
                V.max(top, c).then_inc(vec_b, VEC_B.tick("top"))
                dve.wait_ge(vec_b, VEC_B.at(i, "top"))
                TS(sm[:, 8:9], sm[:, 0:1], -1.0, None, ALU.mult).then_inc(vec_b, VEC_B.tick("negmax"))
                kth = sm[:, TOPK - 1:TOPK]
                TS(above, c, kth, None, ALU.is_gt, ALU.add, accum_out=sm[:, 9:10]).then_inc(vec_b, VEC_B.tick("above"))
                TS(equal, c, kth, None, ALU.is_equal).then_inc(vec_b, VEC_B.tick("equal"))
                dve.wait_ge(vec_b, VEC_B.at(i, "equal"))
                V.tensor_tensor_scan(order, mask[0:BH, 1:2].broadcast_to([BH, L]), equal, 0.0, ALU.mult, ALU.add)\
                    .then_inc(vec_b, VEC_B.tick("order"))
                dve.wait_ge(vec_b, VEC_B.at(i, "order"))
                TS(order, order, sm[:, 9:10], float(TOPK), ALU.add, ALU.is_le).then_inc(vec_b, VEC_B.tick("first"))
                dve.wait_ge(vec_b, VEC_B.at(i, "first"))
                TT(order, order, equal, ALU.mult).then_inc(vec_b, VEC_B.tick("also"))
                dve.wait_ge(vec_b, VEC_B.at(i, "also"))
                TT(above, above, order, ALU.add).then_inc(vec_b, VEC_B.tick("keep"))
                dve.wait_ge(vec_b, VEC_B.at(i, "keep"))
                dve.wait_ge(act_b, ACT_B.at(i, "exp"))
                STT(cor[:, 2, :], cor[:, 4, :], 1.0, above, ALU.mult, ALU.mult, accum_out=sm[:, 10:11])\
                    .then_inc(vec_b, VEC_B.tick("weight"))
                dve.wait_ge(vec_b, VEC_B.at(i, "weight"))
                V.reciprocal(sm[:, 11:12], sm[:, 10:11]).then_inc(vec_b, VEC_B.tick("inv"))
                dve.wait_ge(vec_b, VEC_B.at(i, "inv"))
                TS(cor[:, 0, :], cor[:, 2, :], sm[:, 11:12], None, ALU.mult).then_inc(vec_b, VEC_B.tick("wn"))

            def b_apply(i):
                dve.wait_ge(pe_b, PE_B.at(i, "wf"))
                wa, wb = (ps[:, BANK_B[("wf",)], n * BH:(n + 1) * BH] for n in range(2))
                V.tensor_copy(wspec[:, 0, :], wa).then_inc(vec_b, VEC_B.tick("w1"))
                TS(wspec[:, 1, :], wb, m0, None, ALU.mult).then_inc(vec_b, VEC_B.tick("w2"))
                TS(wspec[:, 2, :], wb, m0, -1.0, ALU.mult, ALU.mult).then_inc(vec_b, VEC_B.tick("w4"))
                TS(cspec[:, 2, :], wb, m1, None, ALU.mult).then_inc(vec_b, VEC_B.tick("w3a"))
                dve.wait_ge(vec_b, VEC_B.at(i, "w3a"))
                STT(wspec[:, 3, :], wa, m0, cspec[:, 2, :], ALU.mult, ALU.add).then_inc(vec_b, VEC_B.tick("w3"))
                dve.wait_ge(vec_b, VEC_B.at(i, "w3"))
                dve.wait_ge(act_b, ACT_B.at(i, "vb"))
                dve.wait_ge(pool_b, POOL_B.at(i, "bv"))
                v = qkv[:, 4:6, :].rearrange("p a (h d) -> p a h d", d=XD)
                for n, name in ((0, "oa"), (2, "ob")):
                    TT(spec[:, n:n + 2, :].rearrange("p a (h d) -> p a h d", d=XD), v,
                       wspec[:, n:n + 2, :].unsqueeze(3).broadcast_to([P, 2, BH, XD]), ALU.mult)\
                        .then_inc(vec_b, VEC_B.tick(name))
                dve.wait_ge(vec_b, VEC_B.at(i, "ob"))
                s4 = spec[:, :, :].rearrange("p (a b) t -> p a b t", b=2)
                TT(qkv[:, 0:2, :], s4[:, :, 0, :], s4[:, :, 1, :], ALU.add).then_inc(vec_b, VEC_B.tick("o"))

            def b_finish(i):
                for n in range(2):
                    dve.wait_ge(pe_b, PE_B.at(i, "out", n))
                    if n == 0:
                        dve.wait_ge(pool_b, POOL_B.at(i, "res"))
                    o = x1[:, 2 * n:2 * n + 2, :]
                    TT(o, o, ps[:, BANK_B[("out", n)], :].rearrange("p (q d) -> p q d", q=2), ALU.add)\
                        .then_inc(vec_b, VEC_B.tick("res", n))
                layer_norm(i, 1, x1, x2, vec_b, VEC_B, pool_b, POOL_B)

            def c_cum(i):
                dve.wait_ge(act_c, ACT_C.at(i, "xT", 1))
                if not isinstance(i, int) or i > 0:
                    dve.wait_ge(pe_c, PE_C.at(i - 1, "c", NJ - 1))
                V.tensor_tensor_scan(cum[:, :, :].rearrange("p a t -> p (a t)"), mask[:, 0:DT * T],
                                     x2t[:, :, :].rearrange("p a t -> p (a t)"), 0.0, ALU.mult, ALU.add)\
                    .then_inc(vec_c, VEC_C.tick("cum"))

            def c_softmax(i):
                n = NQ * 2
                dve.wait_ge(pe_c, PE_C.at(i, "logit"))
                TT(lg[:, :, :].rearrange("p (q b) k -> p q (b k)", b=2),
                   ps[:, BANK_C[("logit",)], 0:n * KEXP].rearrange("p (q b) -> p q b", q=NQ),
                   rb2[:, :, :].rearrange("p b k -> p (b k)").unsqueeze(1).broadcast_to([P, NQ, 2 * KEXP]), ALU.add)\
                    .then_inc(vec_c, VEC_C.tick("logit"))
                dve.wait_ge(vec_c, VEC_C.at(i, "logit"))
                V.tensor_reduce(ls[:, 0, :], lg[:, :, :], AX.X, ALU.max).then_inc(vec_c, VEC_C.tick("max"))
                dve.wait_ge(vec_c, VEC_C.at(i, "max"))
                TT(lg[:, :, :], lg[:, :, :], ls[:, 0, :].unsqueeze(2).broadcast_to([P, n, KEXP]), ALU.subtract)\
                    .then_inc(vec_c, VEC_C.tick("sub"))
                dve.wait_ge(act_c, ACT_C.at(i, "exp"))
                V.tensor_reduce(ls[:, 1, :], lg[:, :, :], AX.X, ALU.add).then_inc(vec_c, VEC_C.tick("sum"))
                dve.wait_ge(vec_c, VEC_C.at(i, "sum"))
                V.reciprocal(ls[:, 1, :], ls[:, 1, :]).then_inc(vec_c, VEC_C.tick("inv"))
                dve.wait_ge(vec_c, VEC_C.at(i, "inv"))
                TT(lg[:, :, :], lg[:, :, :], ls[:, 1, :].unsqueeze(2).broadcast_to([P, n, KEXP]), ALU.mult)\
                    .then_inc(vec_c, VEC_C.tick("weight"))

            def c_prod(i, j):
                dve.wait_ge(pe_c, PE_C.at(i, "x", j))
                dve.wait_ge(pool_c, POOL_C.at(i, "cw", j))
                TT(prod[:, j, :], cs[:, j % 2, :], ps[:, BANK_C[("x", j)], :], ALU.mult)\
                    .then_inc(vec_c, VEC_C.tick("prod", j))

            def c_finish(i):
                for n in range(2):
                    dve.wait_ge(pe_c, PE_C.at(i, "out", n))
                    for q in range(2):
                        o = x2[:, 2 * n + q, :]
                        ins = STT(o, ps[:, BANK_C[("out", n)], q * D:(q + 1) * D], rn[:, q:q + 1], o, ALU.mult, ALU.add)
                    ins.then_inc(vec_c, VEC_C.tick("res", n))
                if not isinstance(i, int) or i > 0:
                    dve.wait_ge(stored, 16 * i)
                layer_norm(i, 2, x2, xs_c, vec_c, VEC_C, pool_c, POOL_C)

            def turn(a, b, c):
                if a is not None:
                    for h in range(2):
                        for tap in (2, 1, 0):
                            a_tap(a, 4 + h, tap)
                        a_exponent(a, h)
                        for tap in (2, 1, 0):
                            a_tap(a, h, tap)
                        if h == 0:
                            a_fraction(a, 0)
                            a_fraction(a, 1)
                        a_poly(a, h)
                        a_den(a, h)
                    for j in (2, 3):
                        for tap in (2, 1, 0):
                            a_tap(a, j, tap)
                if b is not None:
                    b_products(b)
                if c is not None:
                    c_cum(c)
                    c_softmax(c)
                for u in range(UNITS):
                    if b is not None and u == 2:
                        b_topk(b)
                    if b is not None and u == 4:
                        b_apply(b)
                    if c is not None:
                        c_prod(c, u)
                    if a is not None:
                        a_moments(a, u)
                        if u + 2 < UNITS:
                            a_fraction(a, u + 2)
                        a_scan(a, u)
                        if u % M == M - 1:
                            a_heads(a, u // M)
                if c is not None:
                    c_finish(c)
                if b is not None:
                    b_finish(b)
                if a is not None:
                    a_finish(a)

            turn(0, None, None)
            turn(1, 0, None)
            turn(2, 1, 0)
            with dve.Fori(3, NCHUNK) as i:
                turn(i, i - 1, i - 2)
            turn(None, NCHUNK - 1, NCHUNK - 2)
            turn(None, None, NCHUNK - 1)


SETUP_COL = 15
SETUP_DERIV = 17


def shape_constants():
    c = np.zeros((P, C_END), np.float32)
    p = np.arange(P)
    c[:, C_ID:C_ID + P] = np.eye(P)
    c[:, C_BLK:C_BLK + P] = p[:, None] // HD == p[None, :] // HD
    c[:, C_HM:C_HM + 16] = p[:, None] // HD == np.arange(16)[None, :]
    c[:, C_POS:C_POS + L] = np.arange(L)
    c[:, C_RN] = 1.0 / (p + 1.0)
    c[:, C_RN + 1] = 1.0 / (p + P + 1.0)
    c[:, C_M0] = p > 0
    c[:, C_M0 + 1] = p == 0
    c[0:HD, C_E8:C_E8 + P] = np.arange(HD)[:, None] == p[None, :] % HD
    t, f = np.arange(L)[:, None], np.arange(P)[None, :]
    ang = 2.0 * np.pi * ((t * f) % L) / L
    fwd = np.concatenate([np.cos(ang), np.sin(ang)], 1)
    fwd[:, P] = (-1.0) ** np.arange(L)
    scale = np.where(np.arange(P) == 0, 1.0, 2.0)[:, None] / L
    inv = np.stack([fwd[:, 0:P].T * scale, fwd[:, P:].T * scale])
    e = np.zeros((HEADS, 2, P), np.float32)
    s = np.zeros((2 * KEXP, NJ, P), np.float32)
    for h in range(2):
        e[:, h, :] = np.arange(HEADS)[:, None] == h * 16 + p[None, :] // HD
    for j in range(NJ):
        s[:, j, :] = np.arange(2 * KEXP)[:, None] == 2 * j + p[None, :] // R
    return {"consts": c, "dft": fwd.astype(np.float32), "idft": inv.astype(np.float32), "expand": e, "select": s}


_INS = ['x', 'ctx_1024', 'L0_attn_in_proj_w', 'L0_attn_conv_w', 'L0_attn_conv_b', 'L0_attn_theta',
        'L0_attn_decay_slopes', 'L0_attn_anchor_slopes', 'L0_attn_score_scale', 'L0_attn_deriv_logits',
        'L0_attn_norm_scale', 'L0_attn_W_re', 'L0_attn_W_im', 'L0_attn_out_proj_w', 'L0_xattn_Wq',
        'L0_xattn_bq', 'L0_xattn_Wk', 'L0_xattn_bk', 'L0_xattn_Wv', 'L0_xattn_bv', 'L0_xattn_Wo',
        'L0_xattn_bo', 'L0_ffn_W_Q', 'L0_ffn_W_K', 'L0_ffn_W_O', 'L0_ffn_W_inv', 'L0_ffn_V_fwd',
        'L0_ffn_W_fwd', 'L0_ffn_U_fwd', 'L0_ffn_b_fwd', 'L0_ffn_V_inv', 'L0_ffn_W_inv_exp',
        'L0_ffn_U_inv', 'L0_ffn_b_inv', 'L0_ffn_router_w1', 'L0_ffn_router_b1', 'L0_ffn_router_w2',
        'L0_ffn_router_b2', 'L0_ffn_alpha_bi', 'L0_ffn_expert_bias']


def kernel(**inputs):
    import concourse.bacc as _bacc
    from concourse.bass_utils import run_bass_kernel_spmd as _run

    nc = _bacc.Bacc("TRN2", target_bir_lowering=False, num_devices=1)
    arrays, args = {}, []
    given = {name: np.ascontiguousarray(inputs[name]) for name in _INS}
    given['L0_ffn_alpha_bi'] = given['L0_ffn_alpha_bi'].reshape(1)
    given.update(shape_constants())
    for name, a in given.items():
        arrays[f"in_{name}_dram"] = a
        args.append(nc.dram_tensor(f"in_{name}_dram", a.shape, mybir.dt.from_np(a.dtype), kind="ExternalInput").ap())
    args.append(nc.dram_tensor("out_0_dram", (B, L, D), F32, kind="ExternalOutput").ap())
    decoder_kernel(nc, *args)
    r = _run(nc, [arrays], core_ids=[0])
    return r.results[0]["out_0_dram"]
```

```python
import concourse.bass as bass
from concourse import mybir
from contextlib import ExitStack
import math
import numpy as np

F32 = mybir.dt.float32
F32R = mybir.dt.float32r
I32 = mybir.dt.int32
ALU = mybir.AluOpType
ACT = mybir.ActivationFunctionType
AX = mybir.AxisListType

P = 128
B, L, D = 16, 256, 256
SEQ = 2
T = SEQ * L
NCHUNK = B // SEQ
NQ = T // P
DT = D // P
HEADS, HD, M, ANCHORS, TAPS = 32, 8, 4, 4, 4
NZ = 6
XH, XD = 16, 16
TOPK = int(math.log(L + 1))
KEXP, R = 8, 64
NJ = 2 * KEXP * R // P
UNITS = 2 * M
EPS = 1e-5

C_ID, C_BLK, C_HM, C_POS, C_RN, C_M0, C_E8, C_END = 0, 128, 256, 272, 528, 530, 532, 660


class Steps:

    def __init__(self, prefix, names):
        self.prefix, self.order = prefix, {}
        for n in names:
            kind, *which = n if isinstance(n, tuple) else (n,)
            self.order.setdefault(kind, []).append(tuple(which))

    def semaphores(self, sem):
        self.sem = {kind: sem(f"{self.prefix}_{kind}") for kind in self.order}
        self.next = dict.fromkeys(self.order, 0)

    def tick(self, kind, *which):
        order = self.order[kind]
        assert order[self.next[kind] % len(order)] == which, (self.prefix, kind, which)
        self.next[kind] += 1
        return self.sem[kind], 1

    def at(self, i, kind, *which):
        order = self.order[kind]
        return self.sem[kind], i * len(order) + order.index(which) + 1


def each(kinds, over):
    return [(kind, n) for n in over for kind in kinds.split()]


LAYER_NORM = each("res", range(2)) + each("stats aggr norm", range(NQ))

Z_ORDER = [4, 0, 5, 1, 2, 3]
PE_A = Steps("pe_a", each("xT", range(2)) + each("z", Z_ORDER) + each("y", range(UNITS)) + each("S out", range(2)))
VEC_A = Steps("vec_a", [("tap", j, t) for j in Z_ORDER for t in (2, 1, 0)]
              + each("clip expo p1 p2 g den guard w gf y", range(2)) + each("turns frac im re scan", range(UNITS))
              + each("acc", [u for u in range(UNITS) if u % M]) + LAYER_NORM)
ACT_A = Steps("act_a", each("xT exp silu e ln f", range(2)) + each("z", Z_ORDER)
              + each("half cos sin sq", range(UNITS)))
POOL_A = Steps("pool_a", ["var", "rstd"])

SPEC = ["qa", "qb", "ka", "kb", "va", "vb"]
PE_B = Steps("pe_b", each("xf cf ot out", range(2)) + SPEC + ["corr", "wt", "wf"])
ACT_B = Steps("act_b", each("xf cf ot", range(2)) + SPEC + ["exp", "wt"])
POOL_B = Steps("pool_b", ["res", "bq", "bk", "bv", "var", "rstd"])
VEC_B = Steps("vec_b", ["aabb", "ab", "ba", "heads", "ca", "cb0", "cb1", "cb2", "corr", "top", "negmax",
                        "above", "equal", "order", "first", "also", "keep", "weight", "inv", "wn",
                        "w1", "w2", "w4", "w3a", "w3", "oa", "ob", "o"] + LAYER_NORM)

PE_C = Steps("pe_c", each("xT out", range(2)) + each("h", range(4)) + ["logit", "wT"] + each("w c x", range(NJ)))
ACT_C = Steps("act_c", each("xT", range(2)) + each("h", range(4)) + ["exp", "whigh", "wT"] + each("c", range(NJ)))
POOL_C = Steps("pool_c", ["var", "rstd"])
VEC_C = Steps("vec_c", ["cum", "logit", "max", "sub", "sum", "inv", "weight", "wlow"]
              + each("cw prod", range(NJ)) + LAYER_NORM)

BANK_A = {("xT", 0): 0, ("xT", 1): 1, ("z", 4): 2, ("z", 0): 0, ("z", 5): 1, ("z", 1): 2, ("z", 2): 0,
          ("z", 3): 1, ("Y", 0): 0, ("Y", 1): 1, ("S", 0): 2, ("S", 1): 2, ("out", 0): 0, ("out", 1): 1}
BANK_B = {("xf", 0): 3, ("xf", 1): 4, ("cf", 0): 3, ("cf", 1): 4, ("qa",): 3, ("qb",): 4, ("ka",): 3,
          ("kb",): 4, ("va",): 3, ("vb",): 4, ("corr",): 3, ("wt",): 4, ("wf",): 3, ("ot", 0): 4,
          ("ot", 1): 3, ("out", 0): 4, ("out", 1): 3}
BANK_C = {("xT", 0): 5, ("xT", 1): 6, ("h", 0): 7, ("h", 1): 5, ("h", 2): 6, ("h", 3): 7, ("logit",): 7,
          ("wT",): 7}
for _j in range(NJ):
    BANK_C.update({("c", _j): 5, ("x", _j): 6, ("w", _j): 7})
BANK_C.update({("out", 0): 5, ("out", 1): 7})


def before(banks, group):
    order = list(banks)
    k = order.index(group)
    mine = [g for g in order if banks[g] == banks[group]]
    n = mine.index(group)
    return (mine[n - 1], False) if n else (mine[-1], True)


def decoder_kernel(nc, x, ctx_in, in_proj, conv_w, conv_b, theta, decay, anchor, score, deriv, norm_sc,
                   w_re, w_im, out_proj, wq, bq, wk, bk, wv, bv, wo, bo, f_q, f_k, f_o, f_inv, v_fwd,
                   w_fwd, u_fwd, b_fwd, v_inv, w_inv, u_inv, b_inv, r_w1, r_b1, r_w2, r_b2, alpha, ebias,
                   consts, dft, idft, expand, select, out):
    ctx = ExitStack()
    with ctx:
        def sb(name, shape, dt=F32):
            return ctx.enter_context(nc.sbuf_tensor(name, shape, dt))

        def sem(name):
            return ctx.enter_context(nc.semaphore(name))

        ctx.enter_context(nc.allow_non_contiguous_dma("small weights, once"))
        cst = sb("cst", [P, C_END])
        ident = cst[:, C_ID:C_ID + P]
        blk = cst[:, C_BLK:C_BLK + P]
        headm = cst[:, C_HM:C_HM + 16]
        pos = cst[:, C_POS:C_POS + L]
        rn = cst[:, C_RN:C_RN + 2]
        m0, m1 = cst[:, C_M0:C_M0 + 1], cst[:, C_M0 + 1:C_M0 + 2]
        e8 = cst[0:HD, C_E8:C_E8 + P]
        sel = sb("sel", [32 + 2 * KEXP, NJ, P], F32R)
        win = sb("win", [P, DT, NZ * P])
        wopj = sb("wopj", [P, DT, D])
        mask = sb("mask", [P, 2 * T], mybir.dt.bfloat16)
        cw = sb("cw", [P, NZ, TAPS])
        cb = sb("cb", [P, NZ])
        thn = sb("thn", [P, 2, M])
        ss = sb("ss", [P, 2])
        lt = sb("lt", [P, 2, L])
        dw = sb("dw", [P, 4])
        wy = sb("wy", [P, 2, M, P])
        wqs, wks, wvs, wos = (sb(n, [P, DT, D]) for n in ("wqs", "wks", "wvs", "wos"))
        bos = sb("bos", [P, D])
        bqkv = sb("bqkv", [1, 3, D])
        fdft = sb("fdft", [P, 2, L])
        fidft = sb("fidft", [P, 2, L])
        mv = sb("mv", [P, DT, 2, KEXP * R])
        mw = sb("mw", [P, DT, 2, KEXP * R])
        mr = sb("mr", [P, DT, 2, D])
        up = sb("up", [P, NJ, D])
        bp = sb("bp", [2 * KEXP, D])
        w2t = sb("w2t", [P, DT, KEXP])
        rb1 = sb("rb1", [P, DT])
        rb2 = sb("rb2", [P, 2, KEXP])
        acol = sb("acol", [P, 2])
        half_ = sb("half_", [P, NQ])
        eps_ = sb("eps_", [P, NQ])
        seen = sb("seen", [P, 3])
        xa = sb("xa", [P, NQ, D])
        xt = sb("xt", [P, DT, T])
        zc = sb("zc", [P, NZ, T])
        g = sb("g", [P, 2, T])
        frac = sb("frac", [P, 2, T])
        hq = sb("hq", [P, 2, T])
        kturn = hq[:, :, :].bitcast(I32)
        den = zc[:, 4:6, :]
        sc = sb("sc", [P, 4, 2, T])
        sq = sb("sq", [P, 2, 2, T])
        acc = sb("acc", [P, 2, 2, T])
        xs_a = sb("xs_a", [P, NQ, D])
        x1 = sb("x1", [P, NQ, D])
        cin = sb("cin", [P, NQ, D])
        spec = sb("spec", [P, 4, T])
        qkv = sb("qkv", [P, 6, T])
        x2 = sb("x2", [P, NQ, D])
        BH = SEQ * XH
        rsum = sb("rsum", [P, 4, BH])
        cspec = sb("cspec", [P, 4, BH])
        cor = sb("cor", [BH, 5, L])
        sm = sb("sm", [BH, 16])
        wtt = sb("wtt", [P, 2, BH])
        wspec = sb("wspec", [P, 4, BH])
        x2t = sb("x2t", [P, DT, T])
        cum = sb("cum", [P, DT, T])
        prod = sb("prod", [P, NJ, T])
        hT = prod[:, 0:4, :]
        xs_c = prod[:, 4:6, :].rearrange("p t (h d) -> p (t h) d", d=D)
        lg = sb("lg", [P, NQ * 2, KEXP])
        ls = sb("ls", [P, 2, NQ * 2])
        wT = sb("wT", [2 * KEXP, T])
        wpair = sb("wpair", [32 + 2 * KEXP, T], F32R)
        cs = sb("cs", [P, 2, T])
        st = [sb(f"st{n}", [P, NQ, 6]) for n in "abc"]
        mvr = [sb(f"mvr{n}", [P, NQ, 2]) for n in "abc"]
        rs = [sb(f"rs{n}", [P, 2, NQ]) for n in "abc"]
        fq = spec[:, 0, :].rearrange("p (t n) -> p t n", t=DT)
        fk = spec[:, 1, :].rearrange("p (t n) -> p t n", t=DT)
        fo = spec[:, 2, :].rearrange("p (t n) -> p t n", t=DT)
        fi = spec[:, 3, :].rearrange("p (t n) -> p t n", t=DT)
        raw_v = [prod[:, 2 * n:2 * n + 2, :] for n in range(4)]
        raw_u = [qkv[:, 2 * n:2 * n + 2, :] for n in range(2)]
        fr = qkv[:, 4, :].rearrange("p (t n) -> p t n", t=DT)
        fot = qkv[:, 5, :].rearrange("p (t n) -> p t n", t=DT)
        fit = x2t[:, 0, :].rearrange("p (t n) -> p t n", t=DT)
        frt = x2t[:, 1, :].rearrange("p (t n) -> p t n", t=DT)
        nqt = cum[:, 0, :].rearrange("p (t n) -> p t n", t=DT)
        nkt = cum[:, 1, :].rearrange("p (t n) -> p t n", t=DT)
        rw2 = x2[0:KEXP, 0, :]
        selraw = sc[0:32 + 2 * KEXP, 0:2, :, :].rearrange("p a b t -> p (a b t)")[:, 0:NJ * P]\
            .rearrange("p (j n) -> p j n", j=NJ)
        b16 = x2[0:2 * KEXP, 1, :]
        bt = x2[:, 2, 0:DT * 2 * KEXP].rearrange("p (t n) -> p t n", t=DT)
        e32 = x2[0:HEADS, 3, :].rearrange("p (h n) -> p h n", h=2)
        c32 = x1[0:HEADS, 0, 0:8]
        c32t = x1[0:HEADS, 1, 0:16]
        y8 = x1[0:HD, 2, 0:2 * M * HD].rearrange("p (c m n) -> p c m n", c=2, m=M)
        y8s = x1[0:HD, 3, 0:2 * M * HD].rearrange("p (c m n) -> p c m n", c=2, m=M)
        n8 = x1[0:HD, 3, 64:64 + 2 * M].rearrange("p (c m) -> p c m", c=2)
        col7 = x1[:, 1, 32:48].rearrange("p (a b) -> p a b", a=2)
        ybase = x1[:, 2, 64:64 + 2 * M * HD]
        dl = x1[:, 1, 64:72]
        lns = x1[:, 1, 80:84]

        ps = ctx.enter_context(nc.psum_tensor("ps", [P, 8, T], F32))

        for steps in (PE_A, ACT_A, VEC_A, POOL_A, PE_B, ACT_B, VEC_B, POOL_B, PE_C, ACT_C, VEC_C, POOL_C):
            steps.semaphores(sem)
        xa_in, xr_in, ctx_loaded, stored = (sem(n) for n in ("xa_in", "xr_in", "ctx_loaded", "stored"))
        w_attn, w_x, w_raw = (sem(n) for n in ("w_attn", "w_x", "w_raw"))
        pe_s, vec_s, act_s, chain = (sem(n) for n in ("pe_s", "vec_s", "act_s", "chain"))
        ready = sem("ready")
        block = ctx.enter_context(nc.Block())

        def tok(ap, i):
            return ap[i * SEQ:(i + 1) * SEQ] if isinstance(i, int) else ap[bass.ds(i * SEQ, SEQ)]

        def rows(ap, i):
            return tok(ap, i).rearrange("b (h p) d -> p (b h) d", p=P)

        def bb(ap, shape):
            return ap.broadcast_to(shape)

        n_attn = n_x = n_raw = 0

        LOADS_A, LOADS_X, LOADS_RAW = [], [], []
        LOADS_A += [(cst[:, :], consts), (e32[:, :, :], expand)]
        LOADS_A += [(win[:, :, 0:2 * D], in_proj[:, 0:2 * D].rearrange("(t p) n -> p t n", p=P)),
                    (g[:, 0, 0:DT * HEADS].rearrange("p (t n) -> p t n", t=DT),
                     in_proj[:, 2 * D:2 * D + HEADS].rearrange("(t p) n -> p t n", p=P)),
                    (wopj[:, :, :], out_proj.rearrange("(t p) n -> p t n", p=P))]
        for j in range(4):
            LOADS_A += [(cw[:, j, :], conv_w[:, 0, j * P:(j + 1) * P].rearrange("a p -> p a"))]
        LOADS_A += [(cb[:, 0:4], conv_b[0:2 * D].rearrange("(t p) -> p t", p=P)),
                    (thn[:, :, :], theta[0, 0].rearrange("(t k) h m -> (k h) t m", t=2)),
                    (c32[:, 0:4], conv_w[:, 0, 2 * D:].rearrange("a p -> p a")),
                    (c32[:, 4:5], conv_b[2 * D:].rearrange("(p a) -> p a", a=1)),
                    (c32[:, 5:6], score.rearrange("(p a) -> p a", a=1)),
                    (c32[0:HEADS - ANCHORS, 6:7], decay.rearrange("(p a) -> p a", a=1)),
                    (c32[HEADS - ANCHORS:HEADS, 6:7], anchor.rearrange("(p a) -> p a", a=1)),
                    (y8[:, 0, :, :], w_re.rearrange("(h m) n -> h m n", m=M)),
                    (y8[:, 1, :, :], w_im.rearrange("(h m) n -> h m n", m=M)),
                    (n8[:, :, :], norm_sc.rearrange("(c h m) -> h c m", c=2, m=M)),
                    (dl[:, 0:3], deriv.rearrange("(a n) -> a n", a=1).broadcast_to([P, 3]))]
        for dst, src in ((wqs, wq), (wks, wk), (wvs, wv), (wos, wo)):
            LOADS_X += [(dst[:, :, :], src.rearrange("(t p) n -> p t n", p=P))]
        LOADS_X += [(fdft[:, :, :], dft.rearrange("(t p) n -> p t n", p=P)),
                    (fidft[:, :, :], idft.rearrange("t p n -> p t n")),
                    (bos[:, :], bo.rearrange("(a n) -> a n", a=1).broadcast_to([P, D]))]
        for n, src in enumerate((bq, bk, bv)):
            LOADS_X += [(bqkv[:, n, :], src.rearrange("(a n) -> a n", a=1))]
        for dst, src in ((fq, f_q), (fk, f_k), (fo, f_o), (fi, f_inv), (fr, r_w1)):
            LOADS_RAW += [(dst, src.rearrange("(t p) n -> p t n", p=P))]
        for dst, src in list(zip(raw_v, (v_fwd, w_fwd, w_inv, v_inv))) + list(zip(raw_u, (u_fwd, u_inv))):
            for t in range(DT):
                LOADS_RAW += [(dst[:, t, :].rearrange("p (k r) -> p k r", k=KEXP),
                               src[:, t * P:(t + 1) * P, :].rearrange("k p r -> p k r"))]
        LOADS_RAW += [(rw2, r_w2), (b16[0:KEXP, :], b_fwd), (b16[KEXP:2 * KEXP, :], b_inv),
                      (selraw, select), (rb1[:, :], r_b1.rearrange("(t p) -> p t", p=P)),
                      (rb2[:, 0, :], r_b2.rearrange("(a n) -> a n", a=1).broadcast_to([P, KEXP])),
                      (rb2[:, 1, :], ebias.rearrange("(a n) -> a n", a=1).broadcast_to([P, KEXP])),
                      (acol[:, 0:1], alpha.rearrange("(a n) -> a n", a=1).broadcast_to([P, 1]))]

        @block.sync
        def _(sp):
            for dst, src in LOADS_A:
                sp.dma_start(dst, src).then_inc(w_attn, 16)

            def load_x(i):
                if not isinstance(i, int) or i > 0:
                    sp.wait_ge(*PE_A.at(i - 1, "xT", 1))
                sp.dma_start(xa[:, :, :], rows(x, i)).then_inc(xa_in, 16)

            def load_residual(i):
                if not isinstance(i, int) or i > 0:
                    sp.wait_ge(*VEC_A.at(i - 1, "norm", NQ - 1))
                sp.dma_start(xs_a[:, :, :], rows(x, i)).then_inc(xr_in, 16)

            def load_ctx(i):
                if not isinstance(i, int) or i > 0:
                    sp.wait_ge(*PE_B.at(i - 1, "cf", 1))
                sp.dma_start(cin[:, :, :], rows(ctx_in, i)).then_inc(ctx_loaded, 16)

            def store(i):
                sp.wait_ge(*VEC_C.at(i, "norm", NQ - 1))
                sp.dma_start(rows(out, i), xs_c[:, :, :]).then_inc(stored, 16)

            load_x(0)
            load_residual(0)
            for dst, src in LOADS_X:
                sp.dma_start(dst, src).then_inc(w_x, 16)
            load_ctx(0)
            for dst, src in LOADS_RAW:
                sp.dma_start(dst, src).then_inc(w_raw, 16)
            load_x(1)
            load_residual(1)
            load_ctx(1)
            load_x(2)
            load_residual(2)
            load_ctx(2)
            load_x(3)
            load_residual(3)
            store(0)
            with sp.Fori(3, NCHUNK - 1) as i:
                load_ctx(i)
                load_x(i + 1)
                load_residual(i + 1)
                store(i - 2)
            load_ctx(NCHUNK - 1)
            store(NCHUNK - 3)
            store(NCHUNK - 2)
            store(NCHUNK - 1)
            sp.wait_ge(stored, 16 * NCHUNK)

        NS = 0

        SETUP = ([("col", 0), ("col", 1), ("y", 0), ("ot", 0), ("ot", 1), ("it", 0), ("it", 1),
                  ("rt", 0), ("rt", 1), ("w2", 0), ("bt", 0), ("nq", 0), ("nq", 1), ("nk", 0), ("nk", 1)]
                 + [(m, br, t) for m in ("mv", "mw", "mr") for br in range(2) for t in range(DT)]
                 + [("up", j) for j in range(NJ)] + [("bp", 0)])

        def s_at(*name):
            return SETUP.index(name) + 1

        @block.tensor
        def _(pe):
            mm = nc.tensor.matmul

            def group(*name):
                k = SETUP.index(name)
                if k >= 8:
                    pe.wait_ge(vec_s, k - 7)
                return ps[:, k % 8, :]

            pe.wait_ge(w_attn, 16 * len(LOADS_A))
            pe.wait_ge(chain, SETUP_COL)
            for h in range(2):
                o = group("col", h)
                mm(o[:, 0:8], e32[:, h, :], c32t[:, 0:8], start=True, stop=True).then_inc(pe_s, 1)
            o = group("y", 0)
            mm(o[:, 0:2 * M * HD], e8, y8s.rearrange("p c m n -> p (c m n)"), start=True, stop=True)\
                .then_inc(pe_s, 1)
            pe.wait_ge(w_raw, 16 * len(LOADS_RAW))
            for name, src in (("ot", fo), ("it", fi), ("rt", fr)):
                for t in range(DT):
                    o = group(name, t)
                    for r in range(DT):
                        last = nc.tensor.transpose(o[:, r * P:(r + 1) * P], src[:, r, t * P:(t + 1) * P], ident)
                    last.then_inc(pe_s, 1)
            o = group("w2", 0)
            for t in range(DT):
                last = nc.tensor.transpose(o[:, t * KEXP:(t + 1) * KEXP], rw2[:, t * P:(t + 1) * P],
                                           ident[0:KEXP, 0:KEXP])
            last.then_inc(pe_s, 1)
            o = group("bt", 0)
            for t in range(DT):
                last = nc.tensor.transpose(o[:, t * 16:(t + 1) * 16], b16[:, t * P:(t + 1) * P], ident[0:16, 0:16])
            last.then_inc(pe_s, 1)

            def product(dst, lhs, rhs):
                for t in range(DT):
                    last = mm(dst, lhs(t), rhs(t), start=(t == 0), stop=(t == DT - 1))
                return last

            pe.wait_ge(vec_s, s_at("it", 1))
            for name, w in (("nq", fq), ("nk", fk)):
                for t in range(DT):
                    o = group(name, t)
                    product(o[:, 0:D], lambda r: fit[:, r, t * P:(t + 1) * P], lambda r: w[:, r, :])\
                        .then_inc(pe_s, 1)
            for name, lhs, rhs in (("mv", (fq, nqt), (raw_v[0], raw_v[2])),
                                   ("mw", (fk, nkt), (raw_v[1], raw_v[3])), ("mr", (fq, nqt), (frt, frt))):
                for br in range(2):
                    if name == "mv" and br == 1:
                        pe.wait_ge(vec_s, s_at("nk", 1))
                    for t in range(DT):
                        o = group(name, br, t)
                        n = D if name == "mr" else KEXP * R
                        product(o[:, 0:n], lambda r: lhs[br][:, r, t * P:(t + 1) * P],
                                lambda r: rhs[br][:, r, :]).then_inc(pe_s, 1)
            for j in range(NJ):
                o = group("up", j)
                u, c = raw_u[j // 4], (j % 4) * P
                product(o[:, 0:D], lambda r: u[:, r, c:c + P], lambda r: fot[:, r, :]).then_inc(pe_s, 1)
            o = group("bp", 0)
            product(o[0:16, 0:D], lambda r: bt[:, r, :], lambda r: fot[:, r, :]).then_inc(pe_s, 1)
            pe.wait_ge(ready, 1)

            def free_a(i, *name):
                prev, old = before(BANK_A, name)
                if old:
                    if isinstance(i, int) and i == 0:
                        return ps[:, BANK_A[name], :]
                    i = i - 1
                kind, n = prev
                if kind == "xT":
                    pe.wait_ge(*ACT_A.at(i, "xT", n))
                elif kind == "z":
                    pe.wait_ge(*VEC_A.at(i, "tap", n, 0))
                elif kind == "S":
                    pe.wait_ge(*VEC_A.at(i, "w", n))
                elif kind == "Y":
                    pe.wait_ge(*VEC_A.at(i, "y", n))
                else:
                    pe.wait_ge(*VEC_A.at(i, "res", n))
                return ps[:, BANK_A[name], :]

            def free_b(i, *name):
                prev, old = before(BANK_B, name)
                if old:
                    if isinstance(i, int) and i == 0:
                        return ps[:, BANK_B[name], :]
                    i = i - 1
                if prev[0] in ("corr", "out"):
                    pe.wait_ge(*VEC_B.at(i, *(prev if prev[0] == "corr" else ("res", prev[1]))))
                elif prev[0] == "wf":
                    pe.wait_ge(*VEC_B.at(i, "w3"))
                else:
                    pe.wait_ge(*ACT_B.at(i, *prev))
                return ps[:, BANK_B[name], :]

            def free_c(i, *name):
                prev, old = before(BANK_C, name)
                if old:
                    if isinstance(i, int) and i == 0:
                        return ps[:, BANK_C[name], :]
                    i = i - 1
                if prev[0] == "logit":
                    pe.wait_ge(*VEC_C.at(i, "logit"))
                elif prev[0] == "wT":
                    pe.wait_ge(*VEC_C.at(i, "wlow"))
                elif prev[0] == "w":
                    pe.wait_ge(*VEC_C.at(i, "cw", prev[1]))
                elif prev[0] == "x":
                    pe.wait_ge(*VEC_C.at(i, "prod", prev[1]))
                elif prev[0] == "out":
                    pe.wait_ge(*VEC_C.at(i, "res", prev[1]))
                else:
                    pe.wait_ge(*ACT_C.at(i, *prev))
                return ps[:, BANK_C[name], :]

            def a_project(i):
                pe.wait_ge(xa_in, 16 * i + 16)
                for t in range(DT):
                    o = free_a(i, "xT", t)
                    for q in range(NQ):
                        last = nc.tensor.transpose(o[:, q * P:(q + 1) * P], xa[:, q, t * P:(t + 1) * P], ident)
                    last.then_inc(*PE_A.tick("xT", t))
                for j in Z_ORDER:
                    o = free_a(i, "z", j)
                    pe.wait_ge(*ACT_A.at(i, "xT", 1))
                    for t in range(DT):
                        last = mm(o, win[:, t, j * P:(j + 1) * P], xt[:, t, :], start=(t == 0), stop=(t == DT - 1))
                    last.then_inc(*PE_A.tick("z", j))

            def a_sums(i, u):
                h, m = divmod(u, M)
                if m == 0:
                    free_a(i, "Y", h)
                y = ps[:, BANK_A[("Y", h)], :]
                pe.wait_ge(*VEC_A.at(i, "scan", u))
                for c in range(2):
                    last = mm(y, wy[:, 1 - c, m, :], sc[:, u % 4, c, :], start=(m == 0 and c == 0),
                              stop=(m == M - 1 and c == 1))
                last.then_inc(*PE_A.tick("y", u))

            def a_squares(i, h):
                o = free_a(i, "S", h)
                pe.wait_ge(*VEC_A.at(i, "acc", M * h + M - 1))
                for c in range(2):
                    last = mm(o, blk, acc[:, h, c, :], start=(c == 0), stop=(c == 1))
                last.then_inc(*PE_A.tick("S", h))

            def a_out(i):
                pe.wait_ge(*VEC_A.at(i, "y", 1))
                for n in range(2):
                    o = free_a(i, "out", n)
                    for q in range(2 * n, 2 * n + 2):
                        for t in range(DT):
                            last = mm(o[:, (q % 2) * D:(q % 2 + 1) * D], zc[:, 2 + t, q * P:(q + 1) * P],
                                      wopj[:, t, :], start=(t == 0), stop=(t == DT - 1))
                    last.then_inc(*PE_A.tick("out", n))

            def b_spectra(i):
                pe.wait_ge(*VEC_A.at(i, "norm", NQ - 1))
                for name, src in (("xf", x1), ("cf", cin)):
                    if name == "cf":
                        pe.wait_ge(ctx_loaded, 16 * i + 16)
                    for t in range(DT):
                        o = free_b(i, name, t)
                        for b in range(SEQ):
                            for h in range(2):
                                last = mm(o[:, b * L:(b + 1) * L], src[:, 2 * b + h, t * P:(t + 1) * P],
                                          fdft[:, h, :], start=(h == 0), stop=(h == 1))
                        last.then_inc(*PE_B.tick(name, t))
                for k, name in enumerate(SPEC):
                    o = free_b(i, name)
                    first = 0 if name[0] == "q" else 2
                    w = {"q": wqs, "k": wks, "v": wvs}[name[0]]
                    pe.wait_ge(*ACT_B.at(i, "xf" if first == 0 else "cf", 1))
                    for b in range(SEQ):
                        for t in range(DT):
                            c = b * L + (k % 2) * P
                            last = mm(o[:, b * D:(b + 1) * D], spec[:, first + t, c:c + P], w[:, t, :],
                                      start=(t == 0), stop=(t == DT - 1))
                    last.then_inc(*PE_B.tick(name))

            def b_corr(i):
                o = free_b(i, "corr")
                pe.wait_ge(*VEC_B.at(i, "cb2"))
                for part in range(2):
                    last = mm(o[0:BH, 0:L], cspec[:, part, :], fidft[:, part, :], start=(part == 0), stop=(part == 1))
                last.then_inc(*PE_B.tick("corr"))

            def b_weights(i):
                o = free_b(i, "wt")
                pe.wait_ge(*VEC_B.at(i, "wn"))
                for h in range(2):
                    last = mm(o[:, h * BH:(h + 1) * BH], cor[:, 0, h * P:(h + 1) * P], ident[0:BH, 0:BH],
                              start=True, stop=True)
                last.then_inc(*PE_B.tick("wt"))
                o = free_b(i, "wf")
                pe.wait_ge(*ACT_B.at(i, "wt"))
                for part in range(2):
                    for h in range(2):
                        last = mm(o[:, part * BH:(part + 1) * BH], fdft[:, h, part * P:(part + 1) * P], wtt[:, h, :],
                                  start=(h == 0), stop=(h == 1))
                last.then_inc(*PE_B.tick("wf"))

            def b_back(i):
                for t in range(DT):
                    o = free_b(i, "ot", t)
                    pe.wait_ge(*VEC_B.at(i, "o"))
                    for b in range(SEQ):
                        for part in range(2):
                            c = b * D + t * P
                            last = mm(o[:, b * L:(b + 1) * L], qkv[:, part, c:c + P], fidft[:, part, :],
                                      start=(part == 0), stop=(part == 1))
                    last.then_inc(*PE_B.tick("ot", t))

            def b_out(i):
                for n in range(2):
                    o = free_b(i, "out", n)
                    pe.wait_ge(*ACT_B.at(i, "ot", 1))
                    for q in range(2 * n, 2 * n + 2):
                        for t in range(DT):
                            last = mm(o[:, (q % 2) * D:(q % 2 + 1) * D], spec[:, t, q * P:(q + 1) * P],
                                      wos[:, t, :], start=(t == 0), stop=(t == DT - 1))
                    last.then_inc(*PE_B.tick("out", n))

            def c_router(i):
                pe.wait_ge(*VEC_B.at(i, "norm", NQ - 1))
                for t in range(DT):
                    o = free_c(i, "xT", t)
                    for q in range(NQ):
                        last = nc.tensor.transpose(o[:, q * P:(q + 1) * P], x2[:, q, t * P:(t + 1) * P], ident)
                    last.then_inc(*PE_C.tick("xT", t))
                for n in range(4):
                    br, r = divmod(n, 2)
                    o = free_c(i, "h", n)
                    pe.wait_ge(*ACT_C.at(i, "xT", 1))
                    for t in range(DT):
                        last = mm(o, mr[:, t, br, r * P:(r + 1) * P], x2t[:, t, :], start=(t == 0), stop=(t == 1))
                    last.then_inc(*PE_C.tick("h", n))

            def c_logits(i):
                o = free_c(i, "logit")
                pe.wait_ge(*ACT_C.at(i, "h", 3))
                for q in range(NQ):
                    for br in range(2):
                        c = (q * 2 + br) * KEXP
                        for r in range(DT):
                            last = mm(o[:, c:c + KEXP], hT[:, 2 * br + r, q * P:(q + 1) * P], w2t[:, r, :],
                                      start=(r == 0), stop=(r == 1))
                last.then_inc(*PE_C.tick("logit"))

            def c_weights(i):
                o = free_c(i, "wT")
                pe.wait_ge(*VEC_C.at(i, "weight"))
                for q in range(NQ):
                    last = nc.tensor.transpose(o[0:16, q * P:(q + 1) * P],
                                               lg[:, 2 * q:2 * q + 2, :].rearrange("p a b -> p (a b)"), ident)
                last.then_inc(*PE_C.tick("wT"))

            def c_sides(i, j):
                br, c = j // 4, (j % 4) * P
                o = free_c(i, "c", j)
                pe.wait_ge(*VEC_C.at(i, "cum"))
                for t in range(DT):
                    last = mm(o, mw[:, t, br, c:c + P], cum[:, t, :], start=(t == 0), stop=(t == 1))
                last.then_inc(*PE_C.tick("c", j))
                o = free_c(i, "x", j)
                for t in range(DT):
                    last = mm(o, mv[:, t, br, c:c + P], x2t[:, t, :], start=(t == 0), stop=(t == 1))
                last.then_inc(*PE_C.tick("x", j))

            def c_spread(i, j):
                o = free_c(i, "w", j)
                pe.wait_ge(*VEC_C.at(i, "wlow"))
                mm(o, sel[:, j, :], wpair[:, :], start=True, stop=True).then_inc(*PE_C.tick("w", j))

            def c_out(i):
                for n in range(2):
                    o = free_c(i, "out", n)
                    pe.wait_ge(*VEC_C.at(i, "prod", NJ - 1))
                    for q in range(2 * n, 2 * n + 2):
                        d = o[:, (q % 2) * D:(q % 2 + 1) * D]
                        for j in range(NJ):
                            mm(d, prod[:, j, q * P:(q + 1) * P], up[:, j, :], start=(j == 0), stop=False)
                        last = mm(d, wT[:, q * P:(q + 1) * P], bp[:, :], start=False, stop=True)
                    last.then_inc(*PE_C.tick("out", n))

            def turn(a, b, c):
                if a is not None:
                    a_project(a)
                if b is not None:
                    b_spectra(b)
                if c is not None:
                    c_router(c)
                    c_logits(c)
                    c_sides(c, 0)
                    c_weights(c)
                    c_spread(c, 0)
                for u in range(UNITS):
                    if b is not None and u == 1:
                        b_corr(b)
                    if b is not None and u == 3:
                        b_weights(b)
                    if b is not None and u == 5:
                        b_back(b)
                    if b is not None and u == 6:
                        b_out(b)
                    if c is not None and u > 0:
                        c_sides(c, u)
                        c_spread(c, u)
                    if a is not None and u > 0:
                        a_sums(a, u - 1)
                        if u - 1 == M:
                            a_squares(a, 0)
                if a is not None:
                    a_sums(a, UNITS - 1)
                    a_squares(a, 1)
                if c is not None:
                    c_out(c)
                if a is not None:
                    a_out(a)

            turn(0, None, None)
            turn(1, 0, None)
            turn(2, 1, 0)
            with pe.Fori(3, NCHUNK) as i:
                turn(i, i - 1, i - 2)
            turn(None, NCHUNK - 1, NCHUNK - 2)
            turn(None, None, NCHUNK - 1)

        @block.scalar
        def _(act):
            A = nc.scalar.activation
            act.wait_ge(chain, 2)
            A(c32t[:, 9:10], c32t[:, 8:9], ACT.Exp).then_inc(act_s, 1)
            act.wait_ge(chain, 3)
            A(c32t[:, 11:12], c32t[:, 10:11], ACT.Ln).then_inc(act_s, 1)
            act.wait_ge(chain, SETUP_DERIV)
            A(dl[:, 4:7], dl[:, 0:3], ACT.Exp).then_inc(act_s, 1)
            act.wait_ge(ready, 1)

            def a_front(i):
                for t in range(DT):
                    act.wait_ge(*PE_A.at(i, "xT", t))
                    A(xt[:, t, :], ps[:, BANK_A[("xT", t)], :], ACT.Copy).then_inc(*ACT_A.tick("xT", t))

                def z(j):
                    act.wait_ge(*PE_A.at(i, "z", j))
                    if not isinstance(i, int) or i > 0:
                        if j in (2, 3):
                            act.wait_ge(*PE_A.at(i - 1, "out", 1))
                        elif j < 2:
                            act.wait_ge(*VEC_A.at(i - 1, "frac", UNITS - 1))
                        else:
                            act.wait_ge(*VEC_A.at(i - 1, "gf", j - 4))
                    A(zc[:, j, :], ps[:, BANK_A[("z", j)], :], ACT.Identity, bias=cb[:, j:j + 1],
                      scale=cw[:, j, 3:4]).then_inc(*ACT_A.tick("z", j))

                def p(h):
                    act.wait_ge(*VEC_A.at(i, "expo", h))
                    A(zc[:, 4 + h, :], zc[:, 4 + h, :], ACT.Exp).then_inc(*ACT_A.tick("exp", h))

                z(4)
                z(0)
                p(0)
                z(5)
                z(1)
                p(1)
                z(2)
                z(3)
                for h in range(2):
                    act.wait_ge(*VEC_A.at(i, "tap", 2 + h, 0))
                    A(zc[:, 2 + h, :], zc[:, 2 + h, :], ACT.Silu).then_inc(*ACT_A.tick("silu", h))
                for h in range(2):
                    act.wait_ge(*VEC_A.at(i, "guard", h))
                    A(den[:, h, :], den[:, h, :], ACT.Square, scale=math.sqrt(EPS)).then_inc(*ACT_A.tick("e", h))

            def a_angles(i, u):
                act.wait_ge(*VEC_A.at(i, "frac", u))
                if u >= 2:
                    act.wait_ge(*VEC_A.at(i, "re", u - 2))
                elif not isinstance(i, int) or i > 0:
                    act.wait_ge(*VEC_A.at(i - 1, "re", UNITS - 2 + u))
                A(hq[:, u % 2, :], frac[:, u % 2, :], ACT.Sin, scale=math.pi).then_inc(*ACT_A.tick("half", u))
                act.wait_ge(*ACT_A.at(i, "half", u))
                A(hq[:, u % 2, :], hq[:, u % 2, :], ACT.Square, scale=math.sqrt(2.0)).then_inc(*ACT_A.tick("cos", u))
                if u >= 4:
                    pe_i, pe_u = i, u - 4
                else:
                    pe_i, pe_u = i - 1, u + 4
                if u >= 4 or not isinstance(i, int) or i > 0:
                    act.wait_ge(*PE_A.at(pe_i, "y", pe_u))
                A(sc[:, u % 4, 0, :], frac[:, u % 2, :], ACT.Sin, scale=2.0 * math.pi)\
                    .then_inc(*ACT_A.tick("sin", u))

            def a_squares(i, u):
                act.wait_ge(*VEC_A.at(i, "scan", u))
                h, m = divmod(u, M)
                if m == 0:
                    dst = acc[:, h, :, :]
                    if not isinstance(i, int) or i > 0:
                        act.wait_ge(*PE_A.at(i - 1, "S", h))
                else:
                    dst = sq[:, u % 2, :, :]
                    before_it = [v for v in range(UNITS) if v % M and v % 2 == u % 2 and v < u]
                    if before_it:
                        act.wait_ge(*VEC_A.at(i, "acc", before_it[-1]))
                    elif not isinstance(i, int) or i > 0:
                        act.wait_ge(*VEC_A.at(i - 1, "acc", UNITS - 1 if u % 2 else UNITS - 2))
                A(dst, sc[:, u % 4, :, :], ACT.Square, scale=1.0 / math.sqrt(2.0 * HD * M))\
                    .then_inc(*ACT_A.tick("sq", u))

            def a_norm(i, h):
                act.wait_ge(*VEC_A.at(i, "w", h))
                A(den[:, h, :], den[:, h, :], ACT.Ln).then_inc(*ACT_A.tick("ln", h))
                act.wait_ge(*ACT_A.at(i, "ln", h))
                A(den[:, h, :], den[:, h, :], ACT.Exp, scale=-0.5).then_inc(*ACT_A.tick("f", h))

            def b_spectra(i):
                for name, first in (("xf", 0), ("cf", 2)):
                    for t in range(DT):
                        act.wait_ge(*PE_B.at(i, name, t))
                        if t == 0 and first == 0 and (not isinstance(i, int) or i > 0):
                            act.wait_ge(*PE_B.at(i - 1, "out", 1))
                            act.wait_ge(*VEC_B.at(i - 1, "o"))
                        A(spec[:, first + t, :], ps[:, BANK_B[(name, t)], :], ACT.Copy)\
                            .then_inc(*ACT_B.tick(name, t))
                for k, name in enumerate(SPEC):
                    act.wait_ge(*PE_B.at(i, name))
                    if k == 0 and (not isinstance(i, int) or i > 0):
                        act.wait_ge(*PE_B.at(i - 1, "ot", 1))
                    A(qkv[:, k, :], ps[:, BANK_B[(name,)], :], ACT.Copy).then_inc(*ACT_B.tick(name))

            def b_exp(i):
                act.wait_ge(*VEC_B.at(i, "negmax"))
                A(cor[:, 4, :], cor[:, 0, :], ACT.Exp, bias=sm[:, 8:9]).then_inc(*ACT_B.tick("exp"))

            def b_wt(i):
                act.wait_ge(*PE_B.at(i, "wt"))
                A(wtt[:, :, :], ps[:, BANK_B[("wt",)], 0:2 * BH].rearrange("p (a b) -> p a b", a=2), ACT.Copy)\
                    .then_inc(*ACT_B.tick("wt"))

            def b_back(i):
                for t in range(DT):
                    act.wait_ge(*PE_B.at(i, "ot", t))
                    if t == 0:
                        act.wait_ge(*VEC_B.at(i, "o"))
                    A(spec[:, t, :], ps[:, BANK_B[("ot", t)], :], ACT.Copy).then_inc(*ACT_B.tick("ot", t))

            def c_front(i):
                for t in range(DT):
                    act.wait_ge(*PE_C.at(i, "xT", t))
                    A(x2t[:, t, :], ps[:, BANK_C[("xT", t)], :], ACT.Copy).then_inc(*ACT_C.tick("xT", t))
                for n in range(4):
                    act.wait_ge(*PE_C.at(i, "h", n))
                    if n == 0 and (not isinstance(i, int) or i > 0):
                        act.wait_ge(*PE_C.at(i - 1, "out", 1))
                    A(hT[:, n, :], ps[:, BANK_C[("h", n)], :], ACT.Gelu, bias=rb1[:, n % 2:n % 2 + 1])\
                        .then_inc(*ACT_C.tick("h", n))

            def c_exp(i):
                act.wait_ge(*VEC_C.at(i, "sub"))
                A(lg[:, :, :], lg[:, :, :], ACT.Exp).then_inc(*ACT_C.tick("exp"))

            def c_weights(i):
                act.wait_ge(*PE_C.at(i, "wT"))
                A(wT[:, :], ps[0:2 * KEXP, BANK_C[("wT",)], :], ACT.Copy).then_inc(*ACT_C.tick("wT"))
                A(wpair[0:2 * KEXP, :], ps[0:2 * KEXP, BANK_C[("wT",)], :], ACT.Copy).then_inc(*ACT_C.tick("whigh"))

            def c_tile(i, j):
                act.wait_ge(*PE_C.at(i, "c", j))
                if j >= 2:
                    act.wait_ge(*VEC_C.at(i, "prod", j - 2))
                elif not isinstance(i, int) or i > 0:
                    act.wait_ge(*VEC_C.at(i - 1, "prod", NJ - 2 + j))
                A(cs[:, j % 2, :], ps[:, BANK_C[("c", j)], :], ACT.Copy).then_inc(*ACT_C.tick("c", j))

            def turn(a, b, c):
                if a is not None:
                    a_front(a)
                if b is not None:
                    b_spectra(b)
                if c is not None:
                    c_front(c)
                    c_exp(c)
                    c_tile(c, 0)
                    c_weights(c)
                if a is not None:
                    a_angles(a, 0)
                    a_angles(a, 1)
                for u in range(UNITS):
                    if b is not None and u == 1:
                        b_exp(b)
                    if b is not None and u == 3:
                        b_wt(b)
                    if b is not None and u == 5:
                        b_back(b)
                    if a is not None:
                        if u + 2 < UNITS:
                            a_angles(a, u + 2)
                        a_squares(a, u)
                        if u == M + 2:
                            a_norm(a, 0)
                    if c is not None and u > 0:
                        c_tile(c, u)
                if a is not None:
                    a_norm(a, 1)

            turn(0, None, None)
            turn(1, 0, None)
            turn(2, 1, 0)
            with act.Fori(3, NCHUNK) as i:
                turn(i, i - 1, i - 2)
            turn(None, NCHUNK - 1, NCHUNK - 2)
            turn(None, None, NCHUNK - 1)

        @block.gpsimd
        def _(pool):
            G = nc.gpsimd
            pool.wait_ge(ready, 1)

            def rstd(i, k, VEC, OWN):
                pool.wait_ge(*VEC.at(i, "aggr", NQ - 1))
                G.tensor_tensor(rs[k][:, 0, :], mvr[k][:, :, 1], eps_[:, :], ALU.add)\
                    .then_inc(*OWN.tick("var"))
                pool.wait_ge(*OWN.at(i, "var"))
                G.tensor_tensor(rs[k][:, 1, :], rs[k][:, 0, :], half_[:, :], ALU.pow)\
                    .then_inc(*OWN.tick("rstd"))

            def b_front(i):
                pool.wait_ge(*VEC_A.at(i, "norm", NQ - 1))
                pool.wait_ge(*PE_B.at(i, "xf", 1))
                G.tensor_tensor(x1[:, :, :], x1[:, :, :], bos[:, :].unsqueeze(1).broadcast_to([P, NQ, D]), ALU.add)\
                    .then_inc(*POOL_B.tick("res"))
                for n, name in enumerate(("q", "k", "v")):
                    pool.wait_ge(*ACT_B.at(i, name + "a"))
                    row = qkv[0:1, 2 * n, :].rearrange("p (b d) -> p b d", b=SEQ)
                    G.tensor_tensor(row, row, bqkv[:, n, :].unsqueeze(1).broadcast_to([1, SEQ, D]), ALU.add)\
                        .then_inc(*POOL_B.tick("b" + name))

            def turn(a, b, c):
                if b is not None:
                    b_front(b)
                if c is not None:
                    rstd(c, 2, VEC_C, POOL_C)
                if b is not None:
                    rstd(b, 1, VEC_B, POOL_B)
                if a is not None:
                    rstd(a, 0, VEC_A, POOL_A)

            turn(0, None, None)
            turn(1, 0, None)
            turn(2, 1, 0)
            with pool.Fori(3, NCHUNK) as i:
                turn(i, i - 1, i - 2)
            turn(None, NCHUNK - 1, NCHUNK - 2)
            turn(None, None, NCHUNK - 1)

        @block.vector
        def _(dve):
            V = nc.vector
            TS, TT, STT = V.tensor_scalar, V.tensor_tensor, V.scalar_tensor_tensor
            count = [0]

            def link(ins):
                ins.then_inc(chain, 1)
                count[0] += 1
                dve.wait_ge(chain, count[0])

            dve.wait_ge(w_attn, 16 * len(LOADS_A))
            slope, e, u1 = c32[:, 6:7], c32t[:, 9:10], c32t[:, 10:11]
            link(TS(c32t[:, 12:13], slope, -1.0, None, ALU.mult))
            V.memset(mask[:, :], 1.0)
            V.memset(half_[:, :], -0.5)
            V.memset(eps_[:, :], EPS)
            V.tensor_copy(c32t[:, 0:6], c32[:, 0:6])
            link(TT(c32t[:, 8:9], slope, c32t[:, 12:13], ALU.min))
            dve.wait_ge(act_s, 1)
            link(TS(u1, e, 1.0, None, ALU.add))
            link(TS(c32t[:, 12:13], u1, 1.0, None, ALU.subtract))
            link(TS(c32t[:, 13:14], u1, 1.0, None, ALU.is_equal))
            link(TT(c32t[:, 12:13], c32t[:, 12:13], c32t[:, 13:14], ALU.add))
            link(V.reciprocal(c32t[:, 12:13], c32t[:, 12:13]))
            dve.wait_ge(act_s, 2)
            link(TT(c32t[:, 14:15], c32t[:, 11:12], c32t[:, 13:14], ALU.add))
            link(TT(c32t[:, 14:15], c32t[:, 14:15], e, ALU.mult))
            link(TT(c32t[:, 14:15], c32t[:, 14:15], c32t[:, 12:13], ALU.mult))
            link(TS(c32t[:, 15:16], slope, 0.0, None, ALU.max))
            link(V.memset(c32t[:, 7:8], 0.0))
            link(TT(c32t[:, 6:7], c32t[:, 14:15], c32t[:, 15:16], ALU.add))
            link(TT(y8s[:, :, :, :], y8[:, :, :, :], n8.unsqueeze(3).broadcast_to([HD, 2, M, HD]), ALU.mult))
            link(TS(y8s[:, 0, :, :], y8s[:, 0, :, :], -1.0, None, ALU.mult))
            assert count[0] == SETUP_COL
            link(V.tensor_reduce(dl[:, 3:4], dl[:, 0:3], AX.X, ALU.max))
            link(TS(dl[:, 0:3], dl[:, 0:3], dl[:, 3:4], None, ALU.subtract))
            assert count[0] == SETUP_DERIV
            dve.wait_ge(act_s, 3)
            link(V.tensor_reduce(dl[:, 3:4], dl[:, 4:7], AX.X, ALU.add))
            link(V.reciprocal(dl[:, 3:4], dl[:, 3:4]))
            link(TS(dw[:, 0:3], dl[:, 4:7], dl[:, 3:4], None, ALU.mult))
            link(TS(dw[:, 2:3], dw[:, 2:3], -1.0, None, ALU.mult))
            link(TS(thn[:, :, :], thn[:, :, :], 1.0 / (2.0 * math.pi), None, ALU.mult))
            link(V.memset(mask[:, :].rearrange("p (s l) -> p s l", l=L)[:, :, 0:1], 0.0))
            sraw = g[:, 0, 0:DT * HEADS].rearrange("p (t n) -> p t n", t=DT)
            for t in range(DT):
                link(V.tensor_copy(win[:, t, 2 * D:].rearrange("p (k h) -> p k h", h=HD),
                                   sraw[:, t, :].unsqueeze(2).broadcast_to([P, HEADS, HD])))
            evs = [0]

            def evac(*name):
                k = SETUP.index(name)
                assert k == evs[0]
                evs[0] += 1
                dve.wait_ge(pe_s, k + 1)
                return ps[:, k % 8, :]

            for h in range(2):
                V.tensor_copy(col7[:, h, :], evac("col", h)[:, 0:8]).then_inc(vec_s, 1)
            V.tensor_copy(ybase, evac("y", 0)[:, 0:2 * M * HD]).then_inc(vec_s, 1)
            dve.wait_ge(vec_s, 3)
            V.tensor_copy(ss[:, :], col7[:, :, 5])
            for h in range(2):
                V.tensor_copy(cw[:, 4 + h, :], col7[:, h, 0:4])
            link(V.tensor_copy(cb[:, 4:6], col7[:, :, 4]))
            link(TS(lns[:, 0:2], col7[:, :, 6], -(L - 1.0), None, ALU.mult))
            link(TS(lns[:, 2:4], col7[:, :, 6], -1.0, None, ALU.mult))
            for h in range(2):
                link(TS(lt[:, h, :], pos, col7[:, h, 6:7], lns[:, h:h + 1], ALU.mult, ALU.add))
            a0 = (HEADS // 2 - ANCHORS) * HD
            link(TS(lt[a0:P, 1, :], pos[a0:P, :], lns[a0:P, 3:4], None, ALU.mult))
            for c in range(2):
                for m in range(M):
                    k = (c * M + m) * HD
                    link(TT(wy[:, c, m, :].rearrange("p (k n) -> p k n", n=HD),
                            ybase[:, k:k + HD].unsqueeze(1).broadcast_to([P, 16, HD]),
                            headm.unsqueeze(2).broadcast_to([P, 16, HD]), ALU.mult))
            dve.wait_ge(w_x, 16 * len(LOADS_X))
            dve.wait_ge(w_raw, 16 * len(LOADS_RAW))
            link(V.tensor_copy(sel[:, :, :], selraw))
            V.memset(wpair[:, :].bitcast(F32), 0.0)
            link(TS(bqkv[:, :, :], bqkv[:, :, :], float(L), None, ALU.mult))
            link(TT(rb2[:, 0, :], rb2[:, 0, :], rb2[:, 1, :], ALU.add))
            link(V.tensor_copy(rb2[:, 1, :], rb2[:, 0, :]))
            link(V.memset(acol[:, 1:2], 1.0))
            link(TS(dl[0:16, 0:1], cst[0:16, C_HM:C_HM + 1], 1.0, None, ALU.mult))
            link(TS(dl[0:16, 1:2], acol[0:16, 0:1], 1.0, None, ALU.subtract))
            link(TS(dl[0:16, 0:1], dl[0:16, 0:1], -1.0, 1.0, ALU.mult, ALU.add))
            link(TT(dl[0:16, 2:3], dl[0:16, 0:1], dl[0:16, 1:2], ALU.mult))
            link(TT(acol[0:16, 1:2], acol[0:16, 1:2], dl[0:16, 2:3], ALU.add))
            for name, dst in (("ot", fot), ("it", fit), ("rt", frt)):
                for t in range(DT):
                    V.tensor_copy(dst[:, t, :], evac(name, t)[:, 0:D]).then_inc(vec_s, 1)
            V.tensor_copy(w2t[:, :, :], evac("w2", 0)[:, 0:DT * KEXP].rearrange("p (t n) -> p t n", t=DT))\
                .then_inc(vec_s, 1)
            V.tensor_copy(bt, evac("bt", 0)[:, 0:DT * 16].rearrange("p (t n) -> p t n", t=DT)).then_inc(vec_s, 1)
            for name, dst in (("nq", nqt), ("nk", nkt)):
                for t in range(DT):
                    V.tensor_copy(dst[:, t, :], evac(name, t)[:, 0:D]).then_inc(vec_s, 1)
            for name, dst in (("mv", mv), ("mw", mw), ("mr", mr)):
                for br in range(2):
                    for t in range(DT):
                        V.tensor_copy(dst[:, t, br, :], evac(name, br, t)[:, 0:(D if name == "mr" else T)])\
                            .then_inc(vec_s, 1)
            for j in range(NJ):
                TS(up[:, j, :], evac("up", j)[:, 0:D], acol[:, 0:1] if j >= NJ // 2 else 1.0, None, ALU.mult)\
                    .then_inc(vec_s, 1)
            TS(bp[:, :], evac("bp", 0)[0:16, 0:D], acol[0:16, 1:2], None, ALU.mult).then_inc(vec_s, 1)
            dve.wait_ge(vec_s, len(SETUP))
            V.memset(dw[:, 3:4], 0.0).then_inc(ready, 1)

            def a_tap(i, j, tap):
                s = TAPS - 1 - tap
                o = zc[:, j, :].rearrange("p (b l) -> p b l", b=SEQ)
                z = ps[:, BANK_A[("z", j)], :].rearrange("p (b l) -> p b l", b=SEQ)
                if tap == 2:
                    dve.wait_ge(*ACT_A.at(i, "z", j))
                else:
                    dve.wait_ge(*VEC_A.at(i, "tap", j, tap + 1))
                STT(o[:, :, s:L], z[:, :, 0:L - s], cw[:, j, tap:tap + 1], o[:, :, s:L], ALU.mult, ALU.add)\
                    .then_inc(*VEC_A.tick("tap", j, tap))

            def a_exponent(i, h):
                z = zc[:, 4 + h, :]
                dve.wait_ge(*VEC_A.at(i, "tap", 4 + h, 0))
                TS(z, z, ss[:, h:h + 1], 20.0, ALU.mult, ALU.min).then_inc(*VEC_A.tick("clip", h))
                dve.wait_ge(*VEC_A.at(i, "clip", h))
                z3 = z.rearrange("p (b l) -> p b l", b=SEQ)
                STT(z3, z3, -20.0, lt[:, h, :].unsqueeze(1).broadcast_to([P, SEQ, L]), ALU.max, ALU.add)\
                    .then_inc(*VEC_A.tick("expo", h))

            def a_fraction(i, u):
                h, m = divmod(u, M)
                if m == 0:
                    dve.wait_ge(*VEC_A.at(i, "tap", h, 0))
                if u >= 2:
                    dve.wait_ge(*ACT_A.at(i, "sin", u - 2))
                    dve.wait_ge(*VEC_A.at(i, "re", u - 2))
                elif not isinstance(i, int) or i > 0:
                    dve.wait_ge(*ACT_A.at(i - 1, "sin", UNITS - 2 + u))
                TS(kturn[:, u % 2, :], zc[:, h, :], thn[:, h, m:m + 1], None, ALU.mult)\
                    .then_inc(*VEC_A.tick("turns", u))
                dve.wait_ge(*VEC_A.at(i, "turns", u))
                STT(frac[:, u % 2, :], zc[:, h, :], thn[:, h, m:m + 1], kturn[:, u % 2, :], ALU.mult, ALU.subtract)\
                    .then_inc(*VEC_A.tick("frac", u))

            def a_poly(i, h):
                z = zc[:, h, :]
                dve.wait_ge(*VEC_A.at(i, "tap", h, 0))
                if not isinstance(i, int) or i > 0:
                    dve.wait_ge(*VEC_A.at(i - 1, "re", M * h + M - 1))
                TS(g[:, h, :], z, dw[:, 2:3], dw[:, 1:2], ALU.mult, ALU.add).then_inc(*VEC_A.tick("p1", h))
                dve.wait_ge(*VEC_A.at(i, "p1", h))
                TT(g[:, h, :], g[:, h, :], z, ALU.mult).then_inc(*VEC_A.tick("p2", h))
                dve.wait_ge(*VEC_A.at(i, "p2", h))
                dve.wait_ge(*ACT_A.at(i, "exp", h))
                STT(g[:, h, :], g[:, h, :], dw[:, 0:1], zc[:, 4 + h, :], ALU.add, ALU.mult)\
                    .then_inc(*VEC_A.tick("g", h))

            def a_den(i, h):
                dve.wait_ge(*VEC_A.at(i, "g", h))
                V.tensor_tensor_scan(den[:, h, :], mask[:, 0:T], den[:, h, :], 0.0, ALU.mult, ALU.add)\
                    .then_inc(*VEC_A.tick("den", h))
                dve.wait_ge(*VEC_A.at(i, "den", h))
                TS(den[:, h, :], den[:, h, :], 1e-4, None, ALU.max).then_inc(*VEC_A.tick("guard", h))

            def a_moments(i, u):
                h, s = u // M, u % 4
                dve.wait_ge(*ACT_A.at(i, "sin", u))
                if u % M == 0:
                    dve.wait_ge(*VEC_A.at(i, "g", h))
                TT(sc[:, s, 0, :], sc[:, s, 0, :], g[:, h, :], ALU.mult).then_inc(*VEC_A.tick("im", u))
                STT(sc[:, s, 1, :], hq[:, u % 2, :], 1.0, g[:, h, :], ALU.subtract, ALU.mult)\
                    .then_inc(*VEC_A.tick("re", u))

            def a_scan(i, u):
                flat = sc[:, u % 4, :, :].rearrange("p c t -> p (c t)")
                dve.wait_ge(*VEC_A.at(i, "re", u))
                V.tensor_tensor_scan(flat, mask[:, 0:2 * T], flat, 0.0, ALU.mult, ALU.add)\
                    .then_inc(*VEC_A.tick("scan", u))

            def a_accumulate(i, u):
                h, m = divmod(u, M)
                dve.wait_ge(*ACT_A.at(i, "sq", u))
                if m > 1:
                    dve.wait_ge(*VEC_A.at(i, "acc", u - 1))
                TT(acc[:, h, :, :], acc[:, h, :, :], sq[:, u % 2, :, :], ALU.add).then_inc(*VEC_A.tick("acc", u))

            def a_heads(i, h):
                dve.wait_ge(*PE_A.at(i, "S", h))
                dve.wait_ge(*ACT_A.at(i, "e", h))
                TT(den[:, h, :], ps[:, BANK_A[("S", h)], :], den[:, h, :], ALU.add).then_inc(*VEC_A.tick("w", h))
                dve.wait_ge(*ACT_A.at(i, "f", h))
                TT(zc[:, 2 + h, :], zc[:, 2 + h, :], den[:, h, :], ALU.mult).then_inc(*VEC_A.tick("gf", h))
                dve.wait_ge(*VEC_A.at(i, "gf", h))
                dve.wait_ge(*PE_A.at(i, "y", M * h + M - 1))
                TT(zc[:, 2 + h, :], zc[:, 2 + h, :], ps[:, BANK_A[("Y", h)], :], ALU.mult)\
                    .then_inc(*VEC_A.tick("y", h))

            def layer_norm(i, k, xs, dst, VEC, POOL):
                for q in range(NQ):
                    dve.wait_ge(*VEC.at(i, "res", q // 2))
                    V.bn_stats(st[k][:, q, :], xs[:, q, :]).then_inc(*VEC.tick("stats", q))
                dve.wait_ge(*VEC.at(i, "stats", NQ - 1))
                V.tensor_copy(seen[:, k:k + 1], st[k][:, 0, 0:1])
                for q in range(NQ):
                    V.bn_aggr(mvr[k][:, q, :], st[k][:, q, :]).then_inc(*VEC.tick("aggr", q))
                dve.wait_ge(*POOL.at(i, "rstd"))
                for q in range(NQ):
                    TS(dst[:, q, :], xs[:, q, :], mvr[k][:, q, 0:1], rs[k][:, 1, q:q + 1], ALU.subtract, ALU.mult)\
                        .then_inc(*VEC.tick("norm", q))

            def a_finish(i):
                for n in range(2):
                    dve.wait_ge(*PE_A.at(i, "out", n))
                    if n == 0:
                        dve.wait_ge(xr_in, 16 * i + 16)
                    o = xs_a[:, 2 * n:2 * n + 2, :]
                    TT(o, o, ps[:, BANK_A[("out", n)], :].rearrange("p (q d) -> p q d", q=2), ALU.add)\
                        .then_inc(*VEC_A.tick("res", n))
                layer_norm(i, 0, xs_a, x1, VEC_A, POOL_A)

            def b_products(i):
                dve.wait_ge(*ACT_B.at(i, "kb"))
                dve.wait_ge(*POOL_B.at(i, "bk"))
                dve.wait_ge(*PE_B.at(i, "vb"))
                TT(spec[:, 0:2, :], qkv[:, 0:2, :], qkv[:, 2:4, :], ALU.mult).then_inc(*VEC_B.tick("aabb"))
                TT(spec[:, 2, :], qkv[:, 0, :], qkv[:, 3, :], ALU.mult).then_inc(*VEC_B.tick("ab"))
                TT(spec[:, 3, :], qkv[:, 1, :], qkv[:, 2, :], ALU.mult).then_inc(*VEC_B.tick("ba"))
                dve.wait_ge(*VEC_B.at(i, "ba"))
                V.tensor_reduce(rsum[:, :, :], spec[:, :, :].rearrange("p a (h d) -> p a h d", d=XD), AX.X, ALU.add)\
                    .then_inc(*VEC_B.tick("heads"))
                aa, bb_, ab, ba = (rsum[:, n, :] for n in range(4))
                dve.wait_ge(*VEC_B.at(i, "heads"))
                STT(cspec[:, 0, :], bb_, m0, aa, ALU.mult, ALU.add).then_inc(*VEC_B.tick("ca"))
                TT(cspec[:, 2, :], ba, ab, ALU.subtract).then_inc(*VEC_B.tick("cb0"))
                TS(cspec[:, 3, :], bb_, m1, None, ALU.mult).then_inc(*VEC_B.tick("cb1"))
                dve.wait_ge(*VEC_B.at(i, "cb1"))
                STT(cspec[:, 1, :], cspec[:, 2, :], m0, cspec[:, 3, :], ALU.mult, ALU.add)\
                    .then_inc(*VEC_B.tick("cb2"))

            def b_topk(i):
                c, top = cor[:, 0, :], sm[:, 0:8]
                above, equal, order = cor[:, 1, :], cor[:, 2, :], cor[:, 3, :]
                dve.wait_ge(*PE_B.at(i, "corr"))
                TS(c, ps[0:BH, BANK_B[("corr",)], 0:L], 1.0 / XD, None, ALU.mult).then_inc(*VEC_B.tick("corr"))
                dve.wait_ge(*VEC_B.at(i, "corr"))
                V.tensor_copy(sm[:, 12:13], cor[:, 0, 0:1])
                V.max(top, c).then_inc(*VEC_B.tick("top"))
                dve.wait_ge(*VEC_B.at(i, "top"))
                TS(sm[:, 8:9], sm[:, 0:1], -1.0, None, ALU.mult).then_inc(*VEC_B.tick("negmax"))
                kth = sm[:, TOPK - 1:TOPK]
                TS(above, c, kth, None, ALU.is_gt, ALU.add, accum_out=sm[:, 9:10]).then_inc(*VEC_B.tick("above"))
                TS(equal, c, kth, None, ALU.is_equal).then_inc(*VEC_B.tick("equal"))
                dve.wait_ge(*VEC_B.at(i, "equal"))
                V.tensor_tensor_scan(order, mask[0:BH, 1:2].broadcast_to([BH, L]), equal, 0.0, ALU.mult, ALU.add)\
                    .then_inc(*VEC_B.tick("order"))
                dve.wait_ge(*VEC_B.at(i, "order"))
                TS(order, order, sm[:, 9:10], float(TOPK), ALU.add, ALU.is_le).then_inc(*VEC_B.tick("first"))
                dve.wait_ge(*VEC_B.at(i, "first"))
                TT(order, order, equal, ALU.mult).then_inc(*VEC_B.tick("also"))
                dve.wait_ge(*VEC_B.at(i, "also"))
                TT(above, above, order, ALU.add).then_inc(*VEC_B.tick("keep"))
                dve.wait_ge(*VEC_B.at(i, "keep"))
                dve.wait_ge(*ACT_B.at(i, "exp"))
                STT(cor[:, 2, :], cor[:, 4, :], 1.0, above, ALU.mult, ALU.mult, accum_out=sm[:, 10:11])\
                    .then_inc(*VEC_B.tick("weight"))
                dve.wait_ge(*VEC_B.at(i, "weight"))
                V.reciprocal(sm[:, 11:12], sm[:, 10:11]).then_inc(*VEC_B.tick("inv"))
                dve.wait_ge(*VEC_B.at(i, "inv"))
                TS(cor[:, 0, :], cor[:, 2, :], sm[:, 11:12], None, ALU.mult).then_inc(*VEC_B.tick("wn"))

            def b_apply(i):
                dve.wait_ge(*PE_B.at(i, "wf"))
                wa, wb = (ps[:, BANK_B[("wf",)], n * BH:(n + 1) * BH] for n in range(2))
                V.tensor_copy(wspec[:, 0, :], wa).then_inc(*VEC_B.tick("w1"))
                TS(wspec[:, 1, :], wb, m0, None, ALU.mult).then_inc(*VEC_B.tick("w2"))
                TS(wspec[:, 2, :], wb, m0, -1.0, ALU.mult, ALU.mult).then_inc(*VEC_B.tick("w4"))
                TS(cspec[:, 2, :], wb, m1, None, ALU.mult).then_inc(*VEC_B.tick("w3a"))
                dve.wait_ge(*VEC_B.at(i, "w3a"))
                STT(wspec[:, 3, :], wa, m0, cspec[:, 2, :], ALU.mult, ALU.add).then_inc(*VEC_B.tick("w3"))
                dve.wait_ge(*VEC_B.at(i, "w3"))
                dve.wait_ge(*ACT_B.at(i, "vb"))
                dve.wait_ge(*POOL_B.at(i, "bv"))
                v = qkv[:, 4:6, :].rearrange("p a (h d) -> p a h d", d=XD)
                for n, name in ((0, "oa"), (2, "ob")):
                    TT(spec[:, n:n + 2, :].rearrange("p a (h d) -> p a h d", d=XD), v,
                       wspec[:, n:n + 2, :].unsqueeze(3).broadcast_to([P, 2, BH, XD]), ALU.mult)\
                        .then_inc(*VEC_B.tick(name))
                dve.wait_ge(*VEC_B.at(i, "ob"))
                s4 = spec[:, :, :].rearrange("p (a b) t -> p a b t", b=2)
                TT(qkv[:, 0:2, :], s4[:, :, 0, :], s4[:, :, 1, :], ALU.add).then_inc(*VEC_B.tick("o"))

            def b_finish(i):
                for n in range(2):
                    dve.wait_ge(*PE_B.at(i, "out", n))
                    if n == 0:
                        dve.wait_ge(*POOL_B.at(i, "res"))
                    o = x1[:, 2 * n:2 * n + 2, :]
                    TT(o, o, ps[:, BANK_B[("out", n)], :].rearrange("p (q d) -> p q d", q=2), ALU.add)\
                        .then_inc(*VEC_B.tick("res", n))
                layer_norm(i, 1, x1, x2, VEC_B, POOL_B)

            def c_cum(i):
                dve.wait_ge(*ACT_C.at(i, "xT", 1))
                if not isinstance(i, int) or i > 0:
                    dve.wait_ge(*PE_C.at(i - 1, "c", NJ - 1))
                V.tensor_tensor_scan(cum[:, :, :].rearrange("p a t -> p (a t)"), mask[:, 0:DT * T],
                                     x2t[:, :, :].rearrange("p a t -> p (a t)"), 0.0, ALU.mult, ALU.add)\
                    .then_inc(*VEC_C.tick("cum"))

            def c_softmax(i):
                n = NQ * 2
                dve.wait_ge(*PE_C.at(i, "logit"))
                TT(lg[:, :, :].rearrange("p (q b) k -> p q (b k)", b=2),
                   ps[:, BANK_C[("logit",)], 0:n * KEXP].rearrange("p (q b) -> p q b", q=NQ),
                   rb2[:, :, :].rearrange("p b k -> p (b k)").unsqueeze(1).broadcast_to([P, NQ, 2 * KEXP]), ALU.add)\
                    .then_inc(*VEC_C.tick("logit"))
                dve.wait_ge(*VEC_C.at(i, "logit"))
                V.tensor_reduce(ls[:, 0, :], lg[:, :, :], AX.X, ALU.max).then_inc(*VEC_C.tick("max"))
                dve.wait_ge(*VEC_C.at(i, "max"))
                TT(lg[:, :, :], lg[:, :, :], ls[:, 0, :].unsqueeze(2).broadcast_to([P, n, KEXP]), ALU.subtract)\
                    .then_inc(*VEC_C.tick("sub"))
                dve.wait_ge(*ACT_C.at(i, "exp"))
                V.tensor_reduce(ls[:, 1, :], lg[:, :, :], AX.X, ALU.add).then_inc(*VEC_C.tick("sum"))
                dve.wait_ge(*VEC_C.at(i, "sum"))
                V.reciprocal(ls[:, 1, :], ls[:, 1, :]).then_inc(*VEC_C.tick("inv"))
                dve.wait_ge(*VEC_C.at(i, "inv"))
                TT(lg[:, :, :], lg[:, :, :], ls[:, 1, :].unsqueeze(2).broadcast_to([P, n, KEXP]), ALU.mult)\
                    .then_inc(*VEC_C.tick("weight"))

            def c_split(i):
                dve.wait_ge(*ACT_C.at(i, "whigh"))
                if not isinstance(i, int) or i > 0:
                    dve.wait_ge(*PE_C.at(i - 1, "w", NJ - 1))
                TT(wpair[32:32 + 2 * KEXP, :], ps[0:2 * KEXP, BANK_C[("wT",)], :],
                   wpair[0:2 * KEXP, :].bitcast(F32), ALU.subtract).then_inc(*VEC_C.tick("wlow"))

            def c_prod(i, j):
                dve.wait_ge(*ACT_C.at(i, "c", j))
                dve.wait_ge(*PE_C.at(i, "w", j))
                TT(cs[:, j % 2, :], cs[:, j % 2, :], ps[:, BANK_C[("w", j)], :], ALU.mult).then_inc(*VEC_C.tick("cw", j))
                dve.wait_ge(*VEC_C.at(i, "cw", j))
                dve.wait_ge(*PE_C.at(i, "x", j))
                if j == 4 and (not isinstance(i, int) or i > 0):
                    dve.wait_ge(stored, 16 * i)
                TT(prod[:, j, :], cs[:, j % 2, :], ps[:, BANK_C[("x", j)], :], ALU.mult)\
                    .then_inc(*VEC_C.tick("prod", j))

            def c_finish(i):
                for n in range(2):
                    dve.wait_ge(*PE_C.at(i, "out", n))
                    for q in range(2):
                        o = x2[:, 2 * n + q, :]
                        ins = STT(o, ps[:, BANK_C[("out", n)], q * D:(q + 1) * D], rn[:, q:q + 1], o, ALU.mult, ALU.add)
                    ins.then_inc(*VEC_C.tick("res", n))
                layer_norm(i, 2, x2, xs_c, VEC_C, POOL_C)

            def turn(a, b, c):
                if a is not None:
                    for h in range(2):
                        for tap in (2, 1, 0):
                            a_tap(a, 4 + h, tap)
                        a_exponent(a, h)
                        for tap in (2, 1, 0):
                            a_tap(a, h, tap)
                        if h == 0:
                            a_fraction(a, 0)
                            a_fraction(a, 1)
                        a_poly(a, h)
                        a_den(a, h)
                    for j in (2, 3):
                        for tap in (2, 1, 0):
                            a_tap(a, j, tap)
                if b is not None:
                    b_products(b)
                if c is not None:
                    c_cum(c)
                    c_softmax(c)
                    c_split(c)
                for u in range(UNITS):
                    if b is not None and u == 1:
                        b_topk(b)
                    if b is not None and u == 3:
                        b_apply(b)
                    if a is not None:
                        a_moments(a, u)
                        if u + 2 < UNITS:
                            a_fraction(a, u + 2)
                        a_scan(a, u)
                        if (u - 1) % M and u > 0:
                            a_accumulate(a, u - 1)
                        if u == M + 2:
                            a_heads(a, 0)
                    if c is not None:
                        c_prod(c, u)
                if a is not None:
                    a_accumulate(a, UNITS - 1)
                    a_heads(a, 1)
                if c is not None:
                    c_finish(c)
                if b is not None:
                    b_finish(b)
                if a is not None:
                    a_finish(a)

            turn(0, None, None)
            turn(1, 0, None)
            turn(2, 1, 0)
            with dve.Fori(3, NCHUNK) as i:
                turn(i, i - 1, i - 2)
            turn(None, NCHUNK - 1, NCHUNK - 2)
            turn(None, None, NCHUNK - 1)


SETUP_COL = 15
SETUP_DERIV = 17


def shape_constants():
    c = np.zeros((P, C_END), np.float32)
    p = np.arange(P)
    c[:, C_ID:C_ID + P] = np.eye(P)
    c[:, C_BLK:C_BLK + P] = p[:, None] // HD == p[None, :] // HD
    c[:, C_HM:C_HM + 16] = p[:, None] // HD == np.arange(16)[None, :]
    c[:, C_POS:C_POS + L] = np.arange(L)
    c[:, C_RN] = 1.0 / (p + 1.0)
    c[:, C_RN + 1] = 1.0 / (p + P + 1.0)
    c[:, C_M0] = p > 0
    c[:, C_M0 + 1] = p == 0
    c[0:HD, C_E8:C_E8 + P] = np.arange(HD)[:, None] == p[None, :] % HD
    t, f = np.arange(L)[:, None], np.arange(P)[None, :]
    ang = 2.0 * np.pi * ((t * f) % L) / L
    fwd = np.concatenate([np.cos(ang), np.sin(ang)], 1)
    fwd[:, P] = (-1.0) ** np.arange(L)
    scale = np.where(np.arange(P) == 0, 1.0, 2.0)[:, None] / L
    inv = np.stack([fwd[:, 0:P].T * scale, fwd[:, P:].T * scale])
    e = np.zeros((HEADS, 2, P), np.float32)
    s = np.zeros((32 + 2 * KEXP, NJ, P), np.float32)
    for h in range(2):
        e[:, h, :] = np.arange(HEADS)[:, None] == h * 16 + p[None, :] // HD
    for j in range(NJ):
        for first in (0, 32):
            s[first:first + 2 * KEXP, j, :] = np.arange(2 * KEXP)[:, None] == 2 * j + p[None, :] // R
    return {"consts": c, "dft": fwd.astype(np.float32), "idft": inv.astype(np.float32), "expand": e, "select": s}


_INS = ['x', 'ctx_1024', 'L0_attn_in_proj_w', 'L0_attn_conv_w', 'L0_attn_conv_b', 'L0_attn_theta',
        'L0_attn_decay_slopes', 'L0_attn_anchor_slopes', 'L0_attn_score_scale', 'L0_attn_deriv_logits',
        'L0_attn_norm_scale', 'L0_attn_W_re', 'L0_attn_W_im', 'L0_attn_out_proj_w', 'L0_xattn_Wq',
        'L0_xattn_bq', 'L0_xattn_Wk', 'L0_xattn_bk', 'L0_xattn_Wv', 'L0_xattn_bv', 'L0_xattn_Wo',
        'L0_xattn_bo', 'L0_ffn_W_Q', 'L0_ffn_W_K', 'L0_ffn_W_O', 'L0_ffn_W_inv', 'L0_ffn_V_fwd',
        'L0_ffn_W_fwd', 'L0_ffn_U_fwd', 'L0_ffn_b_fwd', 'L0_ffn_V_inv', 'L0_ffn_W_inv_exp',
        'L0_ffn_U_inv', 'L0_ffn_b_inv', 'L0_ffn_router_w1', 'L0_ffn_router_b1', 'L0_ffn_router_w2',
        'L0_ffn_router_b2', 'L0_ffn_alpha_bi', 'L0_ffn_expert_bias']


def kernel(**inputs):
    import concourse.bacc as _bacc
    from concourse.bass_utils import run_bass_kernel_spmd as _run

    nc = _bacc.Bacc("TRN2", target_bir_lowering=False, num_devices=1)
    arrays, args = {}, []
    given = {name: np.ascontiguousarray(inputs[name]) for name in _INS}
    given['L0_ffn_alpha_bi'] = given['L0_ffn_alpha_bi'].reshape(1)
    given.update(shape_constants())
    for name, a in given.items():
        arrays[f"in_{name}_dram"] = a
        args.append(nc.dram_tensor(f"in_{name}_dram", a.shape, mybir.dt.from_np(a.dtype), kind="ExternalInput").ap())
    args.append(nc.dram_tensor("out_0_dram", (B, L, D), F32, kind="ExternalOutput").ap())
    decoder_kernel(nc, *args)
    r = _run(nc, [arrays], core_ids=[0])
    return r.results[0]["out_0_dram"]
```

```python
import concourse.bass as bass
from concourse import mybir
from contextlib import ExitStack
import math
import numpy as np

F32 = mybir.dt.float32
F32R = mybir.dt.float32r
I32 = mybir.dt.int32
ALU = mybir.AluOpType
ACT = mybir.ActivationFunctionType
AX = mybir.AxisListType

P = 128
B, L, D = 16, 256, 256
AT_CORR, AT_TOPK, AT_WEIGHTS, AT_APPLY, AT_BACK = 2, 3, 5, 5, 7
SEQ = 2
T = SEQ * L
NCHUNK = B // SEQ
NQ = T // P
DT = D // P
HEADS, HD, M, ANCHORS, TAPS = 32, 8, 4, 4, 4
NZ = 6
XH, XD = 16, 16
TOPK = int(math.log(L + 1))
KEXP, R = 8, 64
NJ = 2 * KEXP * R // P
UNITS = 2 * M
EPS = 1e-5

C_ID, C_BLK, C_HM, C_POS, C_RN, C_M0, C_E8, C_END = 0, 128, 256, 272, 528, 530, 532, 660


class Steps:

    def __init__(self, prefix, names):
        self.prefix, self.order = prefix, {}
        for n in names:
            kind, *which = n if isinstance(n, tuple) else (n,)
            self.order.setdefault(kind, []).append(tuple(which))

    def semaphores(self, sem):
        self.sem = {kind: sem(f"{self.prefix}_{kind}") for kind in self.order}
        self.next = dict.fromkeys(self.order, 0)

    def tick(self, kind, *which):
        order = self.order[kind]
        assert order[self.next[kind] % len(order)] == which, (self.prefix, kind, which)
        self.next[kind] += 1
        return self.sem[kind], 1

    def at(self, i, kind, *which):
        order = self.order[kind]
        return self.sem[kind], i * len(order) + order.index(which) + 1


def each(kinds, over):
    return [(kind, n) for n in over for kind in kinds.split()]


LAYER_NORM = each("res", range(2)) + each("stats aggr norm", range(NQ))

Z_ORDER = [4, 0, 5, 1, 2, 3]
PE_A = Steps("pe_a", each("xT", range(2)) + each("z", Z_ORDER) + each("y", range(UNITS)) + each("S out", range(2)))
VEC_A = Steps("vec_a", [("tap", j, t) for j in Z_ORDER for t in (2, 1, 0)]
              + each("clip expo p1 p2 g den guard w gf y", range(2)) + each("turns frac im re scan", range(UNITS)) + LAYER_NORM)
ACT_A = Steps("act_a", each("xT exp silu e ln f", range(2)) + each("z", Z_ORDER)
              + each("half cos sin sq", range(UNITS)))
POOL_A = Steps("pool_a", ["var", "rstd"] + [("acc", u) for u in range(UNITS) if u % M] + each("both", range(2)))

SPEC = ["qa", "qb", "ka", "kb", "va", "vb"]
PE_B = Steps("pe_b", each("xf cf ot out", range(2)) + SPEC + ["corr", "wt", "wf"])
ACT_B = Steps("act_b", each("xf cf ot", range(2)) + SPEC + ["exp", "wt"])
POOL_B = Steps("pool_b", ["res", "bq", "bk", "bv", "var", "rstd"])
VEC_B = Steps("vec_b", ["aabb", "ab", "ba", "heads", "ca", "cb0", "cb1", "cb2", "corr", "top", "negmax",
                        "above", "equal", "order", "first", "also", "keep", "weight", "inv", "wn",
                        "w1", "w2", "w4", "w3a", "w3", "oa", "ob", "o"] + LAYER_NORM)

PE_C = Steps("pe_c", each("xT out", range(2)) + each("h", range(4)) + ["logit", "wT"] + each("w c x", range(NJ)))
ACT_C = Steps("act_c", each("xT", range(2)) + each("h", range(4)) + ["exp", "whigh", "wT"] + each("c", range(NJ)))
POOL_C = Steps("pool_c", ["var", "rstd"])
VEC_C = Steps("vec_c", ["cum", "logit", "max", "sub", "sum", "inv", "weight", "wlow"]
              + each("cw prod", range(NJ)) + LAYER_NORM)

BANK_A = {("xT", 0): 2, ("xT", 1): 1, ("z", 4): 2, ("z", 0): 1, ("z", 5): 2, ("out", 0): 0, ("out", 1): 0,
          ("z", 1): 1, ("z", 2): 2, ("z", 3): 0, ("Y", 0): 2, ("Y", 1): 0, ("S", 0): 1, ("S", 1): 1}
BANK_B = {("cf", 0): 3, ("cf", 1): 4, ("xf", 0): 3, ("xf", 1): 4, ("qa",): 3, ("qb",): 4, ("ka",): 3,
          ("kb",): 4, ("va",): 3, ("vb",): 4, ("corr",): 3, ("wt",): 4, ("wf",): 3, ("ot", 0): 4,
          ("ot", 1): 3, ("out", 0): 4, ("out", 1): 3}
BANK_C = {("xT", 0): 5, ("xT", 1): 6, ("h", 0): 7, ("h", 1): 5, ("h", 2): 6, ("h", 3): 7, ("logit",): 7,
          ("wT",): 7}
for _j in range(NJ):
    BANK_C.update({("c", _j): 5, ("x", _j): 6, ("w", _j): 7})
BANK_C.update({("out", 0): 5, ("out", 1): 7})


def before(banks, i, group):
    order = list(banks)
    mine = [g for g in order if banks[g] == banks[group]]
    n = mine.index(group)
    late = lambda g: 1 if banks is BANK_A and g[0] == "out" else 0
    chunk = i + late(group) - late(mine[n - 1]) - (n == 0) if n == 0 or late(group) != late(mine[n - 1]) else i
    return (None if isinstance(chunk, int) and chunk < 0 else mine[n - 1]), chunk


def is_first(i):
    return isinstance(i, int) and i == 0


def decoder_kernel(nc, x, ctx_in, in_proj, conv_w, conv_b, theta, decay, anchor, score, deriv, norm_sc,
                   w_re, w_im, out_proj, wq, bq, wk, bk, wv, bv, wo, bo, f_q, f_k, f_o, f_inv, v_fwd,
                   w_fwd, u_fwd, b_fwd, v_inv, w_inv, u_inv, b_inv, r_w1, r_b1, r_w2, r_b2, alpha, ebias,
                   consts, dft, idft, expand, select, out):
    ctx = ExitStack()
    with ctx:
        def sb(name, shape, dt=F32):
            return ctx.enter_context(nc.sbuf_tensor(name, shape, dt))

        def sem(name):
            return ctx.enter_context(nc.semaphore(name))

        ctx.enter_context(nc.allow_non_contiguous_dma("small weights, once"))
        cst = sb("cst", [P, C_END])
        ident = cst[:, C_ID:C_ID + P]
        blk = cst[:, C_BLK:C_BLK + P]
        headm = cst[:, C_HM:C_HM + 16]
        pos = cst[:, C_POS:C_POS + L]
        rn = cst[:, C_RN:C_RN + 2]
        m0, m1 = cst[:, C_M0:C_M0 + 1], cst[:, C_M0 + 1:C_M0 + 2]
        e8 = cst[0:HD, C_E8:C_E8 + P]
        sel = sb("sel", [32 + 2 * KEXP, NJ, P], F32R)
        win = sb("win", [P, DT, NZ * P])
        wopj = sb("wopj", [P, DT, D])
        mask = sb("mask", [P, 2 * T], mybir.dt.bfloat16)
        cw = sb("cw", [P, NZ, TAPS])
        cb = sb("cb", [P, NZ])
        thn = sb("thn", [P, 2, M])
        ss = sb("ss", [P, 2])
        lt = sb("lt", [P, 2, L])
        dw = sb("dw", [P, 4])
        wy = sb("wy", [P, 2, M, P])
        wqs, wks, wvs, wos = (sb(n, [P, DT, D]) for n in ("wqs", "wks", "wvs", "wos"))
        bos = sb("bos", [P, D])
        bqkv = sb("bqkv", [1, 3, D])
        fdft = sb("fdft", [P, 2, L])
        fidft = sb("fidft", [P, 2, L])
        mv = sb("mv", [P, DT, 2, KEXP * R])
        mw = sb("mw", [P, DT, 2, KEXP * R])
        mr = sb("mr", [P, DT, 2, D])
        up = sb("up", [P, NJ, D])
        bp = sb("bp", [2 * KEXP, D])
        w2t = sb("w2t", [P, DT, KEXP])
        rb1 = sb("rb1", [P, DT])
        rb2 = sb("rb2", [P, 2, KEXP])
        acol = sb("acol", [P, 2])
        half_ = sb("half_", [P, NQ])
        eps_ = sb("eps_", [P, NQ])
        seen = sb("seen", [P, 3])
        xa = sb("xa", [P, NQ, D])
        xt = sb("xt", [P, DT, T])
        zc = sb("zc", [P, NZ, T])
        g = sb("g", [P, 2, T])
        frac = sb("frac", [P, 2, T])
        hq = sb("hq", [P, 2, T])
        kturn = hq[:, :, :].bitcast(I32)
        den = zc[:, 4:6, :]
        sc = sb("sc", [P, 4, 2, T])
        sq = sb("sq", [P, 2, 2, T])
        acc = sb("acc", [P, 2, 2, T])
        xs_a = sb("xs_a", [P, NQ, D])
        x1 = sb("x1", [P, NQ, D])
        cin = sb("cin", [P, NQ, D])
        spec = sb("spec", [P, 4, T])
        qkv = sb("qkv", [P, 6, T])
        x2 = sb("x2", [P, NQ, D])
        BH = SEQ * XH
        rsum = sb("rsum", [P, 4, BH])
        cspec = sb("cspec", [P, 4, BH])
        cor = sb("cor", [BH, 5, L])
        sm = sb("sm", [BH, 16])
        wtt = sb("wtt", [P, 2, BH])
        wspec = sb("wspec", [P, 4, BH])
        x2t = sb("x2t", [P, DT, T])
        cum = sb("cum", [P, DT, T])
        prod = sb("prod", [P, NJ, T])
        hT = prod[:, 0:4, :]
        xs_c = prod[:, 4:6, :].rearrange("p t (h d) -> p (t h) d", d=D)
        lg = sb("lg", [P, NQ * 2, KEXP])
        ls = sb("ls", [P, 2, NQ * 2])
        wT = sb("wT", [2 * KEXP, T])
        wpair = sb("wpair", [32 + 2 * KEXP, T], F32R)
        cs = sb("cs", [P, 2, T])
        st = [sb(f"st{n}", [P, NQ, 6]) for n in "abc"]
        mvr = [sb(f"mvr{n}", [P, NQ, 2]) for n in "abc"]
        rs = [sb(f"rs{n}", [P, 2, NQ]) for n in "abc"]
        fq = spec[:, 0, :].rearrange("p (t n) -> p t n", t=DT)
        fk = spec[:, 1, :].rearrange("p (t n) -> p t n", t=DT)
        fo = spec[:, 2, :].rearrange("p (t n) -> p t n", t=DT)
        fi = spec[:, 3, :].rearrange("p (t n) -> p t n", t=DT)
        raw_v = [prod[:, 2 * n:2 * n + 2, :] for n in range(4)]
        raw_u = [qkv[:, 2 * n:2 * n + 2, :] for n in range(2)]
        fr = qkv[:, 4, :].rearrange("p (t n) -> p t n", t=DT)
        fot = qkv[:, 5, :].rearrange("p (t n) -> p t n", t=DT)
        fit = x2t[:, 0, :].rearrange("p (t n) -> p t n", t=DT)
        frt = x2t[:, 1, :].rearrange("p (t n) -> p t n", t=DT)
        nqt = cum[:, 0, :].rearrange("p (t n) -> p t n", t=DT)
        nkt = cum[:, 1, :].rearrange("p (t n) -> p t n", t=DT)
        rw2 = x2[0:KEXP, 0, :]
        selraw = cs[0:32 + 2 * KEXP, :, :].rearrange("p a (b n) -> p (a b) n", n=P)
        b16 = x2[0:2 * KEXP, 1, :]
        bt = x2[:, 2, 0:DT * 2 * KEXP].rearrange("p (t n) -> p t n", t=DT)
        e32 = x2[0:HEADS, 3, :].rearrange("p (h n) -> p h n", h=2)
        c32 = x1[0:HEADS, 0, 0:8]
        c32t = x1[0:HEADS, 1, 0:16]
        y8 = x1[0:HD, 2, 0:2 * M * HD].rearrange("p (c m n) -> p c m n", c=2, m=M)
        y8s = x1[0:HD, 3, 0:2 * M * HD].rearrange("p (c m n) -> p c m n", c=2, m=M)
        n8 = x1[0:HD, 3, 64:64 + 2 * M].rearrange("p (c m) -> p c m", c=2)
        col7 = x1[:, 1, 32:48].rearrange("p (a b) -> p a b", a=2)
        ybase = x1[:, 2, 64:64 + 2 * M * HD]
        dl = x1[:, 1, 64:72]
        lns = x1[:, 1, 80:84]

        ps = ctx.enter_context(nc.psum_tensor("ps", [P, 8, T], F32))

        for steps in (PE_A, ACT_A, VEC_A, POOL_A, PE_B, ACT_B, VEC_B, POOL_B, PE_C, ACT_C, VEC_C, POOL_C):
            steps.semaphores(sem)
        xa_in, xr_in, ctx_loaded, stored = (sem(n) for n in ("xa_in", "xr_in", "ctx_loaded", "stored"))
        w_small, w_attn, w_x, w_raw = (sem(n) for n in ("w_small", "w_attn", "w_x", "w_raw"))
        pe_s, vec_s, act_s, chain = (sem(n) for n in ("pe_s", "vec_s", "act_s", "chain"))
        ready = sem("ready")
        made, folded = sem("made"), sem("folded")
        block = ctx.enter_context(nc.Block())

        def tok(ap, i):
            return ap[i * SEQ:(i + 1) * SEQ] if isinstance(i, int) else ap[bass.ds(i * SEQ, SEQ)]

        def rows(ap, i):
            return tok(ap, i).rearrange("b (h p) d -> p (b h) d", p=P)

        def bb(ap, shape):
            return ap.broadcast_to(shape)

        LOADS_S, LOADS_A, LOADS_X, LOADS_RAW = [], [], [], []
        LOADS_S += [(cst[:, :], consts), (e32[:, :, :], expand)]
        LOADS_A += [(win[:, :, 0:2 * D], in_proj[:, 0:2 * D].rearrange("(t p) n -> p t n", p=P)),
                    (g[:, 0, 0:DT * HEADS].rearrange("p (t n) -> p t n", t=DT),
                     in_proj[:, 2 * D:2 * D + HEADS].rearrange("(t p) n -> p t n", p=P))]
        for j in range(4):
            LOADS_A += [(cw[:, j, :], conv_w[:, 0, j * P:(j + 1) * P].rearrange("a p -> p a"))]
        LOADS_A += [(cb[:, 0:4], conv_b[0:2 * D].rearrange("(t p) -> p t", p=P)),
                    (thn[:, :, :], theta[0, 0].rearrange("(t k) h m -> (k h) t m", t=2)),
                    ]
        LOADS_S += [(c32[:, 0:4], conv_w[:, 0, 2 * D:].rearrange("a p -> p a")),
                    (c32[:, 4:5], conv_b[2 * D:].rearrange("(p a) -> p a", a=1)),
                    (c32[:, 5:6], score.rearrange("(p a) -> p a", a=1)),
                    (c32[0:HEADS - ANCHORS, 6:7], decay.rearrange("(p a) -> p a", a=1)),
                    (c32[HEADS - ANCHORS:HEADS, 6:7], anchor.rearrange("(p a) -> p a", a=1)),
                    (y8[:, 0, :, :], w_re.rearrange("(h m) n -> h m n", m=M)),
                    (y8[:, 1, :, :], w_im.rearrange("(h m) n -> h m n", m=M)),
                    (n8[:, :, :], norm_sc.rearrange("(c h m) -> h c m", c=2, m=M)),
                    (dl[:, 0:3], deriv.rearrange("(a n) -> a n", a=1).broadcast_to([P, 3]))]
        for dst, src in ((wqs, wq), (wks, wk), (wvs, wv), (wos, wo)):
            LOADS_X += [(dst[:, :, :], src.rearrange("(t p) n -> p t n", p=P))]
        LOADS_X += [(wopj[:, :, :], out_proj.rearrange("(t p) n -> p t n", p=P)),
                    (fdft[:, :, :], dft.rearrange("(t p) n -> p t n", p=P)),
                    (fidft[:, :, :], idft.rearrange("t p n -> p t n")),
                    (bos[:, :], bo.rearrange("(a n) -> a n", a=1).broadcast_to([P, D]))]
        for n, src in enumerate((bq, bk, bv)):
            LOADS_X += [(bqkv[:, n, :], src.rearrange("(a n) -> a n", a=1))]
        for dst, src in ((fq, f_q), (fk, f_k), (fo, f_o), (fi, f_inv), (fr, r_w1)):
            LOADS_RAW += [(dst, src.rearrange("(t p) n -> p t n", p=P))]
        for dst, src in list(zip(raw_v, (v_fwd, w_fwd, w_inv, v_inv))) + list(zip(raw_u, (u_fwd, u_inv))):
            for t in range(DT):
                LOADS_RAW += [(dst[:, t, :].rearrange("p (k r) -> p k r", k=KEXP),
                               src[:, t * P:(t + 1) * P, :].rearrange("k p r -> p k r"))]
        LOADS_RAW += [(rw2, r_w2), (b16[0:KEXP, :], b_fwd), (b16[KEXP:2 * KEXP, :], b_inv),
                      (selraw, select), (rb1[:, :], r_b1.rearrange("(t p) -> p t", p=P)),
                      (rb2[:, 0, :], r_b2.rearrange("(a n) -> a n", a=1).broadcast_to([P, KEXP])),
                      (rb2[:, 1, :], ebias.rearrange("(a n) -> a n", a=1).broadcast_to([P, KEXP])),
                      (acol[:, 0:1], alpha.rearrange("(a n) -> a n", a=1).broadcast_to([P, 1]))]

        @block.sync
        def _(sp):
            for dst, src in LOADS_S:
                sp.dma_start(dst, src).then_inc(w_small, 16)
            for dst, src in LOADS_A[:2]:
                sp.dma_start(dst, src).then_inc(w_attn, 16)
            sp.dma_start(xa[:, :, :], rows(x, 0)).then_inc(xa_in, 16)
            for dst, src in LOADS_A[2:]:
                sp.dma_start(dst, src).then_inc(w_attn, 16)

            def load_x(i):
                if not is_first(i):
                    sp.wait_ge(*PE_A.at(i - 1, "xT", 1))
                sp.dma_start(xa[:, :, :], rows(x, i)).then_inc(xa_in, 16)

            def load_residual(i):
                if not is_first(i):
                    sp.wait_ge(*VEC_A.at(i - 1, "norm", NQ - 1))
                sp.dma_start(xs_a[:, :, :], rows(x, i)).then_inc(xr_in, 16)

            def load_ctx(i):
                if not is_first(i):
                    sp.wait_ge(*PE_B.at(i - 1, "cf", 1))
                sp.dma_start(cin[:, :, :], rows(ctx_in, i)).then_inc(ctx_loaded, 16)

            def store(i):
                sp.wait_ge(*VEC_C.at(i, "norm", NQ - 1))
                sp.dma_start(rows(out, i), xs_c[:, :, :]).then_inc(stored, 16)

            load_residual(0)
            for dst, src in LOADS_X:
                sp.dma_start(dst, src).then_inc(w_x, 16)
            load_ctx(0)
            for dst, src in LOADS_RAW:
                sp.dma_start(dst, src).then_inc(w_raw, 16)
            load_x(1)
            load_x(2)
            load_residual(1)
            load_ctx(1)
            load_x(3)
            load_residual(2)
            load_ctx(2)
            with sp.Fori(3, NCHUNK - 1) as i:
                load_x(i + 1)
                load_residual(i)
                store(i - 3)
                load_ctx(i)
            load_residual(NCHUNK - 1)
            store(NCHUNK - 4)
            load_ctx(NCHUNK - 1)
            store(NCHUNK - 3)
            store(NCHUNK - 2)
            store(NCHUNK - 1)
            sp.wait_ge(stored, 16 * NCHUNK)

        NS = 0

        SETUP = [("col", 0), ("col", 1), ("y", 0)]
        FOLD = ([(m, t) for m in ("ot", "it", "rt") for t in range(DT)] + [("w2", 0), ("bt", 0)]
                + [(m, t) for m in ("nq", "nk") for t in range(DT)]
                + [(m, br, t) for m in ("mv", "mw", "mr") for br in range(2) for t in range(DT)]
                + [("up", j) for j in range(NJ)] + [("bp", 0)])
        FOLD_BANKS = 5
        FOLD_EARLY = 20
        FOLD_STEP = -(-(len(FOLD) - FOLD_EARLY) // UNITS)

        def fold_part(u):
            if u is None:
                return range(FOLD_EARLY)
            return range(FOLD_EARLY + u * FOLD_STEP, min(FOLD_EARLY + (u + 1) * FOLD_STEP, len(FOLD)))

        def fold_bank(name):
            return 3 + FOLD.index(name) % FOLD_BANKS

        @block.tensor
        def _(pe):
            mm = nc.tensor.matmul

            pe.wait_ge(w_small, 16 * len(LOADS_S))
            pe.wait_ge(chain, SETUP_COL)
            for h in range(2):
                mm(ps[:, h, 0:8], e32[:, h, :], c32t[:, 0:8], start=True, stop=True).then_inc(pe_s, 1)
            mm(ps[:, 2, 0:2 * M * HD], e8, y8s.rearrange("p c m n -> p (c m n)"), start=True, stop=True)\
                .then_inc(pe_s, 1)
            pe.wait_ge(ready, 1)

            def product(dst, lhs, rhs):
                for t in range(DT):
                    last = mm(dst, lhs(t), rhs(t), start=(t == 0), stop=(t == DT - 1))
                return last

            def fold(k):
                name, o = FOLD[k], ps[:, fold_bank(FOLD[k]), :]
                kind, t = name[0], name[-1]
                if k == 0:
                    pe.wait_ge(w_raw, 16 * len(LOADS_RAW))
                if k >= FOLD_BANKS:
                    pe.wait_ge(folded, k - FOLD_BANKS + 1)
                if kind in ("ot", "it", "rt"):
                    src = {"ot": fo, "it": fi, "rt": fr}[kind]
                    for r in range(DT):
                        last = nc.tensor.transpose(o[:, r * P:(r + 1) * P], src[:, r, t * P:(t + 1) * P], ident)
                elif kind == "w2":
                    for r in range(DT):
                        last = nc.tensor.transpose(o[:, r * KEXP:(r + 1) * KEXP], rw2[:, r * P:(r + 1) * P],
                                                   ident[0:KEXP, 0:KEXP])
                elif kind == "bt":
                    for r in range(DT):
                        last = nc.tensor.transpose(o[:, r * 16:(r + 1) * 16], b16[:, r * P:(r + 1) * P],
                                                   ident[0:16, 0:16])
                elif kind in ("nq", "nk"):
                    if name == ("nq", 0):
                        pe.wait_ge(folded, FOLD.index(("it", 1)) + 1)
                    w = fq if kind == "nq" else fk
                    last = product(o[:, 0:D], lambda r: fit[:, r, t * P:(t + 1) * P], lambda r: w[:, r, :])
                elif kind in ("mv", "mw", "mr"):
                    br = name[1]
                    if name == ("mv", 1, 0):
                        pe.wait_ge(folded, FOLD.index(("nk", 1)) + 1)
                    lhs, rhs = {"mv": ((fq, nqt), (raw_v[0], raw_v[2])), "mw": ((fk, nkt), (raw_v[1], raw_v[3])),
                                "mr": ((fq, nqt), (frt, frt))}[kind]
                    last = product(o[:, 0:D if kind == "mr" else KEXP * R],
                                   lambda r: lhs[br][:, r, t * P:(t + 1) * P], lambda r: rhs[br][:, r, :])
                elif kind == "up":
                    u, c = raw_u[t // 4], (t % 4) * P
                    last = product(o[:, 0:D], lambda r: u[:, r, c:c + P], lambda r: fot[:, r, :])
                else:
                    last = product(o[0:16, 0:D], lambda r: bt[:, r, :], lambda r: fot[:, r, :])
                last.then_inc(made, 1)

            def free_a(i, *name):
                prev, i = before(BANK_A, i, name)
                if prev is None:
                    return ps[:, BANK_A[name], :]
                kind, n = prev
                if kind == "xT":
                    pe.wait_ge(*ACT_A.at(i, "xT", n))
                elif kind == "z":
                    pe.wait_ge(*VEC_A.at(i, "tap", n, 0))
                elif kind == "S":
                    pe.wait_ge(*VEC_A.at(i, "w", n))
                elif kind == "Y":
                    pe.wait_ge(*VEC_A.at(i, "y", n))
                else:
                    pe.wait_ge(*VEC_A.at(i, "res", n))
                return ps[:, BANK_A[name], :]

            def free_b(i, *name):
                prev, i = before(BANK_B, i, name)
                if prev is None:
                    return ps[:, BANK_B[name], :]
                if prev[0] in ("corr", "out"):
                    pe.wait_ge(*VEC_B.at(i, *(prev if prev[0] == "corr" else ("res", prev[1]))))
                elif prev[0] == "wf":
                    pe.wait_ge(*VEC_B.at(i, "w3"))
                else:
                    pe.wait_ge(*ACT_B.at(i, *prev))
                return ps[:, BANK_B[name], :]

            def free_c(i, *name):
                prev, i = before(BANK_C, i, name)
                if prev is None:
                    return ps[:, BANK_C[name], :]
                if prev[0] == "logit":
                    pe.wait_ge(*VEC_C.at(i, "logit"))
                elif prev[0] == "wT":
                    pe.wait_ge(*VEC_C.at(i, "wlow"))
                elif prev[0] == "w":
                    pe.wait_ge(*VEC_C.at(i, "cw", prev[1]))
                elif prev[0] == "x":
                    pe.wait_ge(*VEC_C.at(i, "prod", prev[1]))
                elif prev[0] == "out":
                    pe.wait_ge(*VEC_C.at(i, "res", prev[1]))
                else:
                    pe.wait_ge(*ACT_C.at(i, *prev))
                return ps[:, BANK_C[name], :]

            def a_transpose(i):
                pe.wait_ge(xa_in, 16 * i + 16)
                for t in range(DT):
                    o = free_a(i, "xT", t)
                    for q in range(NQ):
                        last = nc.tensor.transpose(o[:, q * P:(q + 1) * P], xa[:, q, t * P:(t + 1) * P], ident)
                    last.then_inc(*PE_A.tick("xT", t))

            def a_project(i, j):
                o = free_a(i, "z", j)
                pe.wait_ge(*ACT_A.at(i, "xT", 1))
                for t in range(DT):
                    last = mm(o, win[:, t, j * P:(j + 1) * P], xt[:, t, :], start=(t == 0), stop=(t == DT - 1))
                last.then_inc(*PE_A.tick("z", j))

            def a_sums(i, u):
                h, m = divmod(u, M)
                if m == 0:
                    free_a(i, "Y", h)
                y = ps[:, BANK_A[("Y", h)], :]
                pe.wait_ge(*VEC_A.at(i, "scan", u))
                for c in range(2):
                    last = mm(y, wy[:, 1 - c, m, :], sc[:, u % 4, c, :], start=(m == 0 and c == 0),
                              stop=(m == M - 1 and c == 1))
                last.then_inc(*PE_A.tick("y", u))

            def a_squares(i, h):
                o = free_a(i, "S", h)
                pe.wait_ge(*POOL_A.at(i, "both", h))
                mm(o, blk, acc[:, h, 0, :], start=True, stop=True).then_inc(*PE_A.tick("S", h))

            def a_out(i, n):
                pe.wait_ge(*VEC_A.at(i, "y", 1))
                o = free_a(i, "out", n)
                for q in range(2 * n, 2 * n + 2):
                    for t in range(DT):
                        last = mm(o[:, (q % 2) * D:(q % 2 + 1) * D], zc[:, 2 + t, q * P:(q + 1) * P],
                                  wopj[:, t, :], start=(t == 0), stop=(t == DT - 1))
                last.then_inc(*PE_A.tick("out", n))

            def b_transforms(i):
                for name, src in (("cf", cin), ("xf", x1)):
                    if name == "cf":
                        pe.wait_ge(ctx_loaded, 16 * i + 16)
                    else:
                        pe.wait_ge(*VEC_A.at(i, "norm", NQ - 1))
                    for t in range(DT):
                        o = free_b(i, name, t)
                        for b in range(SEQ):
                            for h in range(2):
                                last = mm(o[:, b * L:(b + 1) * L], src[:, 2 * b + h, t * P:(t + 1) * P],
                                          fdft[:, h, :], start=(h == 0), stop=(h == 1))
                        last.then_inc(*PE_B.tick(name, t))

            def b_spectra(i, names):
                for name in names:
                    k = SPEC.index(name)
                    o = free_b(i, name)
                    first = 0 if name[0] == "q" else 2
                    w = {"q": wqs, "k": wks, "v": wvs}[name[0]]
                    pe.wait_ge(*ACT_B.at(i, "xf" if first == 0 else "cf", 1))
                    for b in range(SEQ):
                        for t in range(DT):
                            c = b * L + (k % 2) * P
                            last = mm(o[:, b * D:(b + 1) * D], spec[:, first + t, c:c + P], w[:, t, :],
                                      start=(t == 0), stop=(t == DT - 1))
                    last.then_inc(*PE_B.tick(name))

            def b_corr(i):
                o = free_b(i, "corr")
                pe.wait_ge(*VEC_B.at(i, "cb2"))
                for part in range(2):
                    last = mm(o[0:BH, 0:L], cspec[:, part, :], fidft[:, part, :], start=(part == 0), stop=(part == 1))
                last.then_inc(*PE_B.tick("corr"))

            def b_weights(i):
                o = free_b(i, "wt")
                pe.wait_ge(*VEC_B.at(i, "wn"))
                for h in range(2):
                    last = mm(o[:, h * BH:(h + 1) * BH], cor[:, 0, h * P:(h + 1) * P], ident[0:BH, 0:BH],
                              start=True, stop=True)
                last.then_inc(*PE_B.tick("wt"))
                o = free_b(i, "wf")
                pe.wait_ge(*ACT_B.at(i, "wt"))
                for part in range(2):
                    for h in range(2):
                        last = mm(o[:, part * BH:(part + 1) * BH], fdft[:, h, part * P:(part + 1) * P], wtt[:, h, :],
                                  start=(h == 0), stop=(h == 1))
                last.then_inc(*PE_B.tick("wf"))

            def b_back(i):
                for t in range(DT):
                    o = free_b(i, "ot", t)
                    pe.wait_ge(*VEC_B.at(i, "o"))
                    for b in range(SEQ):
                        for part in range(2):
                            c = b * D + t * P
                            last = mm(o[:, b * L:(b + 1) * L], qkv[:, part, c:c + P], fidft[:, part, :],
                                      start=(part == 0), stop=(part == 1))
                    last.then_inc(*PE_B.tick("ot", t))

            def b_out(i):
                for n in range(2):
                    o = free_b(i, "out", n)
                    pe.wait_ge(*ACT_B.at(i, "ot", 1))
                    for q in range(2 * n, 2 * n + 2):
                        for t in range(DT):
                            last = mm(o[:, (q % 2) * D:(q % 2 + 1) * D], spec[:, t, q * P:(q + 1) * P],
                                      wos[:, t, :], start=(t == 0), stop=(t == DT - 1))
                    last.then_inc(*PE_B.tick("out", n))

            def c_router(i):
                pe.wait_ge(*VEC_B.at(i, "norm", NQ - 1))
                for t in range(DT):
                    o = free_c(i, "xT", t)
                    for q in range(NQ):
                        last = nc.tensor.transpose(o[:, q * P:(q + 1) * P], x2[:, q, t * P:(t + 1) * P], ident)
                    last.then_inc(*PE_C.tick("xT", t))
                for n in range(4):
                    br, r = divmod(n, 2)
                    o = free_c(i, "h", n)
                    pe.wait_ge(*ACT_C.at(i, "xT", 1))
                    for t in range(DT):
                        last = mm(o, mr[:, t, br, r * P:(r + 1) * P], x2t[:, t, :], start=(t == 0), stop=(t == 1))
                    last.then_inc(*PE_C.tick("h", n))

            def c_logits(i):
                o = free_c(i, "logit")
                pe.wait_ge(*ACT_C.at(i, "h", 3))
                for q in range(NQ):
                    for br in range(2):
                        c = (q * 2 + br) * KEXP
                        for r in range(DT):
                            last = mm(o[:, c:c + KEXP], hT[:, 2 * br + r, q * P:(q + 1) * P], w2t[:, r, :],
                                      start=(r == 0), stop=(r == 1))
                last.then_inc(*PE_C.tick("logit"))

            def c_weights(i):
                o = free_c(i, "wT")
                pe.wait_ge(*VEC_C.at(i, "weight"))
                for q in range(NQ):
                    last = nc.tensor.transpose(o[0:16, q * P:(q + 1) * P],
                                               lg[:, 2 * q:2 * q + 2, :].rearrange("p a b -> p (a b)"), ident)
                last.then_inc(*PE_C.tick("wT"))

            def c_running(i, j):
                br, c = j // 4, (j % 4) * P
                o = free_c(i, "c", j)
                pe.wait_ge(*VEC_C.at(i, "cum"))
                for t in range(DT):
                    last = mm(o, mw[:, t, br, c:c + P], cum[:, t, :], start=(t == 0), stop=(t == 1))
                last.then_inc(*PE_C.tick("c", j))

            def c_own(i, j):
                br, c = j // 4, (j % 4) * P
                o = free_c(i, "x", j)
                for t in range(DT):
                    last = mm(o, mv[:, t, br, c:c + P], x2t[:, t, :], start=(t == 0), stop=(t == 1))
                last.then_inc(*PE_C.tick("x", j))

            def c_spread(i, j):
                o = free_c(i, "w", j)
                pe.wait_ge(*VEC_C.at(i, "wlow"))
                mm(o, sel[:, j, :], wpair[:, :], start=True, stop=True).then_inc(*PE_C.tick("w", j))

            def c_out(i, n):
                o = free_c(i, "out", n)
                pe.wait_ge(*VEC_C.at(i, "prod", NJ - 1))
                for q in range(2 * n, 2 * n + 2):
                    d = o[:, (q % 2) * D:(q % 2 + 1) * D]
                    for j in range(NJ):
                        mm(d, prod[:, j, q * P:(q + 1) * P], up[:, j, :], start=(j == 0), stop=False)
                    last = mm(d, wT[:, q * P:(q + 1) * P], bp[:, :], start=False, stop=True)
                last.then_inc(*PE_C.tick("out", n))

            def turn(a, b, c, d):
                if a is not None:
                    a_transpose(a)
                if d is not None:
                    c_out(d, 0)
                if a is not None:
                    a_project(a, 4)
                    a_project(a, 0)
                if d is not None:
                    c_out(d, 1)
                if b is not None:
                    a_out(b, 0)
                if a is not None:
                    a_project(a, 5)
                if b is not None:
                    a_out(b, 1)
                if a is not None:
                    a_project(a, 1)
                    a_project(a, 2)
                    a_project(a, 3)
                if is_first(a):
                    for k in fold_part(None):
                        fold(k)
                if c is not None:
                    c_router(c)
                if b is not None:
                    b_transforms(b)
                if c is not None:
                    c_logits(c)
                    c_running(c, 0)
                    c_own(c, 0)
                if b is not None:
                    b_spectra(b, SPEC[0:2])
                if c is not None:
                    c_weights(c)
                if b is not None:
                    b_spectra(b, SPEC[2:4])
                if c is not None:
                    c_spread(c, 0)
                if b is not None:
                    b_spectra(b, SPEC[4:6])
                for u in range(UNITS):
                    if b is not None and u == AT_WEIGHTS:
                        b_weights(b)
                    if b is not None and u == AT_BACK:
                        b_back(b)
                    if c is not None and u > 0:
                        c_running(c, u)
                    if a is not None:
                        a_sums(a, u)
                        if u == M:
                            a_squares(a, 0)
                    if c is not None and u > 0:
                        c_spread(c, u)
                        c_own(c, u)
                    if b is not None and u == AT_CORR:
                        b_corr(b)
                    if is_first(a):
                        for k in fold_part(u):
                            fold(k)
                if a is not None:
                    a_squares(a, 1)
                if b is not None:
                    b_out(b)

            turn(0, None, None, None)
            pe.wait_ge(folded, len(FOLD))
            turn(1, 0, None, None)
            turn(2, 1, 0, None)
            with pe.Fori(3, NCHUNK) as i:
                turn(i, i - 1, i - 2, i - 3)
            turn(None, NCHUNK - 1, NCHUNK - 2, NCHUNK - 3)
            turn(None, None, NCHUNK - 1, NCHUNK - 2)
            turn(None, None, None, NCHUNK - 1)
        @block.scalar
        def _(act):
            A = nc.scalar.activation
            act.wait_ge(chain, 2)
            A(c32t[:, 9:10], c32t[:, 8:9], ACT.Exp).then_inc(act_s, 1)
            act.wait_ge(chain, 3)
            A(c32t[:, 11:12], c32t[:, 10:11], ACT.Ln).then_inc(act_s, 1)
            act.wait_ge(chain, SETUP_DERIV)
            A(dl[:, 4:7], dl[:, 0:3], ACT.Exp).then_inc(act_s, 1)
            act.wait_ge(ready, 1)

            def fold(k):
                name, o = FOLD[k], ps[:, fold_bank(FOLD[k]), :]
                kind, t = name[0], name[-1]
                act.wait_ge(made, k + 1)
                if kind in ("w2", "bt"):
                    w = KEXP if kind == "w2" else 16
                    dst, src = (w2t[:, :, :] if kind == "w2" else bt), o[:, 0:DT * w].rearrange("p (t n) -> p t n", t=DT)
                elif kind in ("mv", "mw", "mr"):
                    w = D if kind == "mr" else KEXP * R
                    dst, src = {"mv": mv, "mw": mw, "mr": mr}[kind][:, t, name[1], :], o[:, 0:w]
                elif kind == "up":
                    dst, src = up[:, t, :], o[:, 0:D]
                elif kind == "bp":
                    dst, src = bp[:, :], o[0:16, 0:D]
                else:
                    dst, src = {"ot": fot, "it": fit, "rt": frt, "nq": nqt, "nk": nkt}[kind][:, t, :], o[:, 0:D]
                if name == ("up", 0):
                    act.wait_ge(ready, 2)
                if kind == "up" and t >= NJ // 2:
                    A(dst, src, ACT.Identity, scale=acol[:, 0:1]).then_inc(folded, 1)
                elif kind == "bp":
                    A(dst, src, ACT.Identity, scale=acol[0:16, 1:2]).then_inc(folded, 1)
                else:
                    A(dst, src, ACT.Copy).then_inc(folded, 1)

            def a_transpose(i):
                for t in range(DT):
                    act.wait_ge(*PE_A.at(i, "xT", t))
                    if t == 0 and not is_first(i):
                        act.wait_ge(*PE_A.at(i - 1, "z", 3))
                    A(xt[:, t, :], ps[:, BANK_A[("xT", t)], :], ACT.Copy).then_inc(*ACT_A.tick("xT", t))

            def a_project(i, j):
                act.wait_ge(*PE_A.at(i, "z", j))
                if not is_first(i):
                    if j in (2, 3):
                        act.wait_ge(*PE_A.at(i - 1, "out", 1))
                    elif j < 2:
                        act.wait_ge(*VEC_A.at(i - 1, "frac", UNITS - 1))
                    else:
                        act.wait_ge(*VEC_A.at(i - 1, "gf", j - 4))
                A(zc[:, j, :], ps[:, BANK_A[("z", j)], :], ACT.Identity, bias=cb[:, j:j + 1],
                  scale=cw[:, j, 3:4]).then_inc(*ACT_A.tick("z", j))

            def a_exp(i, h):
                act.wait_ge(*VEC_A.at(i, "expo", h))
                A(zc[:, 4 + h, :], zc[:, 4 + h, :], ACT.Exp).then_inc(*ACT_A.tick("exp", h))

            def a_gates(i):
                for h in range(2):
                    act.wait_ge(*VEC_A.at(i, "tap", 2 + h, 0))
                    A(zc[:, 2 + h, :], zc[:, 2 + h, :], ACT.Silu).then_inc(*ACT_A.tick("silu", h))

            def a_guard(i):
                for h in range(2):
                    act.wait_ge(*VEC_A.at(i, "guard", h))
                    A(den[:, h, :], den[:, h, :], ACT.Square, scale=math.sqrt(EPS)).then_inc(*ACT_A.tick("e", h))

            def a_angles(i, u):
                act.wait_ge(*VEC_A.at(i, "frac", u))
                if u >= 2:
                    act.wait_ge(*VEC_A.at(i, "re", u - 2))
                elif not is_first(i):
                    act.wait_ge(*VEC_A.at(i - 1, "re", UNITS - 2 + u))
                A(hq[:, u % 2, :], frac[:, u % 2, :], ACT.Sin, scale=math.pi).then_inc(*ACT_A.tick("half", u))
                act.wait_ge(*ACT_A.at(i, "half", u))
                A(hq[:, u % 2, :], hq[:, u % 2, :], ACT.Square, scale=math.sqrt(2.0)).then_inc(*ACT_A.tick("cos", u))
                if u >= 4:
                    pe_i, pe_u = i, u - 4
                else:
                    pe_i, pe_u = i - 1, u + 4
                if u >= 4 or not isinstance(i, int) or i > 0:
                    act.wait_ge(*PE_A.at(pe_i, "y", pe_u))
                A(sc[:, u % 4, 0, :], frac[:, u % 2, :], ACT.Sin, scale=2.0 * math.pi)\
                    .then_inc(*ACT_A.tick("sin", u))

            def a_squares(i, u):
                act.wait_ge(*VEC_A.at(i, "scan", u))
                h, m = divmod(u, M)
                if m == 0:
                    dst = acc[:, h, :, :]
                    if not is_first(i):
                        act.wait_ge(*PE_A.at(i - 1, "S", h))
                else:
                    dst = sq[:, u % 2, :, :]
                    before_it = [v for v in range(UNITS) if v % M and v % 2 == u % 2 and v < u]
                    if before_it:
                        act.wait_ge(*POOL_A.at(i, "acc", before_it[-1]))
                    elif not is_first(i):
                        act.wait_ge(*POOL_A.at(i - 1, "acc", UNITS - 1 if u % 2 else UNITS - 2))
                A(dst, sc[:, u % 4, :, :], ACT.Square, scale=1.0 / math.sqrt(2.0 * HD * M))\
                    .then_inc(*ACT_A.tick("sq", u))

            def a_norm(i, h):
                act.wait_ge(*VEC_A.at(i, "w", h))
                A(den[:, h, :], den[:, h, :], ACT.Ln).then_inc(*ACT_A.tick("ln", h))
                act.wait_ge(*ACT_A.at(i, "ln", h))
                A(den[:, h, :], den[:, h, :], ACT.Exp, scale=-0.5).then_inc(*ACT_A.tick("f", h))

            def b_transforms(i):
                for name, first in (("cf", 2), ("xf", 0)):
                    for t in range(DT):
                        act.wait_ge(*PE_B.at(i, name, t))
                        if t == 0 and name == "cf" and not is_first(i):
                            act.wait_ge(*PE_B.at(i - 1, "out", 1))
                            act.wait_ge(*VEC_B.at(i - 1, "o"))
                        A(spec[:, first + t, :], ps[:, BANK_B[(name, t)], :], ACT.Copy)\
                            .then_inc(*ACT_B.tick(name, t))

            def b_spectra(i, names):
                for name in names:
                    k = SPEC.index(name)
                    act.wait_ge(*PE_B.at(i, name))
                    if k == 0 and not is_first(i):
                        act.wait_ge(*PE_B.at(i - 1, "ot", 1))
                    A(qkv[:, k, :], ps[:, BANK_B[(name,)], :], ACT.Copy).then_inc(*ACT_B.tick(name))

            def b_exp(i):
                act.wait_ge(*VEC_B.at(i, "negmax"))
                A(cor[:, 4, :], cor[:, 0, :], ACT.Exp, bias=sm[:, 8:9]).then_inc(*ACT_B.tick("exp"))

            def b_wt(i):
                act.wait_ge(*PE_B.at(i, "wt"))
                A(wtt[:, :, :], ps[:, BANK_B[("wt",)], 0:2 * BH].rearrange("p (a b) -> p a b", a=2), ACT.Copy)\
                    .then_inc(*ACT_B.tick("wt"))

            def b_back(i):
                for t in range(DT):
                    act.wait_ge(*PE_B.at(i, "ot", t))
                    if t == 0:
                        act.wait_ge(*VEC_B.at(i, "o"))
                    A(spec[:, t, :], ps[:, BANK_B[("ot", t)], :], ACT.Copy).then_inc(*ACT_B.tick("ot", t))

            def c_front(i):
                for t in range(DT):
                    act.wait_ge(*PE_C.at(i, "xT", t))
                    A(x2t[:, t, :], ps[:, BANK_C[("xT", t)], :], ACT.Copy).then_inc(*ACT_C.tick("xT", t))
                for n in range(4):
                    act.wait_ge(*PE_C.at(i, "h", n))
                    if n == 0 and not is_first(i):
                        act.wait_ge(*PE_C.at(i - 1, "out", 1))
                    A(hT[:, n, :], ps[:, BANK_C[("h", n)], :], ACT.Gelu, bias=rb1[:, n % 2:n % 2 + 1])\
                        .then_inc(*ACT_C.tick("h", n))

            def c_exp(i):
                act.wait_ge(*VEC_C.at(i, "sub"))
                A(lg[:, :, :], lg[:, :, :], ACT.Exp).then_inc(*ACT_C.tick("exp"))

            def c_weights(i):
                act.wait_ge(*PE_C.at(i, "wT"))
                A(wT[:, :], ps[0:2 * KEXP, BANK_C[("wT",)], :], ACT.Copy).then_inc(*ACT_C.tick("wT"))
                A(wpair[0:2 * KEXP, :], ps[0:2 * KEXP, BANK_C[("wT",)], :], ACT.Copy).then_inc(*ACT_C.tick("whigh"))

            def c_tile(i, j):
                act.wait_ge(*PE_C.at(i, "c", j))
                if j >= 2:
                    act.wait_ge(*VEC_C.at(i, "prod", j - 2))
                elif not is_first(i):
                    act.wait_ge(*VEC_C.at(i - 1, "prod", NJ - 2 + j))
                A(cs[:, j % 2, :], ps[:, BANK_C[("c", j)], :], ACT.Copy).then_inc(*ACT_C.tick("c", j))

            def turn(a, b, c, d):
                if a is not None:
                    a_transpose(a)
                    a_project(a, 4)
                    a_project(a, 0)
                    a_exp(a, 0)
                    a_project(a, 5)
                    a_exp(a, 1)
                    a_angles(a, 0)
                    a_angles(a, 1)
                    for j in (1, 2, 3):
                        a_project(a, j)
                if is_first(a):
                    for k in fold_part(None):
                        fold(k)
                if c is not None:
                    c_front(c)
                if b is not None:
                    b_transforms(b)
                if a is not None:
                    a_gates(a)
                if a is not None:
                    a_angles(a, 2)
                    a_squares(a, 0)
                if c is not None:
                    c_exp(c)
                    c_tile(c, 0)
                if b is not None:
                    b_spectra(b, SPEC[0:2])
                if c is not None:
                    c_weights(c)
                if b is not None:
                    b_spectra(b, SPEC[2:6])
                if a is not None:
                    a_guard(a)
                    a_angles(a, 3)
                    a_squares(a, 1)
                for u in range(UNITS):
                    if b is not None and u == AT_WEIGHTS:
                        b_wt(b)
                    if b is not None and u == AT_BACK:
                        b_back(b)
                    if c is not None and u > 0:
                        c_tile(c, u)
                    if b is not None and u == AT_TOPK:
                        b_exp(b)
                    if a is not None:
                        if u + 4 < UNITS:
                            a_angles(a, u + 4)
                        if u + 2 < UNITS:
                            a_squares(a, u + 2)
                        if u == M + 1:
                            a_norm(a, 0)
                    if is_first(a):
                        for k in fold_part(u):
                            fold(k)
                if a is not None:
                    a_norm(a, 1)

            turn(0, None, None, None)
            turn(1, 0, None, None)
            turn(2, 1, 0, None)
            with act.Fori(3, NCHUNK) as i:
                turn(i, i - 1, i - 2, i - 3)
            turn(None, NCHUNK - 1, NCHUNK - 2, NCHUNK - 3)
            turn(None, None, NCHUNK - 1, NCHUNK - 2)
            turn(None, None, None, NCHUNK - 1)

        @block.gpsimd
        def _(pool):
            G = nc.gpsimd
            pool.wait_ge(ready, 2)

            def rstd(i, k, VEC, OWN):
                pool.wait_ge(*VEC.at(i, "aggr", NQ - 1))
                G.tensor_tensor(rs[k][:, 0, :], mvr[k][:, :, 1], eps_[:, :], ALU.add)\
                    .then_inc(*OWN.tick("var"))
                pool.wait_ge(*OWN.at(i, "var"))
                G.tensor_tensor(rs[k][:, 1, :], rs[k][:, 0, :], half_[:, :], ALU.pow)\
                    .then_inc(*OWN.tick("rstd"))

            def b_front(i):
                pool.wait_ge(*VEC_A.at(i, "norm", NQ - 1))
                pool.wait_ge(*PE_B.at(i, "xf", 1))
                G.tensor_tensor(x1[:, :, :], x1[:, :, :], bos[:, :].unsqueeze(1).broadcast_to([P, NQ, D]), ALU.add)\
                    .then_inc(*POOL_B.tick("res"))
                for n, name in enumerate(("q", "k", "v")):
                    pool.wait_ge(*ACT_B.at(i, name + "a"))
                    row = qkv[0:1, 2 * n, :].rearrange("p (b d) -> p b d", b=SEQ)
                    G.tensor_tensor(row, row, bqkv[:, n, :].unsqueeze(1).broadcast_to([1, SEQ, D]), ALU.add)\
                        .then_inc(*POOL_B.tick("b" + name))

            def a_accumulate(i, u):
                h, m = divmod(u, M)
                pool.wait_ge(*ACT_A.at(i, "sq", u))
                if m > 1:
                    pool.wait_ge(*POOL_A.at(i, "acc", u - 1))
                G.tensor_tensor(acc[:, h, :, :], acc[:, h, :, :], sq[:, u % 2, :, :], ALU.add).then_inc(*POOL_A.tick("acc", u))

            def a_both(i, h):
                pool.wait_ge(*POOL_A.at(i, "acc", M * h + M - 1))
                G.tensor_tensor(acc[:, h, 0, :], acc[:, h, 0, :], acc[:, h, 1, :], ALU.add)\
                    .then_inc(*POOL_A.tick("both", h))

            def turn(a, b, c, d):
                if c is not None:
                    rstd(c, 1, VEC_B, POOL_B)
                if d is not None:
                    rstd(d, 2, VEC_C, POOL_C)
                if b is not None:
                    rstd(b, 0, VEC_A, POOL_A)
                if b is not None:
                    b_front(b)
                if a is not None:
                    for u in range(UNITS):
                        if u % M:
                            a_accumulate(a, u)
                        if u % M == M - 1:
                            a_both(a, u // M)

            turn(0, None, None, None)
            turn(1, 0, None, None)
            turn(2, 1, 0, None)
            with pool.Fori(3, NCHUNK) as i:
                turn(i, i - 1, i - 2, i - 3)
            turn(None, NCHUNK - 1, NCHUNK - 2, NCHUNK - 3)
            turn(None, None, NCHUNK - 1, NCHUNK - 2)
            turn(None, None, None, NCHUNK - 1)

        @block.vector
        def _(dve):
            V = nc.vector
            TS, TT, STT = V.tensor_scalar, V.tensor_tensor, V.scalar_tensor_tensor
            count = [0]

            def link(ins):
                ins.then_inc(chain, 1)
                count[0] += 1
                dve.wait_ge(chain, count[0])

            dve.wait_ge(w_small, 16 * len(LOADS_S))
            slope, e, u1 = c32[:, 6:7], c32t[:, 9:10], c32t[:, 10:11]
            link(TS(c32t[:, 12:13], slope, -1.0, None, ALU.mult))
            V.memset(mask[:, :], 1.0)
            V.memset(half_[:, :], -0.5)
            V.memset(eps_[:, :], EPS)
            V.tensor_copy(c32t[:, 0:6], c32[:, 0:6])
            link(TT(c32t[:, 8:9], slope, c32t[:, 12:13], ALU.min))
            dve.wait_ge(act_s, 1)
            link(TS(u1, e, 1.0, None, ALU.add))
            link(TS(c32t[:, 12:13], u1, 1.0, None, ALU.subtract))
            link(TS(c32t[:, 13:14], u1, 1.0, None, ALU.is_equal))
            link(TT(c32t[:, 12:13], c32t[:, 12:13], c32t[:, 13:14], ALU.add))
            link(V.reciprocal(c32t[:, 12:13], c32t[:, 12:13]))
            dve.wait_ge(act_s, 2)
            link(TT(c32t[:, 14:15], c32t[:, 11:12], c32t[:, 13:14], ALU.add))
            link(TT(c32t[:, 14:15], c32t[:, 14:15], e, ALU.mult))
            link(TT(c32t[:, 14:15], c32t[:, 14:15], c32t[:, 12:13], ALU.mult))
            link(TS(c32t[:, 15:16], slope, 0.0, None, ALU.max))
            link(V.memset(c32t[:, 7:8], 0.0))
            link(TT(c32t[:, 6:7], c32t[:, 14:15], c32t[:, 15:16], ALU.add))
            link(TT(y8s[:, :, :, :], y8[:, :, :, :], n8.unsqueeze(3).broadcast_to([HD, 2, M, HD]), ALU.mult))
            link(TS(y8s[:, 0, :, :], y8s[:, 0, :, :], -1.0, None, ALU.mult))
            assert count[0] == SETUP_COL
            link(V.tensor_reduce(dl[:, 3:4], dl[:, 0:3], AX.X, ALU.max))
            link(TS(dl[:, 0:3], dl[:, 0:3], dl[:, 3:4], None, ALU.subtract))
            assert count[0] == SETUP_DERIV
            dve.wait_ge(act_s, 3)
            link(V.tensor_reduce(dl[:, 3:4], dl[:, 4:7], AX.X, ALU.add))
            link(V.reciprocal(dl[:, 3:4], dl[:, 3:4]))
            link(TS(dw[:, 0:3], dl[:, 4:7], dl[:, 3:4], None, ALU.mult))
            link(TS(dw[:, 2:3], dw[:, 2:3], -1.0, None, ALU.mult))
            dve.wait_ge(w_attn, 16 * len(LOADS_A))
            link(TS(thn[:, :, :], thn[:, :, :], 1.0 / (2.0 * math.pi), None, ALU.mult))
            link(V.memset(mask[:, :].rearrange("p (s l) -> p s l", l=L)[:, :, 0:1], 0.0))
            sraw = g[:, 0, 0:DT * HEADS].rearrange("p (t n) -> p t n", t=DT)
            for t in range(DT):
                link(V.tensor_copy(win[:, t, 2 * D:].rearrange("p (k h) -> p k h", h=HD),
                                   sraw[:, t, :].unsqueeze(2).broadcast_to([P, HEADS, HD])))
            for h in range(2):
                dve.wait_ge(pe_s, h + 1)
                V.tensor_copy(col7[:, h, :], ps[:, h, 0:8]).then_inc(vec_s, 1)
            dve.wait_ge(pe_s, 3)
            V.tensor_copy(ybase, ps[:, 2, 0:2 * M * HD]).then_inc(vec_s, 1)
            dve.wait_ge(vec_s, len(SETUP))
            V.tensor_copy(ss[:, :], col7[:, :, 5])
            for h in range(2):
                V.tensor_copy(cw[:, 4 + h, :], col7[:, h, 0:4])
            link(V.tensor_copy(cb[:, 4:6], col7[:, :, 4]))
            link(TS(lns[:, 0:2], col7[:, :, 6], -(L - 1.0), None, ALU.mult))
            link(TS(lns[:, 2:4], col7[:, :, 6], -1.0, None, ALU.mult))
            for h in range(2):
                link(TS(lt[:, h, :], pos, col7[:, h, 6:7], lns[:, h:h + 1], ALU.mult, ALU.add))
            a0 = (HEADS // 2 - ANCHORS) * HD
            link(TS(lt[a0:P, 1, :], pos[a0:P, :], lns[a0:P, 3:4], None, ALU.mult))
            for c in range(2):
                for m in range(M):
                    k = (c * M + m) * HD
                    link(TT(wy[:, c, m, :].rearrange("p (k n) -> p k n", n=HD),
                            ybase[:, k:k + HD].unsqueeze(1).broadcast_to([P, 16, HD]),
                            headm.unsqueeze(2).broadcast_to([P, 16, HD]), ALU.mult))
            V.memset(dw[:, 3:4], 0.0).then_inc(ready, 1)

            def biases():
                dve.wait_ge(w_x, 16 * len(LOADS_X))
                dve.wait_ge(w_raw, 16 * len(LOADS_RAW))
                link(V.tensor_copy(sel[:, :, :], selraw))
                V.memset(wpair[:, :].bitcast(F32), 0.0)
                link(TS(bqkv[:, :, :], bqkv[:, :, :], float(L), None, ALU.mult))
                link(TT(rb2[:, 0, :], rb2[:, 0, :], rb2[:, 1, :], ALU.add))
                link(V.tensor_copy(rb2[:, 1, :], rb2[:, 0, :]))
                link(V.memset(acol[:, 1:2], 1.0))
                link(TS(dl[0:16, 0:1], cst[0:16, C_HM:C_HM + 1], 1.0, None, ALU.mult))
                link(TS(dl[0:16, 1:2], acol[0:16, 0:1], 1.0, None, ALU.subtract))
                link(TS(dl[0:16, 0:1], dl[0:16, 0:1], -1.0, 1.0, ALU.mult, ALU.add))
                link(TT(dl[0:16, 2:3], dl[0:16, 0:1], dl[0:16, 1:2], ALU.mult))
                link(TT(acol[0:16, 1:2], acol[0:16, 1:2], dl[0:16, 2:3], ALU.add))
                V.memset(seen[:, :], 0.0).then_inc(ready, 1)

            def a_tap(i, j, tap):
                s = TAPS - 1 - tap
                o = zc[:, j, :].rearrange("p (b l) -> p b l", b=SEQ)
                z = ps[:, BANK_A[("z", j)], :].rearrange("p (b l) -> p b l", b=SEQ)
                if tap == 2:
                    dve.wait_ge(*ACT_A.at(i, "z", j))
                else:
                    dve.wait_ge(*VEC_A.at(i, "tap", j, tap + 1))
                STT(o[:, :, s:L], z[:, :, 0:L - s], cw[:, j, tap:tap + 1], o[:, :, s:L], ALU.mult, ALU.add)\
                    .then_inc(*VEC_A.tick("tap", j, tap))

            def a_conv(i, j):
                for tap in (2, 1, 0):
                    a_tap(i, j, tap)

            def a_exponent(i, h):
                z = zc[:, 4 + h, :]
                dve.wait_ge(*VEC_A.at(i, "tap", 4 + h, 0))
                TS(z, z, ss[:, h:h + 1], 20.0, ALU.mult, ALU.min).then_inc(*VEC_A.tick("clip", h))
                dve.wait_ge(*VEC_A.at(i, "clip", h))
                z3 = z.rearrange("p (b l) -> p b l", b=SEQ)
                STT(z3, z3, -20.0, lt[:, h, :].unsqueeze(1).broadcast_to([P, SEQ, L]), ALU.max, ALU.add)\
                    .then_inc(*VEC_A.tick("expo", h))

            def a_fraction(i, u):
                h, m = divmod(u, M)
                if m == 0:
                    dve.wait_ge(*VEC_A.at(i, "tap", h, 0))
                if u >= 2:
                    dve.wait_ge(*ACT_A.at(i, "sin", u - 2))
                    dve.wait_ge(*VEC_A.at(i, "re", u - 2))
                elif not is_first(i):
                    dve.wait_ge(*ACT_A.at(i - 1, "sin", UNITS - 2 + u))
                TS(kturn[:, u % 2, :], zc[:, h, :], thn[:, h, m:m + 1], None, ALU.mult)\
                    .then_inc(*VEC_A.tick("turns", u))
                dve.wait_ge(*VEC_A.at(i, "turns", u))
                STT(frac[:, u % 2, :], zc[:, h, :], thn[:, h, m:m + 1], kturn[:, u % 2, :], ALU.mult, ALU.subtract)\
                    .then_inc(*VEC_A.tick("frac", u))

            def a_poly(i, h):
                z = zc[:, h, :]
                dve.wait_ge(*VEC_A.at(i, "tap", h, 0))
                if not is_first(i):
                    dve.wait_ge(*VEC_A.at(i - 1, "re", M * h + M - 1))
                TS(g[:, h, :], z, dw[:, 2:3], dw[:, 1:2], ALU.mult, ALU.add).then_inc(*VEC_A.tick("p1", h))
                dve.wait_ge(*VEC_A.at(i, "p1", h))
                TT(g[:, h, :], g[:, h, :], z, ALU.mult).then_inc(*VEC_A.tick("p2", h))
                dve.wait_ge(*VEC_A.at(i, "p2", h))
                dve.wait_ge(*ACT_A.at(i, "exp", h))
                STT(g[:, h, :], g[:, h, :], dw[:, 0:1], zc[:, 4 + h, :], ALU.add, ALU.mult)\
                    .then_inc(*VEC_A.tick("g", h))

            def a_den(i, h):
                dve.wait_ge(*VEC_A.at(i, "g", h))
                V.tensor_tensor_scan(den[:, h, :], mask[:, 0:T], den[:, h, :], 0.0, ALU.mult, ALU.add)\
                    .then_inc(*VEC_A.tick("den", h))
                dve.wait_ge(*VEC_A.at(i, "den", h))
                TS(den[:, h, :], den[:, h, :], 1e-4, None, ALU.max).then_inc(*VEC_A.tick("guard", h))

            def a_moments(i, u):
                h, s = u // M, u % 4
                dve.wait_ge(*ACT_A.at(i, "sin", u))
                if u % M == 0:
                    dve.wait_ge(*VEC_A.at(i, "g", h))
                TT(sc[:, s, 0, :], sc[:, s, 0, :], g[:, h, :], ALU.mult).then_inc(*VEC_A.tick("im", u))
                STT(sc[:, s, 1, :], hq[:, u % 2, :], 1.0, g[:, h, :], ALU.subtract, ALU.mult)\
                    .then_inc(*VEC_A.tick("re", u))

            def a_scan(i, u):
                flat = sc[:, u % 4, :, :].rearrange("p c t -> p (c t)")
                dve.wait_ge(*VEC_A.at(i, "re", u))
                V.tensor_tensor_scan(flat, mask[:, 0:2 * T], flat, 0.0, ALU.mult, ALU.add)\
                    .then_inc(*VEC_A.tick("scan", u))

            def a_square(i, h):
                dve.wait_ge(*PE_A.at(i, "S", h))
                dve.wait_ge(*ACT_A.at(i, "e", h))
                TT(den[:, h, :], ps[:, BANK_A[("S", h)], :], den[:, h, :], ALU.add).then_inc(*VEC_A.tick("w", h))

            def a_heads(i, h):
                dve.wait_ge(*ACT_A.at(i, "f", h))
                TT(zc[:, 2 + h, :], zc[:, 2 + h, :], den[:, h, :], ALU.mult).then_inc(*VEC_A.tick("gf", h))
                dve.wait_ge(*VEC_A.at(i, "gf", h))
                dve.wait_ge(*PE_A.at(i, "y", M * h + M - 1))
                TT(zc[:, 2 + h, :], zc[:, 2 + h, :], ps[:, BANK_A[("Y", h)], :], ALU.mult)\
                    .then_inc(*VEC_A.tick("y", h))

            def ln_stats(i, k, xs, VEC):
                for q in range(NQ):
                    dve.wait_ge(*VEC.at(i, "res", q // 2))
                    V.bn_stats(st[k][:, q, :], xs[:, q, :]).then_inc(*VEC.tick("stats", q))
                dve.wait_ge(*VEC.at(i, "stats", NQ - 1))
                V.tensor_copy(seen[:, k:k + 1], st[k][:, 0, 0:1])
                for q in range(NQ):
                    V.bn_aggr(mvr[k][:, q, :], st[k][:, q, :]).then_inc(*VEC.tick("aggr", q))

            def ln_apply(i, k, xs, dst, VEC, POOL):
                dve.wait_ge(*POOL.at(i, "rstd"))
                for q in range(NQ):
                    TS(dst[:, q, :], xs[:, q, :], mvr[k][:, q, 0:1], rs[k][:, 1, q:q + 1], ALU.subtract, ALU.mult)\
                        .then_inc(*VEC.tick("norm", q))

            def a_residual(i, n):
                dve.wait_ge(*PE_A.at(i, "out", n))
                if n == 0:
                    dve.wait_ge(xr_in, 16 * i + 16)
                o = xs_a[:, 2 * n:2 * n + 2, :]
                TT(o, o, ps[:, BANK_A[("out", n)], :].rearrange("p (q d) -> p q d", q=2), ALU.add)\
                    .then_inc(*VEC_A.tick("res", n))

            def b_norm(i):
                ln_apply(i, 1, x1, x2, VEC_B, POOL_B)

            def a_norm(i):
                if not is_first(i):
                    dve.wait_ge(*VEC_B.at(i - 1, "norm", NQ - 1))
                ln_apply(i, 0, xs_a, x1, VEC_A, POOL_A)

            def b_products(i):
                dve.wait_ge(*ACT_B.at(i, "kb"))
                dve.wait_ge(*POOL_B.at(i, "bk"))
                dve.wait_ge(*PE_B.at(i, "vb"))
                TT(spec[:, 0:2, :], qkv[:, 0:2, :], qkv[:, 2:4, :], ALU.mult).then_inc(*VEC_B.tick("aabb"))
                TT(spec[:, 2, :], qkv[:, 0, :], qkv[:, 3, :], ALU.mult).then_inc(*VEC_B.tick("ab"))
                TT(spec[:, 3, :], qkv[:, 1, :], qkv[:, 2, :], ALU.mult).then_inc(*VEC_B.tick("ba"))
                dve.wait_ge(*VEC_B.at(i, "ba"))
                V.tensor_reduce(rsum[:, :, :], spec[:, :, :].rearrange("p a (h d) -> p a h d", d=XD), AX.X, ALU.add)\
                    .then_inc(*VEC_B.tick("heads"))
                aa, bb_, ab, ba = (rsum[:, n, :] for n in range(4))
                dve.wait_ge(*VEC_B.at(i, "heads"))
                STT(cspec[:, 0, :], bb_, m0, aa, ALU.mult, ALU.add).then_inc(*VEC_B.tick("ca"))
                TT(cspec[:, 2, :], ba, ab, ALU.subtract).then_inc(*VEC_B.tick("cb0"))
                TS(cspec[:, 3, :], bb_, m1, None, ALU.mult).then_inc(*VEC_B.tick("cb1"))
                dve.wait_ge(*VEC_B.at(i, "cb1"))
                STT(cspec[:, 1, :], cspec[:, 2, :], m0, cspec[:, 3, :], ALU.mult, ALU.add)\
                    .then_inc(*VEC_B.tick("cb2"))

            def b_topk(i):
                c, top = cor[:, 0, :], sm[:, 0:8]
                above, equal, order = cor[:, 1, :], cor[:, 2, :], cor[:, 3, :]
                dve.wait_ge(*PE_B.at(i, "corr"))
                TS(c, ps[0:BH, BANK_B[("corr",)], 0:L], 1.0 / XD, None, ALU.mult).then_inc(*VEC_B.tick("corr"))
                dve.wait_ge(*VEC_B.at(i, "corr"))
                V.tensor_copy(sm[:, 12:13], cor[:, 0, 0:1])
                V.max(top, c).then_inc(*VEC_B.tick("top"))
                dve.wait_ge(*VEC_B.at(i, "top"))
                TS(sm[:, 8:9], sm[:, 0:1], -1.0, None, ALU.mult).then_inc(*VEC_B.tick("negmax"))
                kth = sm[:, TOPK - 1:TOPK]
                TS(above, c, kth, None, ALU.is_gt, ALU.add, accum_out=sm[:, 9:10]).then_inc(*VEC_B.tick("above"))
                TS(equal, c, kth, None, ALU.is_equal).then_inc(*VEC_B.tick("equal"))
                dve.wait_ge(*VEC_B.at(i, "equal"))
                V.tensor_tensor_scan(order, mask[0:BH, 1:2].broadcast_to([BH, L]), equal, 0.0, ALU.mult, ALU.add)\
                    .then_inc(*VEC_B.tick("order"))
                dve.wait_ge(*VEC_B.at(i, "order"))
                TS(order, order, sm[:, 9:10], float(TOPK), ALU.add, ALU.is_le).then_inc(*VEC_B.tick("first"))
                dve.wait_ge(*VEC_B.at(i, "first"))
                TT(order, order, equal, ALU.mult).then_inc(*VEC_B.tick("also"))
                dve.wait_ge(*VEC_B.at(i, "also"))
                TT(above, above, order, ALU.add).then_inc(*VEC_B.tick("keep"))
                dve.wait_ge(*VEC_B.at(i, "keep"))
                dve.wait_ge(*ACT_B.at(i, "exp"))
                STT(cor[:, 2, :], cor[:, 4, :], 1.0, above, ALU.mult, ALU.mult, accum_out=sm[:, 10:11])\
                    .then_inc(*VEC_B.tick("weight"))
                dve.wait_ge(*VEC_B.at(i, "weight"))
                V.reciprocal(sm[:, 11:12], sm[:, 10:11]).then_inc(*VEC_B.tick("inv"))
                dve.wait_ge(*VEC_B.at(i, "inv"))
                TS(cor[:, 0, :], cor[:, 2, :], sm[:, 11:12], None, ALU.mult).then_inc(*VEC_B.tick("wn"))

            def b_apply(i):
                dve.wait_ge(*PE_B.at(i, "wf"))
                wa, wb = (ps[:, BANK_B[("wf",)], n * BH:(n + 1) * BH] for n in range(2))
                V.tensor_copy(wspec[:, 0, :], wa).then_inc(*VEC_B.tick("w1"))
                TS(wspec[:, 1, :], wb, m0, None, ALU.mult).then_inc(*VEC_B.tick("w2"))
                TS(wspec[:, 2, :], wb, m0, -1.0, ALU.mult, ALU.mult).then_inc(*VEC_B.tick("w4"))
                TS(cspec[:, 2, :], wb, m1, None, ALU.mult).then_inc(*VEC_B.tick("w3a"))
                dve.wait_ge(*VEC_B.at(i, "w3a"))
                STT(wspec[:, 3, :], wa, m0, cspec[:, 2, :], ALU.mult, ALU.add).then_inc(*VEC_B.tick("w3"))
                dve.wait_ge(*VEC_B.at(i, "w3"))
                dve.wait_ge(*ACT_B.at(i, "vb"))
                dve.wait_ge(*POOL_B.at(i, "bv"))
                v = qkv[:, 4:6, :].rearrange("p a (h d) -> p a h d", d=XD)
                for n, name in ((0, "oa"), (2, "ob")):
                    TT(spec[:, n:n + 2, :].rearrange("p a (h d) -> p a h d", d=XD), v,
                       wspec[:, n:n + 2, :].unsqueeze(3).broadcast_to([P, 2, BH, XD]), ALU.mult)\
                        .then_inc(*VEC_B.tick(name))
                dve.wait_ge(*VEC_B.at(i, "ob"))
                s4 = spec[:, :, :].rearrange("p (a b) t -> p a b t", b=2)
                TT(qkv[:, 0:2, :], s4[:, :, 0, :], s4[:, :, 1, :], ALU.add).then_inc(*VEC_B.tick("o"))

            def b_residual(i):
                for n in range(2):
                    dve.wait_ge(*PE_B.at(i, "out", n))
                    if n == 0:
                        dve.wait_ge(*POOL_B.at(i, "res"))
                    o = x1[:, 2 * n:2 * n + 2, :]
                    TT(o, o, ps[:, BANK_B[("out", n)], :].rearrange("p (q d) -> p q d", q=2), ALU.add)\
                        .then_inc(*VEC_B.tick("res", n))
                ln_stats(i, 1, x1, VEC_B)

            def c_cum(i):
                dve.wait_ge(*ACT_C.at(i, "xT", 1))
                if not is_first(i):
                    dve.wait_ge(*PE_C.at(i - 1, "c", NJ - 1))
                V.tensor_tensor_scan(cum[:, :, :].rearrange("p a t -> p (a t)"), mask[:, 0:DT * T],
                                     x2t[:, :, :].rearrange("p a t -> p (a t)"), 0.0, ALU.mult, ALU.add)\
                    .then_inc(*VEC_C.tick("cum"))

            def c_softmax(i):
                n = NQ * 2
                dve.wait_ge(*PE_C.at(i, "logit"))
                TT(lg[:, :, :].rearrange("p (q b) k -> p q (b k)", b=2),
                   ps[:, BANK_C[("logit",)], 0:n * KEXP].rearrange("p (q b) -> p q b", q=NQ),
                   rb2[:, :, :].rearrange("p b k -> p (b k)").unsqueeze(1).broadcast_to([P, NQ, 2 * KEXP]), ALU.add)\
                    .then_inc(*VEC_C.tick("logit"))
                dve.wait_ge(*VEC_C.at(i, "logit"))
                V.tensor_reduce(ls[:, 0, :], lg[:, :, :], AX.X, ALU.max).then_inc(*VEC_C.tick("max"))
                dve.wait_ge(*VEC_C.at(i, "max"))
                TT(lg[:, :, :], lg[:, :, :], ls[:, 0, :].unsqueeze(2).broadcast_to([P, n, KEXP]), ALU.subtract)\
                    .then_inc(*VEC_C.tick("sub"))

            def c_normalise(i):
                n = NQ * 2
                dve.wait_ge(*ACT_C.at(i, "exp"))
                V.tensor_reduce(ls[:, 1, :], lg[:, :, :], AX.X, ALU.add).then_inc(*VEC_C.tick("sum"))
                dve.wait_ge(*VEC_C.at(i, "sum"))
                V.reciprocal(ls[:, 1, :], ls[:, 1, :]).then_inc(*VEC_C.tick("inv"))
                dve.wait_ge(*VEC_C.at(i, "inv"))
                TT(lg[:, :, :], lg[:, :, :], ls[:, 1, :].unsqueeze(2).broadcast_to([P, n, KEXP]), ALU.mult)\
                    .then_inc(*VEC_C.tick("weight"))

            def c_split(i):
                dve.wait_ge(*ACT_C.at(i, "whigh"))
                if not is_first(i):
                    dve.wait_ge(*PE_C.at(i - 1, "w", NJ - 1))
                TT(wpair[32:32 + 2 * KEXP, :], ps[0:2 * KEXP, BANK_C[("wT",)], :],
                   wpair[0:2 * KEXP, :].bitcast(F32), ALU.subtract).then_inc(*VEC_C.tick("wlow"))

            def c_prod(i, j):
                dve.wait_ge(*ACT_C.at(i, "c", j))
                dve.wait_ge(*PE_C.at(i, "w", j))
                TT(cs[:, j % 2, :], cs[:, j % 2, :], ps[:, BANK_C[("w", j)], :], ALU.mult).then_inc(*VEC_C.tick("cw", j))
                dve.wait_ge(*VEC_C.at(i, "cw", j))
                dve.wait_ge(*PE_C.at(i, "x", j))
                if j == 4 and not is_first(i):
                    dve.wait_ge(stored, 16 * i)
                TT(prod[:, j, :], cs[:, j % 2, :], ps[:, BANK_C[("x", j)], :], ALU.mult)\
                    .then_inc(*VEC_C.tick("prod", j))

            def c_residual(i, n):
                dve.wait_ge(*PE_C.at(i, "out", n))
                for q in range(2):
                    o = x2[:, 2 * n + q, :]
                    ins = STT(o, ps[:, BANK_C[("out", n)], q * D:(q + 1) * D], rn[:, q:q + 1], o, ALU.mult, ALU.add)
                ins.then_inc(*VEC_C.tick("res", n))

            def a_unit(i, u):
                a_moments(i, u)
                if u + 2 < UNITS:
                    a_fraction(i, u + 2)
                a_scan(i, u)

            def turn(a, b, c, d):
                if c is not None:
                    b_residual(c)
                if d is not None:
                    c_residual(d, 0)
                if a is not None:
                    a_conv(a, 4)
                    a_exponent(a, 0)
                    a_conv(a, 0)
                    a_fraction(a, 0)
                    a_fraction(a, 1)
                if d is not None:
                    c_residual(d, 1)
                    ln_stats(d, 2, x2, VEC_C)
                if b is not None:
                    a_residual(b, 0)
                if a is not None:
                    a_conv(a, 5)
                    a_exponent(a, 1)
                if d is not None:
                    ln_apply(d, 2, x2, xs_c, VEC_C, POOL_C)
                    dve.wait_ge(*VEC_C.at(d, "norm", NQ - 1))
                if c is not None:
                    b_norm(c)
                if b is not None:
                    a_residual(b, 1)
                    ln_stats(b, 0, xs_a, VEC_A)
                if a is not None:
                    a_conv(a, 1)
                    a_poly(a, 0)
                    a_den(a, 0)
                if b is not None:
                    a_norm(b)
                if a is not None:
                    a_unit(a, 0)
                    a_conv(a, 2)
                if is_first(a):
                    biases()
                if c is not None:
                    c_cum(c)
                if a is not None:
                    a_conv(a, 3)
                    a_poly(a, 1)
                    a_den(a, 1)
                if c is not None:
                    c_softmax(c)
                if a is not None:
                    a_unit(a, 1)
                if c is not None:
                    c_normalise(c)
                if a is not None:
                    a_unit(a, 2)
                if c is not None:
                    c_split(c)
                for u in range(UNITS):
                    if a is not None and u == M + 1:
                        a_square(a, 0)
                    if b is not None and u == AT_TOPK:
                        b_topk(b)
                    if c is not None:
                        c_prod(c, u)
                    if b is not None and u == AT_APPLY:
                        b_apply(b)
                    if b is not None and u == 0:
                        b_products(b)
                    if a is not None:
                        if u + 3 < UNITS:
                            a_unit(a, u + 3)
                        if u == M + 2:
                            a_heads(a, 0)
                if a is not None:
                    a_square(a, 1)
                if a is not None:
                    a_heads(a, 1)

            turn(0, None, None, None)
            turn(1, 0, None, None)
            turn(2, 1, 0, None)
            with dve.Fori(3, NCHUNK) as i:
                turn(i, i - 1, i - 2, i - 3)
            turn(None, NCHUNK - 1, NCHUNK - 2, NCHUNK - 3)
            turn(None, None, NCHUNK - 1, NCHUNK - 2)
            turn(None, None, None, NCHUNK - 1)


SETUP_COL = 15
SETUP_DERIV = 17


def shape_constants():
    c = np.zeros((P, C_END), np.float32)
    p = np.arange(P)
    c[:, C_ID:C_ID + P] = np.eye(P)
    c[:, C_BLK:C_BLK + P] = p[:, None] // HD == p[None, :] // HD
    c[:, C_HM:C_HM + 16] = p[:, None] // HD == np.arange(16)[None, :]
    c[:, C_POS:C_POS + L] = np.arange(L)
    c[:, C_RN] = 1.0 / (p + 1.0)
    c[:, C_RN + 1] = 1.0 / (p + P + 1.0)
    c[:, C_M0] = p > 0
    c[:, C_M0 + 1] = p == 0
    c[0:HD, C_E8:C_E8 + P] = np.arange(HD)[:, None] == p[None, :] % HD
    t, f = np.arange(L)[:, None], np.arange(P)[None, :]
    ang = 2.0 * np.pi * ((t * f) % L) / L
    fwd = np.concatenate([np.cos(ang), np.sin(ang)], 1)
    fwd[:, P] = (-1.0) ** np.arange(L)
    scale = np.where(np.arange(P) == 0, 1.0, 2.0)[:, None] / L
    inv = np.stack([fwd[:, 0:P].T * scale, fwd[:, P:].T * scale])
    e = np.zeros((HEADS, 2, P), np.float32)
    s = np.zeros((32 + 2 * KEXP, NJ, P), np.float32)
    for h in range(2):
        e[:, h, :] = np.arange(HEADS)[:, None] == h * 16 + p[None, :] // HD
    for j in range(NJ):
        for first in (0, 32):
            s[first:first + 2 * KEXP, j, :] = np.arange(2 * KEXP)[:, None] == 2 * j + p[None, :] // R
    return {"consts": c, "dft": fwd.astype(np.float32), "idft": inv.astype(np.float32), "expand": e, "select": s}


_INS = ['x', 'ctx_1024', 'L0_attn_in_proj_w', 'L0_attn_conv_w', 'L0_attn_conv_b', 'L0_attn_theta',
        'L0_attn_decay_slopes', 'L0_attn_anchor_slopes', 'L0_attn_score_scale', 'L0_attn_deriv_logits',
        'L0_attn_norm_scale', 'L0_attn_W_re', 'L0_attn_W_im', 'L0_attn_out_proj_w', 'L0_xattn_Wq',
        'L0_xattn_bq', 'L0_xattn_Wk', 'L0_xattn_bk', 'L0_xattn_Wv', 'L0_xattn_bv', 'L0_xattn_Wo',
        'L0_xattn_bo', 'L0_ffn_W_Q', 'L0_ffn_W_K', 'L0_ffn_W_O', 'L0_ffn_W_inv', 'L0_ffn_V_fwd',
        'L0_ffn_W_fwd', 'L0_ffn_U_fwd', 'L0_ffn_b_fwd', 'L0_ffn_V_inv', 'L0_ffn_W_inv_exp',
        'L0_ffn_U_inv', 'L0_ffn_b_inv', 'L0_ffn_router_w1', 'L0_ffn_router_b1', 'L0_ffn_router_w2',
        'L0_ffn_router_b2', 'L0_ffn_alpha_bi', 'L0_ffn_expert_bias']


def kernel(**inputs):
    import concourse.bacc as _bacc
    from concourse.bass_utils import run_bass_kernel_spmd as _run

    nc = _bacc.Bacc("TRN2", target_bir_lowering=False, num_devices=1)
    arrays, args = {}, []
    given = {name: np.ascontiguousarray(inputs[name]) for name in _INS}
    given['L0_ffn_alpha_bi'] = given['L0_ffn_alpha_bi'].reshape(1)
    given.update(shape_constants())
    for name, a in given.items():
        arrays[f"in_{name}_dram"] = a
        args.append(nc.dram_tensor(f"in_{name}_dram", a.shape, mybir.dt.from_np(a.dtype), kind="ExternalInput").ap())
    args.append(nc.dram_tensor("out_0_dram", (B, L, D), F32, kind="ExternalOutput").ap())
    decoder_kernel(nc, *args)
    r = _run(nc, [arrays], core_ids=[0])
    return r.results[0]["out_0_dram"]
```
